# Optimizing a Trainium2 kernel written in Bass

```python
import numpy as np
import jax
import jax.numpy as jnp

def _softmax(x, axis=-1):
    return jax.nn.softmax(x, axis=axis)

def _gelu(x):
    return jax.nn.gelu(x, approximate=True)

def _silu(x):
    return jax.nn.silu(x)

def _sigmoid(x):
    return jax.nn.sigmoid(x)

def _layernorm(x, axis=-1, eps=1e-05):
    m = jnp.mean(x, axis=axis, keepdims=True)
    v = jnp.var(x, axis=axis, keepdims=True)
    return (x - m) / jnp.sqrt(v + eps)

def _scatter_add(tgt, idx, src, axis=0):
    return tgt.at[idx].add(src)

def _segment_sum(src, seg, n):
    return jax.ops.segment_sum(src, seg, n)
kernel_name = 'mk_audio_tower_d1_tok_audfeat2048_r4_dc79f2'

def setup_inputs(seed: int=0):
    np.random.seed(seed)
    _w = jnp.asarray

    def _rec_inputs():
        import jax
        import jax.numpy as jnp
        _rk = jax.random.key(seed)
        x = -0.000125008 + 0.999885 * jax.random.normal(jax.random.fold_in(_rk, 1), (32, 256, 512), jnp.float32)
        return x
    x = _rec_inputs()

    def _L0_tok_setup():
        import jax, jax.numpy as jnp
        import numpy as np
        D_MODEL = 512
        N_HEADS = 16
        HEAD_DIM = D_MODEL // N_HEADS
        SEGMENT_SIZE = 128
        DILATION = 2
        BATCH = 2
        SEQ_LEN = 2048
        key = jax.random.key(seed)
        k1, k2, k3 = jax.random.split(key, 3)
        x = jax.random.normal(k1, (BATCH, SEQ_LEN, D_MODEL), dtype=jnp.float32)
        Wqkv = jax.random.normal(k2, (3 * D_MODEL, D_MODEL), dtype=jnp.float32) * 0.02
        b_qkv = jnp.zeros((3 * D_MODEL,), dtype=jnp.float32)
        Wout = jax.random.normal(k3, (D_MODEL, D_MODEL), dtype=jnp.float32) * 0.02
        b_out = jnp.zeros((D_MODEL,), dtype=jnp.float32)
        return {'x': x, 'Wqkv': Wqkv, 'b_qkv': b_qkv, 'Wout': Wout, 'b_out': b_out}
    _L0_tok_all = _L0_tok_setup()
    _L0_tok_in = {k: v for k, v in _L0_tok_all.items() if k in ('Wqkv', 'b_qkv', 'Wout', 'b_out')}
    del _L0_tok_all

    def _L0_attn_setup():
        import jax, jax.numpy as jnp
        import numpy as np
        N_HEADS = 16
        N_KV_HEADS = 4
        WINDOW = 128
        N_META = 16
        ROPE_BASE = 10000.0

        def rotate_half(x):
            x1 = x[..., 0::2]
            x2 = x[..., 1::2]
            return jnp.stack((-x2, x1), axis=-1).reshape(x.shape)

        def apply_rope(x, positions):
            d = x.shape[-1]
            inv_freq = 1.0 / ROPE_BASE ** (jnp.arange(0, d, 2, dtype=jnp.float32) / d)
            angles = positions.astype(jnp.float32)[:, None] * inv_freq
            cos = jnp.repeat(jnp.cos(angles), 2, axis=-1)[None, None]
            sin = jnp.repeat(jnp.sin(angles), 2, axis=-1)[None, None]
            return x * cos + rotate_half(x) * sin
        key = jax.random.key(seed)
        ks = jax.random.split(key, 4)
        B, S, E = (2, 1024, 512)
        hd = E // N_HEADS
        kv_out = 2 * N_KV_HEADS * hd
        sc = 1.0 / np.sqrt(E).astype(np.float32)
        return {'x': jax.random.normal(ks[0], (B, S, E), jnp.float32), 'Wq': jax.random.normal(ks[1], (E, E), jnp.float32) * sc, 'bq': jnp.zeros((E,), jnp.float32), 'Wkv': jax.random.normal(ks[2], (E, kv_out), jnp.float32) * sc, 'bkv': jnp.zeros((kv_out,), jnp.float32), 'Wo': jax.random.normal(ks[3], (E, E), jnp.float32) * sc, 'bo': jnp.zeros((E,), jnp.float32)}
    _L0_attn_all = _L0_attn_setup()
    _L0_attn_in = {k: v for k, v in _L0_attn_all.items() if k in ('Wq', 'bq', 'Wkv', 'bkv', 'Wo', 'bo')}
    del _L0_attn_all

    def _L0_ffn_setup():
        import jax, jax.numpy as jnp
        import numpy as np
        N_EXPERTS = 8
        TOP_K = 2
        D_MODEL = 512
        D_FF = 256
        BATCH, SEQ = (2, 512)

        def _trunc_normal(key, shape, fan_in):
            std = jnp.sqrt(1.0 / 3.0) / jnp.sqrt(float(fan_in))
            return jax.random.truncated_normal(key, -2.0, 2.0, shape, dtype=jnp.float32) * std
        key = jax.random.key(seed)
        kx, kr, k1, k2, k3 = jax.random.split(key, 5)
        x = jax.random.normal(kx, (BATCH, SEQ, D_MODEL), dtype=jnp.float32)
        router_w = jax.random.uniform(kr, (N_EXPERTS, D_MODEL), dtype=jnp.float32, minval=-1.0, maxval=1.0) / jnp.sqrt(float(D_MODEL))
        w1 = _trunc_normal(k1, (N_EXPERTS, D_MODEL, D_FF), D_MODEL)
        w2 = _trunc_normal(k2, (N_EXPERTS, D_MODEL, D_FF), D_MODEL)
        w3 = _trunc_normal(k3, (N_EXPERTS, D_FF, D_MODEL), D_FF)
        return {'x': x, 'router_w': router_w, 'w1': w1, 'w2': w2, 'w3': w3}
    _L0_ffn_all = _L0_ffn_setup()
    _L0_ffn_in = {k: v for k, v in _L0_ffn_all.items() if k in ('router_w', 'w1', 'w2', 'w3')}
    del _L0_ffn_all
    return {'x': x, 'L0_tok_Wqkv': _L0_tok_in['Wqkv'], 'L0_tok_b_qkv': _L0_tok_in['b_qkv'], 'L0_tok_Wout': _L0_tok_in['Wout'], 'L0_tok_b_out': _L0_tok_in['b_out'], 'L0_attn_Wq': _L0_attn_in['Wq'], 'L0_attn_bq': _L0_attn_in['bq'], 'L0_attn_Wkv': _L0_attn_in['Wkv'], 'L0_attn_bkv': _L0_attn_in['bkv'], 'L0_attn_Wo': _L0_attn_in['Wo'], 'L0_attn_bo': _L0_attn_in['bo'], 'L0_ffn_router_w': _L0_ffn_in['router_w'], 'L0_ffn_w1': _L0_ffn_in['w1'], 'L0_ffn_w2': _L0_ffn_in['w2'], 'L0_ffn_w3': _L0_ffn_in['w3']}

def reference(x, L0_tok_Wqkv, L0_tok_b_qkv, L0_tok_Wout, L0_tok_b_out, L0_attn_Wq, L0_attn_bq, L0_attn_Wkv, L0_attn_bkv, L0_attn_Wo, L0_attn_bo, L0_ffn_router_w, L0_ffn_w1, L0_ffn_w2, L0_ffn_w3):
    import jax
    import jax.numpy as jnp

    def _L0_tok_ref(x, Wqkv, b_qkv, Wout, b_out):
        import jax, jax.numpy as jnp
        import numpy as np
        D_MODEL = 512
        N_HEADS = 16
        HEAD_DIM = D_MODEL // N_HEADS
        SEGMENT_SIZE = 128
        DILATION = 2
        BATCH = 2
        SEQ_LEN = 2048
        B, S, D = x.shape
        H, hd = (N_HEADS, HEAD_DIM)
        xs = x.reshape(B, -1, SEGMENT_SIZE, D)[:, :, ::DILATION, :]
        N, L = (xs.shape[1], xs.shape[2])
        qkv = jnp.einsum('bnld,ed->bnle', xs, Wqkv) + b_qkv
        q, k, v = jnp.split(qkv, 3, axis=-1)
        q = q.reshape(B, N, L, H, hd)
        k = k.reshape(B, N, L, H, hd)
        v = v.reshape(B, N, L, H, hd)
        scale = 1.0 / jnp.sqrt(jnp.asarray(hd, dtype=x.dtype))
        scores = jnp.einsum('bnqhd,bnkhd->bnhqk', q, k) * scale
        attn = jax.nn.softmax(scores, axis=-1)
        out = jnp.einsum('bnhqk,bnkhd->bnqhd', attn, v).reshape(B, N, L, D)
        out = jnp.einsum('bnld,ed->bnle', out, Wout) + b_out
        return out.reshape(B, -1, D)

    def _L0_attn_ref(x, Wq, bq, Wkv, bkv, Wo, bo):
        import jax, jax.numpy as jnp
        import numpy as np
        N_HEADS = 16
        N_KV_HEADS = 4
        WINDOW = 128
        N_META = 16
        ROPE_BASE = 10000.0

        def rotate_half(x):
            x1 = x[..., 0::2]
            x2 = x[..., 1::2]
            return jnp.stack((-x2, x1), axis=-1).reshape(x.shape)

        def apply_rope(x, positions):
            d = x.shape[-1]
            inv_freq = 1.0 / ROPE_BASE ** (jnp.arange(0, d, 2, dtype=jnp.float32) / d)
            angles = positions.astype(jnp.float32)[:, None] * inv_freq
            cos = jnp.repeat(jnp.cos(angles), 2, axis=-1)[None, None]
            sin = jnp.repeat(jnp.sin(angles), 2, axis=-1)[None, None]
            return x * cos + rotate_half(x) * sin
        B, S, E = x.shape
        hd = E // N_HEADS
        q = (x @ Wq + bq).reshape(B, S, N_HEADS, hd).transpose(0, 2, 1, 3)
        kv = (x @ Wkv + bkv).reshape(B, S, 2, N_KV_HEADS, hd)
        k = kv[:, :, 0].transpose(0, 2, 1, 3)
        v = kv[:, :, 1].transpose(0, 2, 1, 3)
        pos = jnp.arange(S)
        q = apply_rope(q, pos)
        k = apply_rope(k, pos)
        rep = N_HEADS // N_KV_HEADS
        k = jnp.repeat(k, rep, axis=1)
        v = jnp.repeat(v, rep, axis=1)
        meta_end = min(N_META, S)
        scale = 1.0 / float(np.sqrt(hd))
        chunks = []
        for qs in range(0, S, WINDOW):
            qe = min(qs + WINDOW, S)
            ls = max(meta_end, qs - WINDOW + 1)
            q_c = q[:, :, qs:qe]
            k_c = jnp.concatenate([k[:, :, :meta_end], k[:, :, ls:qe]], axis=2)
            v_c = jnp.concatenate([v[:, :, :meta_end], v[:, :, ls:qe]], axis=2)
            k_pos = jnp.concatenate([jnp.arange(meta_end), jnp.arange(ls, qe)])
            q_pos = jnp.arange(qs, qe)
            causal = k_pos[None, :] <= q_pos[:, None]
            in_window = k_pos[None, :] >= q_pos[:, None] - WINDOW + 1
            meta = k_pos[None, :] < meta_end
            allowed = causal & (in_window | meta)
            scores = jnp.einsum('bhqd,bhkd->bhqk', q_c, k_c) * scale
            scores = jnp.where(allowed[None, None], scores, -jnp.inf)
            attn = jax.nn.softmax(scores, axis=-1)
            chunks.append(jnp.einsum('bhqk,bhkd->bhqd', attn, v_c))
        y = jnp.concatenate(chunks, axis=2)
        y = y.transpose(0, 2, 1, 3).reshape(B, S, E)
        return y @ Wo + bo

    def _L0_ffn_ref(x, router_w, w1, w2, w3):
        import jax, jax.numpy as jnp
        import numpy as np
        N_EXPERTS = 8
        TOP_K = 2
        D_MODEL = 512
        D_FF = 256
        BATCH, SEQ = (2, 512)

        def _trunc_normal(key, shape, fan_in):
            std = jnp.sqrt(1.0 / 3.0) / jnp.sqrt(float(fan_in))
            return jax.random.truncated_normal(key, -2.0, 2.0, shape, dtype=jnp.float32) * std
        B, S, D = x.shape
        xf = x.reshape(-1, D)
        n_tokens = xf.shape[0]
        logits = xf @ router_w.T
        topk_vals, topk_idx = jax.lax.top_k(logits, TOP_K)
        topk_weights = jax.nn.softmax(topk_vals, axis=-1)
        gate = jax.nn.silu(jnp.einsum('nd,edf->enf', xf, w1))
        value = jnp.einsum('nd,edf->enf', xf, w2)
        expert_out = jnp.einsum('enf,efd->end', gate * value, w3)
        tok = jnp.arange(n_tokens)[:, None]
        selected = expert_out[topk_idx, tok]
        out = jnp.sum(selected * topk_weights[..., None], axis=1)
        return out.reshape(B, S, D)
    h = _L0_tok_ref(x, L0_tok_Wqkv, L0_tok_b_qkv, L0_tok_Wout, L0_tok_b_out)
    h = h + _L0_attn_ref(_layernorm(h, axis=-1), L0_attn_Wq, L0_attn_bq, L0_attn_Wkv, L0_attn_bkv, L0_attn_Wo, L0_attn_bo)
    h = h + _L0_ffn_ref(_layernorm(h, axis=-1), L0_ffn_router_w, L0_ffn_w1, L0_ffn_w2, L0_ffn_w3)
    return h

_drawn_inputs = setup_inputs


def setup_inputs(seed=0):
    import zlib

    import numpy as np

    out = dict(_drawn_inputs(seed))
    spreads = {'L0_tok_b_qkv': (0.0, 0.1),
     'L0_tok_b_out': (0.0, 0.1),
     'L0_attn_bq': (0.0, 2.0),
     'L0_attn_bkv': (0.0, 0.1),
     'L0_attn_bo': (0.0, 0.1)}
    factors = {}
    for name, (base, spread) in spreads.items():
        noise = np.random.default_rng([zlib.crc32(name.encode()), seed]).standard_normal(out[name].shape)
        drawn = base * np.exp(spread * noise) if base else spread * noise
        out[name] = jnp.asarray(drawn.astype(out[name].dtype))
    for name, factor in factors.items():
        out[name] = (out[name] * factor).astype(out[name].dtype)
    return out
```

```python
import numpy as np
import concourse.bass as bass
from concourse import mybir
from contextlib import ExitStack

F32, F32R, BF16, U32 = mybir.dt.float32, mybir.dt.float32r, mybir.dt.bfloat16, mybir.dt.uint32
ACT, ALU, AX = mybir.ActivationFunctionType, mybir.AluOpType, mybir.AxisListType

P = 128
D = 512
KT = D // P
NH, HD = 16, 32
NG = 4
SEG = 64
T = 32 * P
NTILE = T // P
PAIR = 2 * P
NPAIR = NTILE // 2
SCALE = 1.0 / float(np.sqrt(HD))
EPS = 1e-5

NE = 8
NBLOCK = 2 * T // P + NE
I32 = mybir.dt.int32


def dilated_attention(nc, x_pairs, wqkv, bqk, bv, wout, bout, h1_dram, consts):
    ctx = ExitStack()
    with ctx:
        sb = lambda name, shape, dt=F32: ctx.enter_context(nc.sbuf_tensor("a_" + name, shape, dt))
        sem = lambda name: ctx.enter_context(nc.semaphore("a_" + name))
        bank = [ctx.enter_context(nc.psum_tensor(f"a_bank{i}", [P, 512], F32)) for i in range(8)]

        w_stage = sb("w_stage", [P, KT, 3 * D])
        wo_stage = sb("wo_stage", [P, KT, D])
        w_hi = sb("w_hi", [P, KT, 3 * D], F32R)
        w_lo = sb("w_lo", [P, KT, 3 * D], F32R)
        wo_hi = sb("wo_hi", [P, KT, D], F32R)
        wo_lo = sb("wo_lo", [P, KT, D], F32R)
        bqk_raw = sb("bqk_raw", [P, 8])
        bqk_sb = sb("bqk_sb", [P, 8])
        bv_sb = sb("bv_sb", [P, D])
        bout_sb = sb("bout_sb", [P, D])
        ident = sb("ident", [P, P])
        x_raw = sb("x_raw", [P, KT, PAIR])
        x_hi = sb("x_hi", [P, KT, PAIR], F32R)
        x_lo = sb("x_lo", [P, KT, PAIR], F32R)
        q_T = sb("q_T", [P, KT, PAIR])
        k_blk = sb("k_blk", [P, 4, KT, 4, SEG])
        v_blk = [sb(f"v_blk{a}", [P, 2, 8, 64]) for a in range(2)]
        neg_max = [sb(f"neg_max{a}", [P, NH]) for a in range(2)]
        probs = [sb(f"probs{a}", [P, NH, SEG]) for a in range(2)]
        probs_T = sb("probs_T", [P, 8, P])
        sums = [sb(f"sums{a}", [P, NH]) for a in range(2)]
        recip = [sb(f"recip{a}", [P, NH]) for a in range(2)]
        y_hi = [sb(f"y_hi{a}", [P, KT, P], F32R) for a in range(2)]
        y_lo = [sb(f"y_lo{a}", [P, KT, P], F32R) for a in range(2)]
        h1 = [sb(f"h1_{a}", [P, D]) for a in range(2)]

        consts_in, zeroed, scaled_bias = sem("consts_in"), sem("zeroed"), sem("scaled_bias")
        w_in = [sem(f"w_in{c}") for c in range(4)]
        w_hi_done, w_split = sem("w_hi_done"), sem("w_split")
        x_in, x_hi_done, x_split = sem("x_in"), sem("x_hi_done"), sem("x_split")
        qk_full, q_taken, k_taken = sem("qk_full"), sem("q_taken"), sem("k_taken")
        v_full, v_taken = sem("v_full"), sem("v_taken")
        s_full, max_done, exp_done = sem("s_full"), sem("max_done"), sem("exp_done")
        pT_full, pT_taken = sem("pT_full"), sem("pT_taken")
        recip_done, probs_scaled = sem("recip_done"), sem("probs_scaled")
        pv_full, y_hi_done, y_lo_done = sem("pv_full"), sem("y_hi_done"), sem("y_lo_done")
        out_full, h1_done = sem("out_full"), sem("h1_done")
        h1_stored = [sem(f"h1_stored{a}") for a in range(2)]

        pool_held = sem("pool_held")

        stage = [w_stage[:, :, c * D:(c + 1) * D] for c in range(3)] + [wo_stage[:, :, :]]
        his = [w_hi[:, :, c * D:(c + 1) * D] for c in range(3)] + [wo_hi[:, :, :]]
        los = [w_lo[:, :, c * D:(c + 1) * D] for c in range(3)] + [wo_lo[:, :, :]]

        block = ctx.enter_context(nc.Block())

        @block.sync
        def _(sp):
            sp.dma_start(x_raw[:], x_pairs[0, 0:1].rearrange("o p k t -> (o p) k t")).then_inc(x_in, 16)
            for c in range(3):
                sp.dma_start(stage[c], wqkv[:, :, c * D:(c + 1) * D]).then_inc(w_in[c], 16)
                if c == 0:
                    sp.dma_start(bqk_raw[:], bqk).then_inc(consts_in, 16)
                    sp.dma_start(ident[:], consts["ident"]).then_inc(consts_in, 16)
                    sp.dma_start(bv_sb[:], bv).then_inc(consts_in, 16)
                    sp.dma_start(bout_sb[:], bout).then_inc(consts_in, 16)
            sp.dma_start(stage[3], wout).then_inc(w_in[3], 16)

            def store(p, a):
                sp.wait_ge(h1_done, 2 * p + a + 1)
                sp.dma_start(h1_dram[bass.ds((2 * p + a) * P, P), :], h1[a][:]).then_inc(h1_stored[a], 16)

            def load(p):
                sp.wait_ge(x_split, p)
                sp.dma_start(x_raw[:], x_pairs[0, bass.ds(p, 1)].rearrange("o p k t -> (o p) k t")).then_inc(x_in, 16)

            load(1)
            with sp.Fori(1, NPAIR - 1) as p:
                load(p + 1)
                store(p - 1, 0)
                store(p - 1, 1)
            for p in (NPAIR - 2, NPAIR - 1):
                store(p, 0)
                store(p, 1)
            for a in range(2):
                sp.wait_ge(h1_stored[a], 16 * NPAIR)

        @block.gpsimd
        def _(pool):
            pool.memset(k_blk[:], 0.0).then_inc(zeroed, 1)
            pool.memset(v_blk[0][:], 0.0).then_inc(zeroed, 1)
            pool.memset(v_blk[1][:], 0.0).then_inc(zeroed, 1)

            def split(p):
                pool.wait_ge(x_in, 16 * (p + 1))
                pool.sem_inc(pool_held, 1)
                pool.tensor_copy(x_hi[:], x_raw[:]).then_inc(x_hi_done, 1)
                pool.wait_ge(x_hi_done, p + 1)
                pool.tensor_tensor(x_lo[:], x_raw[:], x_hi[:].bitcast(F32), ALU.subtract).then_inc(x_split, 1)

            split(0)
            with pool.Fori(1, NPAIR) as p:
                pool.wait_ge(v_full, 2 * p)
                split(p)

        @block.scalar
        def _(act):
            act.wait_ge(consts_in, 16 * 4)
            for c in range(4):
                act.wait_ge(w_in[c], 16)
                nc.scalar.copy(his[c], stage[c]).then_inc(w_hi_done, 1)
            act.wait_ge(scaled_bias, 1)
            act.wait_ge(zeroed, 3)

            def take_qk(p):
                for i in range(2):
                    act.wait_ge(qk_full, 4 * p + i + 1)
                    for ft in (2 * i, 2 * i + 1):
                        last = nc.scalar.activation(q_T[:, ft, :], bank[i][:, (ft % 2) * PAIR:(ft % 2 + 1) * PAIR],
                                                    ACT.Identity, bias=bqk_sb[:, ft:ft + 1], scale=SCALE)
                    last.then_inc(q_taken, 1)
                for i in range(2):
                    act.wait_ge(qk_full, 4 * p + i + 3)
                    for ft in (2 * i, 2 * i + 1):
                        for h in range(4):
                            r = slice(HD * h, HD * h + HD)
                            src = bank[2 + i][r, (ft % 2) * PAIR:(ft % 2 + 1) * PAIR]
                            last = nc.scalar.activation(k_blk[r, :, ft, h, :], src.rearrange("p (s k) -> p s k", s=4),
                                                        ACT.Identity, bias=bqk_sb[r, 4 + ft:5 + ft])
                    last.then_inc(k_taken, 1)

            def exps(p, a):
                for i in range(2):
                    act.wait_ge(max_done, 4 * p + 2 * a + i + 1)
                    for h in range(8 * i, 8 * i + 8):
                        last = nc.scalar.activation(probs[a][:, h, :], bank[2 * a + i][:, (h % 8) * SEG:(h % 8 + 1) * SEG],
                                                    ACT.Exp, bias=neg_max[a][:, h:h + 1], accum_out=sums[a][:, h:h + 1])
                    last.then_inc(exp_done, 1)

            def y_high(p, a):
                act.wait_ge(pv_full, 2 * p + a + 1)
                nc.scalar.copy(y_hi[a][:].rearrange("p k t -> p (k t)"), bank[5][:]).then_inc(y_hi_done, 1)

            def iteration(p, new, old):
                if new:
                    take_qk(p)
                if old:
                    y_high(p - 1, 0)
                if new:
                    exps(p, 0)
                if old:
                    y_high(p - 1, 1)
                if new:
                    exps(p, 1)

            iteration(0, True, False)
            with act.Fori(1, NPAIR) as p:
                iteration(p, True, True)
            iteration(NPAIR, False, True)

        @block.vector
        def _(dve):
            dve.wait_ge(consts_in, 16 * 4)
            nc.vector.tensor_scalar(bqk_sb[:, 0:4], bqk_raw[:, 0:4], SCALE, None, ALU.mult)
            nc.vector.tensor_copy(bqk_sb[:, 4:8], bqk_raw[:, 4:8]).then_inc(scaled_bias, 1)
            for c in range(4):
                dve.wait_ge(w_hi_done, c + 1)
                nc.vector.tensor_tensor(los[c], stage[c], his[c].bitcast(F32), ALU.subtract).then_inc(w_split, 1)
            dve.wait_ge(zeroed, 3)

            def take_probs_T(p, a):
                for i in range(2):
                    dve.wait_ge(pT_full, 4 * p + 2 * a + i + 1)
                    nc.vector.tensor_copy(probs_T[:, 4 * i:4 * i + 4, :].rearrange("p h q -> p (h q)"),
                                          bank[4 + i][:]).then_inc(pT_taken, 1)

            def take_v(p, a, old):
                dve.wait_ge(v_full, 2 * p + a + 1)
                if old:
                    dve.wait_ge(pv_full, 2 * p + a - 1)
                for s in range(2):
                    for r in range(2):
                        src = bank[6 + a][64 * s:64 * s + 64, :].rearrange("p (h r d) -> p r h d", r=2, d=HD)[:, r]
                        b = bv_sb[64 * s:64 * s + 64, :].rearrange("p (h r d) -> p r h d", r=2, d=HD)[:, r]
                        last = nc.vector.tensor_tensor(v_blk[a][64 * r:64 * r + 64, s, :, HD * r:HD * r + HD],
                                                       src, b, ALU.add)
                last.then_inc(v_taken, 1)

            def scale_probs(p, a):
                for i in range(2):
                    n = 4 * p + 2 * a + i + 1
                    hs = slice(8 * i, 8 * i + 8)
                    dve.wait_ge(exp_done, n)
                    nc.vector.reciprocal(recip[a][:, hs], sums[a][:, hs]).then_inc(recip_done, 1)
                    dve.wait_ge(recip_done, n)
                    nc.vector.tensor_tensor(probs[a][:, hs, :], probs[a][:, hs, :],
                                            recip[a][:, hs].unsqueeze(2).to_broadcast([P, 8, SEG]), ALU.mult).then_inc(probs_scaled, 1)

            def y_low(p, a):
                dve.wait_ge(y_hi_done, 2 * p + a + 1)
                nc.vector.tensor_tensor(y_lo[a][:].rearrange("p k t -> p (k t)"), bank[5][:],
                                        y_hi[a][:].rearrange("p k t -> p (k t)").bitcast(F32), ALU.subtract).then_inc(y_lo_done, 1)

            def maxima(p, a):
                for i in range(2):
                    dve.wait_ge(s_full, 4 * p + 2 * a + i + 1)
                    nc.vector.tensor_reduce(neg_max[a][:, 8 * i:8 * i + 8], bank[2 * a + i][:].rearrange("p (h k) -> p h k", k=SEG),
                                            AX.X, ALU.max, negate=True).then_inc(max_done, 1)

            def take_out(p, a, peeled):
                dve.wait_ge(out_full, 2 * p + a + 1)
                if not peeled:
                    dve.wait_ge(h1_stored[a], 16 * p)
                nc.vector.tensor_tensor(h1[a][:], bank[6 + a][:], bout_sb[:], ALU.add).then_inc(h1_done, 1)

            def iteration(p, new, old, first_old=False):
                if old:
                    scale_probs(p - 1, 0)
                    take_probs_T(p - 1, 0)
                    scale_probs(p - 1, 1)
                if new:
                    take_v(p, 0, old)
                if old:
                    y_low(p - 1, 0)
                    take_probs_T(p - 1, 1)
                if new:
                    maxima(p, 0)
                    maxima(p, 1)
                if old:
                    y_low(p - 1, 1)
                if new:
                    take_v(p, 1, old)
                if old:
                    take_out(p - 1, 0, first_old)
                    take_out(p - 1, 1, first_old)

            iteration(0, True, False)
            iteration(1, True, True, True)
            with dve.Fori(2, NPAIR) as p:
                iteration(p, True, True)
            iteration(NPAIR, False, True)

        @block.tensor
        def _(pe):
            pe.wait_ge(consts_in, 16 * 4)

            def project_qk(p, first):
                pe.wait_ge(x_split, p + 1)
                for i in range(4):
                    if first:
                        pe.wait_ge(w_split, i // 2 + 1)
                    else:
                        pe.wait_ge(exp_done, 4 * (p - 1) + i + 1)
                    for half in range(2):
                        e = (2 * i + half) * P
                        dst = bank[i][:, half * PAIR:(half + 1) * PAIR]
                        n = 0
                        for kt in range(KT):
                            for w, x in ((w_hi, x_hi), (w_hi, x_lo), (w_lo, x_hi)):
                                last = nc.tensor.matmul(dst, w[:, kt, e:e + P], x[:, kt, :], start=n == 0, stop=n == 3 * KT - 1)
                                n += 1
                    last.then_inc(qk_full, 1)

            def project_v(p, a, first):
                if first:
                    pe.wait_ge(w_split, 3)
                if not first:
                    pe.wait_ge(h1_done, 2 * (p - 1) + a - 1) if not isinstance(p, int) or p > 1 else None
                n = 0
                for kt in range(KT):
                    for x, w in ((x_hi, w_hi), (x_hi, w_lo), (x_lo, w_hi)):
                        last = nc.tensor.matmul(bank[6 + a][:], x[:, kt, a * P:(a + 1) * P], w[:, kt, 2 * D:3 * D],
                                                start=n == 0, stop=n == 3 * KT - 1)
                        n += 1
                last.then_inc(v_full, 1)

            def transpose_probs(p, a, peeled):
                if not peeled or a:
                    pe.wait_ge(y_lo_done, 2 * p + a)
                for i in range(2):
                    pe.wait_ge(probs_scaled, 4 * p + 2 * a + i + 1)
                    for hp in range(4 * i, 4 * i + 4):
                        last = nc.tensor.transpose(bank[4 + i][:, (hp % 4) * P:(hp % 4 + 1) * P],
                                                   probs[a][:, 2 * hp:2 * hp + 2, :].rearrange("p h k -> p (h k)"), ident[:])
                    last.then_inc(pT_full, 1)

            def scores(p, a):
                pe.wait_ge(q_taken, 2 * (p + 1))
                pe.wait_ge(k_taken, 2 * (p + 1))
                for i in range(2):
                    for ft in (2 * i, 2 * i + 1):
                        for s in range(2):
                            c = (ft % 2) * PAIR
                            last = nc.tensor.matmul(bank[2 * a + i][64 * s:64 * s + 64, c:c + PAIR],
                                                    q_T[:, ft, a * P + s * SEG:a * P + (s + 1) * SEG],
                                                    k_blk[:, 2 * a + s, ft, :, :].rearrange("p h k -> p (h k)"), start=True, stop=True)
                    last.then_inc(s_full, 1)

            def weigh_values(p, a):
                pe.wait_ge(pT_taken, 4 * p + 2 * a + 2)
                pe.wait_ge(v_taken, 2 * p + a + 1)
                for hp in range(8):
                    for s in range(2):
                        r, c = hp % 2, (hp // 2) * P + s * SEG
                        last = nc.tensor.matmul(bank[5][64 * r:64 * r + 64, c:c + SEG], v_blk[a][:, s, hp, :],
                                                probs_T[:, hp, s * SEG:(s + 1) * SEG], start=True, stop=True)
                last.then_inc(pv_full, 1)

            def project_out(p, a, new):
                if new:
                    pe.wait_ge(v_taken, 2 * (p + 1) + a + 1)
                pe.wait_ge(w_split, 4)
                pe.wait_ge(y_lo_done, 2 * p + a + 1)
                n = 0
                for ft in range(KT):
                    for y, w in ((y_hi[a], wo_hi), (y_hi[a], wo_lo), (y_lo[a], wo_hi)):
                        last = nc.tensor.matmul(bank[6 + a][:], y[:, ft, :], w[:, ft, :], start=n == 0, stop=n == 3 * KT - 1)
                        n += 1
                last.then_inc(out_full, 1)

            def iteration(p, new, old, first_old=False):
                if new:
                    project_qk(p, not old)
                if old:
                    transpose_probs(p - 1, 0, first_old)
                if new:
                    project_v(p, 0, not old)
                if old:
                    weigh_values(p - 1, 0)
                if new:
                    project_v(p, 1, not old)
                if old:
                    transpose_probs(p - 1, 1, first_old)
                if new:
                    scores(p, 0)
                    scores(p, 1)
                if old:
                    weigh_values(p - 1, 1)
                    project_out(p - 1, 0, new)
                    project_out(p - 1, 1, new)

            iteration(0, True, False)
            iteration(1, True, True, True)
            with pe.Fori(2, NPAIR) as p:
                iteration(p, True, True)
            iteration(NPAIR, False, True)


def causal_attention(nc, h1_dram, wq, wkv, wo, bq, bkv, bo, router, h2_dram, xn_dram, logits, consts):
    ctx = ExitStack()
    with ctx:
        sb = lambda name, shape, dt=F32: ctx.enter_context(nc.sbuf_tensor("b_" + name, shape, dt))
        sem = lambda name: ctx.enter_context(nc.semaphore("b_" + name))
        bank = [ctx.enter_context(nc.psum_tensor(f"b_bank{i}", [P, 512], F32)) for i in range(8)]

        wq_stage, wkv_stage, wo_stage = sb("wq_stage", [P, KT, D]), sb("wkv_stage", [P, KT, PAIR]), sb("wo_stage", [P, KT, D])
        wq_hi, wq_lo = sb("wq_hi", [P, KT, D], F32R), sb("wq_lo", [P, KT, D], F32R)
        wkv_hi, wkv_lo = sb("wkv_hi", [P, KT, PAIR], F32R), sb("wkv_lo", [P, KT, PAIR], F32R)
        wo_hi, wo_lo = sb("wo_hi", [P, KT, D], F32R), sb("wo_lo", [P, KT, D], F32R)
        router_sb = sb("router", [P, KT, NE])
        bq_sb, bkv_sb, bo_sb = sb("bq", [P, D]), sb("bkv", [P, PAIR]), sb("bo", [P, D])
        cos_sb, sin_sb = sb("cos", [P, HD]), sb("sin", [P, HD])
        ident = sb("ident", [P, P])
        ident_16 = sb("ident_16", [P, P], BF16)
        mask_f = sb("mask_f", [P, P])
        mask_16 = sb("mask_16", [P, NG, P], BF16)
        minus_half = sb("minus_half", [P, 1])

        h1 = sb("h1", [P, D])
        stats1, mv1, rstd1 = sb("stats1", [P, 6]), sb("mv1", [P, 2]), sb("rstd1", [P, 2])
        xn1 = sb("xn1", [P, D])
        xT_hi, xT_lo = sb("xT_hi", [P, KT, P], F32R), sb("xT_lo", [P, KT, P], F32R)
        qk = sb("qk", [P, NH + NG, HD])
        v = sb("v", [P, NG * HD])
        rope_c, rope_s = sb("rope_c", [P, NH + NG, HD]), sb("rope_s", [P, NH + NG, HD])
        q_rot = sb("q_rot", [P, 4, NG, HD])
        k_rot = sb("k_rot", [P, NG * (P + HD)])
        qT_hi, qT_lo = sb("qT_hi", [P, 4, P], F32R), sb("qT_lo", [P, 4, P], F32R)
        kT_hi, kT_lo = sb("kT_hi", [P, NG * P], F32R), sb("kT_lo", [P, NG * P], F32R)
        neg_max, sums, recip = sb("neg_max", [P, NH]), sb("sums", [P, NH]), sb("recip", [P, NH])
        probs = sb("probs", [P, 4, NG, P])
        probs_T = sb("probs_T", [P, NG, 4, P])
        y_hi, y_lo = sb("y_hi", [P, 4, P], F32R), sb("y_lo", [P, 4, P], F32R)
        resid, resid_b = sb("resid", [P, D]), sb("resid_b", [P, D])
        h2 = sb("h2", [P, D])
        stats2, mv2, rstd2 = sb("stats2", [P, 6]), sb("mv2", [P, 2]), sb("rstd2", [P, 2])
        xn2 = sb("xn2", [P, D])
        xn2_T = sb("xn2_T", [P, KT, P])

        consts_in, zeroed, consts_16 = sem("consts_in"), sem("zeroed"), sem("consts_16")
        w_in = [sem(f"w_in{c}") for c in range(3)]
        w_hi_done, w_split = sem("w_hi_done"), sem("w_split")
        h1_in, resid_in, resid_done = sem("h1_in"), sem("resid_in"), sem("resid_done")
        stats1_done, mv1_done, eps1_done, rstd1_done, xn1_done = (sem(n) for n in ("stats1_done", "mv1_done", "eps1_done", "rstd1_done", "xn1_done"))
        stats2_done, mv2_done, eps2_done, rstd2_done, xn2_done = (sem(n) for n in ("stats2_done", "mv2_done", "eps2_done", "rstd2_done", "xn2_done"))
        xT_full, xT_hi_done, xT_lo_done = sem("xT_full"), sem("xT_hi_done"), sem("xT_lo_done")
        q_full, kv_full, qk_taken, v_taken = sem("q_full"), sem("kv_full"), sem("qk_taken"), sem("v_taken")
        cos_done, sin_done, rope_done = sem("cos_done"), sem("sin_done"), sem("rope_done")
        qT_full, kT_full, qkT_hi_done, qkT_lo_done = sem("qT_full"), sem("kT_full"), sem("qkT_hi_done"), sem("qkT_lo_done")
        s_full, max_done, exp_done = sem("s_full"), sem("max_done"), sem("exp_done")
        recip_done, probs_scaled = sem("recip_done"), sem("probs_scaled")
        pT_full, pT_taken, pv_full = sem("pT_full"), sem("pT_taken"), sem("pv_full")
        y_hi_done, y_lo_done, wo_full = sem("y_hi_done"), sem("y_lo_done"), sem("wo_full")
        h2_done, h2_stored, xn2_stored = sem("h2_done"), sem("h2_stored"), sem("xn2_stored")
        xn2_T_full, xn2_T_taken = sem("xn2_T_full"), sem("xn2_T_taken")
        logits_full, logits_taken = sem("logits_full"), sem("logits_taken")

        dve_held, pool_held = sem("dve_held"), sem("pool_held")

        stage = [wq_stage, wkv_stage, wo_stage]
        his, los = [wq_hi, wkv_hi, wo_hi], [wq_lo, wkv_lo, wo_lo]
        k_diag = k_rot[:].rearrange("p (g c) -> p g c", g=NG)[:, :, 0:HD]

        block = ctx.enter_context(nc.Block())

        @block.sync
        def _(sp):
            def load_h1(t):
                sp.wait_ge(xn1_done, t)
                sp.dma_start(h1[:], h1_dram[bass.ds(t * P, P), :]).then_inc(h1_in, 16)

            def load_residual(t):
                sp.wait_ge(resid_done, t)
                sp.dma_start(resid[:], h1_dram[bass.ds(t * P, P), :]).then_inc(resid_in, 16)

            def store(t):
                sp.wait_ge(h2_done, t + 1)
                sp.dma_start(h2_dram[bass.ds(t * P, P), :], h2[:]).then_inc(h2_stored, 16)
                sp.wait_ge(xn2_done, t + 1)
                sp.dma_start(xn_dram[bass.ds(t * P, P), :], xn2[:]).then_inc(xn2_stored, 16)

            sp.dma_start(h1[:], h1_dram[0:P, :]).then_inc(h1_in, 16)
            for src, dst in ((consts["ident"], ident), (consts["mask"], mask_f), (consts["cos"], cos_sb), (consts["sin"], sin_sb),
                             (bq, bq_sb), (bkv, bkv_sb), (bo, bo_sb), (router, router_sb)):
                sp.dma_start(dst[:], src).then_inc(consts_in, 16)
            for c, src in enumerate((wq, wkv, wo)):
                sp.dma_start(stage[c][:], src).then_inc(w_in[c], 16)
            sp.dma_start(resid[:], h1_dram[0:P, :]).then_inc(resid_in, 16)
            load_h1(1)
            load_h1(2)
            with sp.Fori(2, NTILE - 1) as t:
                load_h1(t + 1)
                load_residual(t - 1)
                store(t - 2)
            load_residual(NTILE - 2)
            store(NTILE - 3)
            load_residual(NTILE - 1)
            store(NTILE - 2)
            store(NTILE - 1)
            sp.wait_ge(h2_stored, 16 * NTILE)
            sp.wait_ge(xn2_stored, 16 * NTILE)

        @block.gpsimd
        def _(pool):
            pool.memset(k_rot[:], 0.0).then_inc(zeroed, 1)
            pool.memset(minus_half[:], -0.5).then_inc(zeroed, 1)
            pool.wait_ge(zeroed, 2)
            pool.wait_ge(consts_in, 16 * 8)

            def rstd(t, mv, out, mv_done, eps_done, done):
                pool.wait_ge(mv_done, t + 1)
                pool.sem_inc(pool_held, 1)
                pool.tensor_scalar_add(out[:, 0:1], mv[:, 1:2], EPS).then_inc(eps_done, 1)
                pool.wait_ge(eps_done, t + 1)
                pool.tensor_tensor(out[:, 1:2], out[:, 0:1], minus_half[:], ALU.pow).then_inc(done, 1)

            def rotate(t):
                pool.wait_ge(qk_taken, t + 1)
                pool.tensor_tensor(rope_s[:, :, 0::2], qk[:, :, 1::2], sin_sb[:, 0::2].unsqueeze(1).to_broadcast([P, NH + NG, HD // 2]), ALU.mult)
                pool.tensor_tensor(rope_s[:, :, 1::2], qk[:, :, 0::2], sin_sb[:, 1::2].unsqueeze(1).to_broadcast([P, NH + NG, HD // 2]), ALU.mult).then_inc(sin_done, 1)

            def residual(t):
                pool.wait_ge(resid_in, 16 * (t + 1))
                if not isinstance(t, int) or t > 0:
                    pool.wait_ge(h2_done, t)
                pool.tensor_tensor(resid_b[:], resid[:], bo_sb[:], ALU.add).then_inc(resid_done, 1)

            def iteration(t, new, late, next_norm):
                if new:
                    rotate(t)
                if late:
                    residual(t - 2)
                    rstd(t - 2, mv2, rstd2, mv2_done, eps2_done, rstd2_done)
                if next_norm:
                    rstd(t + 1, mv1, rstd1, mv1_done, eps1_done, rstd1_done)

            rstd(0, mv1, rstd1, mv1_done, eps1_done, rstd1_done)
            iteration(0, True, False, True)
            iteration(1, True, False, True)
            iteration(2, True, True, True)
            with pool.Fori(3, NTILE - 1) as t:
                iteration(t, True, True, True)
            iteration(NTILE - 1, True, True, False)
            iteration(NTILE, False, True, False)
            iteration(NTILE + 1, False, True, False)

        @block.scalar
        def _(act):
            act.wait_ge(consts_in, 16 * 8)
            nc.scalar.copy(ident_16[:], ident[:])
            for g in range(NG):
                last = nc.scalar.copy(mask_16[:, g, :], mask_f[:])
            last.then_inc(consts_16, 1)
            for c in range(3):
                act.wait_ge(w_in[c], 16)
                nc.scalar.copy(his[c][:], stage[c][:]).then_inc(w_hi_done, 1)

            def xT_high(t):
                act.wait_ge(xT_full, t + 1)
                nc.scalar.copy(xT_hi[:].rearrange("p k t -> p (k t)"), bank[7][:]).then_inc(xT_hi_done, 1)

            def qkT_high(t):
                act.wait_ge(qT_full, t + 1)
                nc.scalar.activation(qT_hi[:].rearrange("p j t -> p (j t)"), bank[7][:], ACT.Copy, scale=SCALE).then_inc(qkT_hi_done, 1)
                act.wait_ge(kT_full, t + 1)
                nc.scalar.copy(kT_hi[:], bank[6][:]).then_inc(qkT_hi_done, 1)

            def exps(t):
                for j in range(4):
                    act.wait_ge(max_done, 4 * t + j + 1)
                    for g in range(NG):
                        h = 4 * j + g
                        last = nc.scalar.activation(probs[:, j, g, :], bank[j][:, g * P:(g + 1) * P], ACT.Exp,
                                                    bias=neg_max[:, h:h + 1], accum_out=sums[:, h:h + 1])
                    last.then_inc(exp_done, 1)

            def take_probs_T(t):
                for j in range(4):
                    act.wait_ge(pT_full, 4 * t + j + 1)
                    nc.scalar.copy(probs_T[:, :, j, :], bank[j][:].rearrange("p (g q) -> p g q", g=NG)).then_inc(pT_taken, 1)

            def y_high(t):
                act.wait_ge(pv_full, t + 1)
                nc.scalar.copy(y_hi[:].rearrange("p j t -> p (j t)"), bank[4][:]).then_inc(y_hi_done, 1)

            def take_xn2_T(t):
                act.wait_ge(xn2_T_full, t + 1)
                nc.scalar.copy(xn2_T[:].rearrange("p k t -> p (k t)"), bank[7][:]).then_inc(xn2_T_taken, 1)

            def iteration(t, new, mid, late, next_norm):
                if mid:
                    take_probs_T(t - 1)
                if new:
                    qkT_high(t)
                if late:
                    take_xn2_T(t - 2)
                if mid:
                    y_high(t - 1)
                if next_norm:
                    xT_high(t + 1)
                if new:
                    exps(t)

            xT_high(0)
            iteration(0, True, False, False, True)
            iteration(1, True, True, False, True)
            with act.Fori(2, NTILE - 1) as t:
                iteration(t, True, True, True, True)
            iteration(NTILE - 1, True, True, True, False)
            iteration(NTILE, False, True, True, False)
            iteration(NTILE + 1, False, False, True, False)

        @block.vector
        def _(dve):
            dve.wait_ge(consts_in, 16 * 8)
            dve.wait_ge(zeroed, 2)

            def norm_stats(t, src, stats, mv, stats_done, mv_done):
                nc.vector.bn_stats(stats[:], src[:]).then_inc(stats_done, 1)
                dve.wait_ge(stats_done, t + 1)
                dve.sem_inc(dve_held, 1)
                nc.vector.bn_aggr(mv[:], stats[:]).then_inc(mv_done, 1)

            def norm(t, out, src, mv, rstd, rstd_done, done):
                dve.wait_ge(rstd_done, t + 1)
                nc.vector.tensor_scalar(out[:], src[:], mv[:, 0:1], rstd[:, 1:2], ALU.subtract, ALU.mult).then_inc(done, 1)

            def stats_of_h1(t):
                dve.wait_ge(h1_in, 16 * (t + 1))
                norm_stats(t, h1, stats1, mv1, stats1_done, mv1_done)

            def norm_h1(t):
                norm(t, xn1, h1, mv1, rstd1, rstd1_done, xn1_done)

            def xT_low(t):
                dve.wait_ge(xT_hi_done, t + 1)
                nc.vector.tensor_tensor(xT_lo[:].rearrange("p k t -> p (k t)"), bank[7][:],
                                        xT_hi[:].rearrange("p k t -> p (k t)").bitcast(F32), ALU.subtract).then_inc(xT_lo_done, 1)

            def take_qk(t):
                dve.wait_ge(q_full, t + 1)
                nc.vector.tensor_tensor(qk[:, 0:NH, :].rearrange("p h d -> p (h d)"), bank[4][:], bq_sb[:], ALU.add)
                dve.wait_ge(kv_full, t + 1)
                nc.vector.tensor_tensor(qk[:, NH:, :].rearrange("p h d -> p (h d)"), bank[5][:, 0:P], bkv_sb[:, 0:P], ALU.add).then_inc(qk_taken, 1)
                dve.wait_ge(qk_taken, t + 1)
                nc.vector.tensor_tensor(rope_c[:], qk[:], cos_sb[:].unsqueeze(1).to_broadcast([P, NH + NG, HD]), ALU.mult).then_inc(cos_done, 1)

            def rope(t):
                dve.wait_ge(cos_done, t + 1)
                dve.wait_ge(sin_done, t + 1)
                nc.vector.tensor_tensor(q_rot[:].rearrange("p j g d -> p g j d"), rope_c[:, 0:NH, :].rearrange("p (g j) d -> p g j d", g=NG),
                                        rope_s[:, 0:NH, :].rearrange("p (g j) d -> p g j d", g=NG), ALU.add)
                nc.vector.tensor_tensor(k_diag, rope_c[:, NH:, :], rope_s[:, NH:, :], ALU.add).then_inc(rope_done, 1)

            def qkT_low(t):
                dve.wait_ge(qkT_hi_done, 2 * t + 1)
                nc.vector.scalar_tensor_tensor(qT_lo[:].rearrange("p j t -> p (j t)"), bank[7][:], SCALE,
                                               qT_hi[:].rearrange("p j t -> p (j t)").bitcast(F32), ALU.mult, ALU.subtract).then_inc(qkT_lo_done, 1)
                dve.wait_ge(qkT_hi_done, 2 * t + 2)
                nc.vector.tensor_tensor(kT_lo[:], bank[6][:], kT_hi[:].bitcast(F32), ALU.subtract).then_inc(qkT_lo_done, 1)

            def maxima(t):
                for j in range(4):
                    dve.wait_ge(s_full, 4 * t + j + 1)
                    nc.vector.tensor_reduce(neg_max[:, 4 * j:4 * j + 4], bank[j][:].rearrange("p (g k) -> p g k", g=NG),
                                            AX.X, ALU.max, negate=True).then_inc(max_done, 1)

            def scale_probs(t):
                for j in range(4):
                    hs = slice(4 * j, 4 * j + 4)
                    dve.wait_ge(exp_done, 4 * t + j + 1)
                    nc.vector.reciprocal(recip[:, hs], sums[:, hs]).then_inc(recip_done, 1)
                    dve.wait_ge(recip_done, 4 * t + j + 1)
                    nc.vector.tensor_tensor(probs[:, j], probs[:, j], recip[:, hs].unsqueeze(2).to_broadcast([P, NG, P]),
                                            ALU.mult).then_inc(probs_scaled, 1)

            def take_v(t, mid):
                if mid:
                    dve.wait_ge(pv_full, t)
                dve.wait_ge(kv_full, t + 1)
                nc.vector.tensor_tensor(v[:], bank[5][:, P:2 * P], bkv_sb[:, P:2 * P], ALU.add).then_inc(v_taken, 1)

            def y_low(t):
                dve.wait_ge(y_hi_done, t + 1)
                nc.vector.tensor_tensor(y_lo[:].rearrange("p j t -> p (j t)"), bank[4][:],
                                        y_hi[:].rearrange("p j t -> p (j t)").bitcast(F32), ALU.subtract).then_inc(y_lo_done, 1)

            def residual_sum(t):
                dve.wait_ge(wo_full, t + 1)
                dve.wait_ge(resid_done, t + 1)
                if not isinstance(t, int) or t > 0:
                    dve.wait_ge(h2_stored, 16 * t)
                nc.vector.tensor_tensor(h2[:], bank[6][:], resid_b[:], ALU.add).then_inc(h2_done, 1)
                dve.wait_ge(h2_done, t + 1)
                norm_stats(t, h2, stats2, mv2, stats2_done, mv2_done)

            def norm_h2(t):
                if not isinstance(t, int) or t > 0:
                    dve.wait_ge(xn2_stored, 16 * t)
                norm(t, xn2, h2, mv2, rstd2, rstd2_done, xn2_done)

            def take_logits(t):
                dve.wait_ge(logits_full, t + 1)
                nc.vector.tensor_copy(logits[:, bass.ds(t * NE, NE)], bank[6][:, 0:NE]).then_inc(logits_taken, 1)

            def iteration(t, new, mid, late, next_norm):
                if new:
                    take_qk(t)
                if mid:
                    scale_probs(t - 1)
                if new:
                    rope(t)
                if late:
                    residual_sum(t - 2)
                if next_norm:
                    stats_of_h1(t + 1)
                if late:
                    norm_h2(t - 2)
                if next_norm:
                    norm_h1(t + 1)
                if new:
                    qkT_low(t)
                if late:
                    take_logits(t - 2)
                if mid:
                    y_low(t - 1)
                if new:
                    take_v(t, mid)
                if next_norm:
                    xT_low(t + 1)
                if new:
                    maxima(t)

            stats_of_h1(0)
            norm_h1(0)
            for c in range(3):
                dve.wait_ge(w_hi_done, c + 1)
                nc.vector.tensor_tensor(los[c][:], stage[c][:], his[c][:].bitcast(F32), ALU.subtract).then_inc(w_split, 1)
            xT_low(0)
            iteration(0, True, False, False, True)
            iteration(1, True, True, False, True)
            iteration(2, True, True, True, True)
            with dve.Fori(3, NTILE - 1) as t:
                iteration(t, True, True, True, True)
            iteration(NTILE - 1, True, True, True, False)
            iteration(NTILE, False, True, True, False)
            iteration(NTILE + 1, False, False, True, False)

        @block.tensor
        def _(pe):
            pe.wait_ge(consts_in, 16 * 8)
            pe.wait_ge(consts_16, 1)

            def three_products(dst, parts):
                n, count = 0, 3 * len(parts)
                for a_hi, a_lo, b_hi, b_lo in parts:
                    for a, b in ((a_hi, b_hi), (a_hi, b_lo), (a_lo, b_hi)):
                        last = nc.tensor.matmul(dst, a, b, start=n == 0, stop=n == count - 1)
                        n += 1
                return last

            def transpose_x(t):
                pe.wait_ge(xn1_done, t + 1)
                for kt in range(KT):
                    last = nc.tensor.transpose(bank[7][:, kt * P:(kt + 1) * P], xn1[:, kt * P:(kt + 1) * P], ident[:])
                last.then_inc(xT_full, 1)

            def project(t):
                pe.wait_ge(xT_lo_done, t + 1)
                if not isinstance(t, int) or t > 1:
                    pe.wait_ge(y_lo_done, t - 1)
                three_products(bank[4][:], [(xT_hi[:, k], xT_lo[:, k], wq_hi[:, k], wq_lo[:, k]) for k in range(KT)]).then_inc(q_full, 1)
                if not isinstance(t, int) or t > 0:
                    pe.wait_ge(v_taken, t)
                three_products(bank[5][:, 0:PAIR], [(xT_hi[:, k], xT_lo[:, k], wkv_hi[:, k], wkv_lo[:, k]) for k in range(KT)]).then_inc(kv_full, 1)

            def transpose_qk(t):
                pe.wait_ge(rope_done, t + 1)
                for j in range(4):
                    last = nc.tensor.transpose(bank[7][:, j * P:(j + 1) * P], q_rot[:, j].rearrange("p g d -> p (g d)"), ident[:])
                last.then_inc(qT_full, 1)
                if not isinstance(t, int) or t > 1:
                    pe.wait_ge(h2_done, t - 1)
                for g in range(NG):
                    last = nc.tensor.transpose(bank[6][:, g * P:(g + 1) * P], k_rot[:, g * P:(g + 1) * P], ident[:])
                last.then_inc(kT_full, 1)

            def scores(t):
                pe.wait_ge(qkT_lo_done, 2 * (t + 1))
                for j in range(4):
                    if not isinstance(t, int) or t > 0:
                        pe.wait_ge(pT_taken, 4 * (t - 1) + j + 1)
                    nc.tensor.matmul(bank[j][:], ident_16[:], mask_16[:].rearrange("p g k -> p (g k)"), start=True, stop=False)
                    for n, (q, k) in enumerate(((qT_hi, kT_hi), (qT_hi, kT_lo), (qT_lo, kT_hi))):
                        last = nc.tensor.matmul(bank[j][:], q[:, j], k[:], start=False, stop=n == 2)
                    last.then_inc(s_full, 1)

            def transpose_probs(t):
                for j in range(4):
                    pe.wait_ge(probs_scaled, 4 * t + j + 1)
                    for g in range(NG):
                        last = nc.tensor.transpose(bank[j][:, g * P:(g + 1) * P], probs[:, j, g], ident[:])
                    last.then_inc(pT_full, 1)

            def weigh_values(t):
                pe.wait_ge(pT_taken, 4 * (t + 1))
                pe.wait_ge(v_taken, t + 1)
                if t != NTILE - 1 if isinstance(t, int) else True:
                    pe.wait_ge(qk_taken, t + 2)
                for g in range(NG):
                    last = nc.tensor.matmul(bank[4][g * HD:(g + 1) * HD, :], v[:, g * HD:(g + 1) * HD],
                                            probs_T[:, g].rearrange("p j q -> p (j q)"), start=True, stop=True)
                last.then_inc(pv_full, 1)

            def project_out(t):
                pe.wait_ge(w_split, 3)
                pe.wait_ge(y_lo_done, t + 1)
                if not isinstance(t, int) or t > 0:
                    pe.wait_ge(logits_taken, t)
                three_products(bank[6][:], [(y_hi[:, j], y_lo[:, j], wo_hi[:, j], wo_lo[:, j]) for j in range(4)]).then_inc(wo_full, 1)

            def route(t, new):
                pe.wait_ge(xn2_done, t + 1)
                if new:
                    pe.wait_ge(qkT_lo_done, 2 * (t + 3))
                elif isinstance(t, int):
                    pe.wait_ge(xn2_T_taken, t)
                for kt in range(KT):
                    last = nc.tensor.transpose(bank[7][:, kt * P:(kt + 1) * P], xn2[:, kt * P:(kt + 1) * P], ident[:])
                last.then_inc(xn2_T_full, 1)
                pe.wait_ge(xn2_T_taken, t + 1)
                for kt in range(KT):
                    last = nc.tensor.matmul(bank[6][:, 0:NE], xn2_T[:, kt], router_sb[:, kt], start=kt == 0, stop=kt == KT - 1)
                last.then_inc(logits_full, 1)

            def iteration(t, new, mid, late, next_norm):
                if new:
                    project(t)
                if late:
                    project_out(t - 2)
                if mid:
                    transpose_probs(t - 1)
                if new:
                    transpose_qk(t)
                if late:
                    route(t - 2, new)
                if mid:
                    weigh_values(t - 1)
                if next_norm:
                    if not late:
                        pe.wait_ge(qkT_lo_done, 2 * (t + 1))
                    transpose_x(t + 1)
                if new:
                    scores(t)

            transpose_x(0)
            pe.wait_ge(w_split, 2)
            iteration(0, True, False, False, True)
            iteration(1, True, True, False, True)
            iteration(2, True, True, True, True)
            with pe.Fori(3, NTILE - 1) as t:
                iteration(t, True, True, True, True)
            iteration(NTILE - 1, True, True, True, False)
            iteration(NTILE, False, True, True, False)
            iteration(NTILE + 1, False, False, True, False)


def routed_experts(nc, logits, w12, w3, xn_dram, wt_dram, out_dram, consts):
    ctx = ExitStack()
    with ctx:
        sb = lambda name, shape, dt=F32: ctx.enter_context(nc.sbuf_tensor("d_" + name, shape, dt))
        sem = lambda name: ctx.enter_context(nc.semaphore("d_" + name))
        bank = [ctx.enter_context(nc.psum_tensor(f"d_bank{i}", [P, 512], F32)) for i in range(8)]

        w12_sb = sb("w12", [P, NE * KT * D])
        w3_sb = sb("w3", [P, NE * 2 * D])
        ident = sb("ident", [P, P])
        before = sb("before", [P, P])
        ones = sb("ones", [P, P])
        expert_m8 = sb("expert_m8", [P, NE])
        expert_low = sb("expert_low", [P, NE, NE])
        rows_full = sb("rows_full", [P, NTILE])
        part_1 = sb("part_1", [P, 1])
        part_pad = sb("part_pad", [P, 1])
        assign_ik = sb("assign_ik", [P, 2 * NTILE])
        col = sb("col", [P, P])
        zero = sb("zero", [P, D])

        TE = [P, NTILE, NE]
        top = [sb(f"top{k}", [P, NTILE]) for k in range(2)]
        hit, hit_m8 = sb("hit", TE), sb("hit_m8", TE)
        choice = sb("choice", [P, NTILE])
        onehot = [sb(f"onehot{k}", TE) for k in range(2)]
        rest = sb("rest", TE)
        gap, exp_gap, denom = sb("gap", [P, NTILE]), sb("exp_gap", [P, NTILE]), sb("denom", [P, NTILE])
        weights = sb("weights", [P, NTILE, 2])
        chosen, total = sb("chosen", TE), sb("total", TE)
        cum = [sb(f"cum{i}", TE) for i in range(2)]
        earlier, slot_e, pick = sb("earlier", TE), sb("slot_e", TE), sb("pick", TE)
        over = sb("over", [P, NE, NTILE])
        nblk, first, last_b = sb("nblk", [P, NE]), sb("first", [P, NE]), sb("last_b", [P, NE])
        prod = sb("prod", [P, NE, NE])
        slot_f = sb("slot_f", [P, NTILE, 2])
        slot_i, blk_i, row_i = (sb(n, [P, 2 * NTILE], I32) for n in ("slot_i", "blk_i", "row_i"))
        blk_f, row_f = sb("blk_f", [P, 2 * NTILE]), sb("row_f", [P, 2 * NTILE])
        in_row = sb("in_row", [P, 2 * NTILE, P], BF16)
        in_blk = sb("in_blk", [P, 2 * NTILE, NBLOCK], BF16)
        marks = sb("marks", [P, 2 * NTILE, 2, NBLOCK], BF16)
        listed = sb("listed", [P, 2, NBLOCK])
        tile_i, tile_f = sb("tile_i", [P, NBLOCK], I32), sb("tile_f", [P, NBLOCK])
        unused, token = sb("unused", [P, NBLOCK]), sb("token", [P, NBLOCK])
        index_f = sb("index_f", [P, 3, NBLOCK])
        index = sb("index", [P, 3, NBLOCK], U32)
        done_cmp, expert_f = sb("done_cmp", [1, NBLOCK, NE]), sb("expert_f", [1, NBLOCK])
        expert = sb("expert", [1, NBLOCK], U32)

        idx_in = [sb(f"idx_in{i}", [P, 1], U32) for i in range(2)]
        idx_wt = [sb(f"idx_wt{i}", [P, 1], U32) for i in range(2)]
        idx_out = [sb(f"idx_out{i}", [P, 1], U32) for i in range(2)]
        xg = [sb(f"xg{i}", [P, D]) for i in range(2)]
        wg = [sb(f"wg{i}", [P, 1]) for i in range(2)]
        xg_T = sb("xg_T", [P, KT, P])
        gate = [sb(f"gate{i}", [P, PAIR]) for i in range(2)]
        hidden = [sb(f"hidden{i}", [P, PAIR]) for i in range(2)]
        hidden_T = sb("hidden_T", [P, 2, P])
        y = [sb(f"y{i}", [P, D]) for i in range(2)]

        consts_in, weights_in, zeroed, pad_rows = sem("consts_in"), sem("weights_in"), sem("zeroed"), sem("pad_rows")
        route = sem("route")
        gap_ready, exp_gap_done = sem("gap_ready"), sem("exp_gap_done")
        chosen_ready, ranked = sem("chosen_ready"), sem("ranked")
        weights_ready, weights_out = sem("weights_ready"), sem("weights_out")
        marks_ready, list_full, routed = sem("marks_ready"), sem("list_full"), sem("routed")
        pool_held = sem("pool_held")
        idx_in_done, idx_wt_done, idx_out_done = sem("idx_in_done"), sem("idx_wt_done"), sem("idx_out_done")
        xg_in = [sem(f"xg_in{i}") for i in range(2)]
        wg_in = [sem(f"wg_in{i}") for i in range(2)]
        xg_T_full, xg_T_taken = sem("xg_T_full"), sem("xg_T_taken")
        up_full, gate_done, hidden_done = sem("up_full"), sem("gate_done"), sem("hidden_done")
        hidden_T_full, hidden_T_taken = sem("hidden_T_full"), sem("hidden_T_taken")
        down_full, y_done, added = sem("down_full"), sem("y_done"), sem("added")

        CONSTS = ((ident, "ident"), (before, "before"), (expert_m8, "expert_m8"), (expert_low, "expert_low"), (rows_full, "rows_full"),
                  (part_1, "part_1"), (part_pad, "part_pad"), (assign_ik, "assign_ik"), (col, "col"))

        block = ctx.enter_context(nc.Block())

        @block.sync
        def _(sp):
            for dst, name in CONSTS:
                sp.dma_start(dst[:], consts[name]).then_inc(consts_in, 16)
            sp.wait_ge(zeroed, 1)
            sp.dma_start(out_dram[T:T + P, :], zero[:]).then_inc(pad_rows, 16)
            for e in range(NE):
                sp.dma_start(w12_sb[:, e * KT * D:(e + 1) * KT * D], w12[e]).then_inc(weights_in, 16)
                sp.dma_start(w3_sb[:, e * 2 * D:(e + 1) * 2 * D], w3[e]).then_inc(weights_in, 16)
            sp.wait_ge(weights_ready, 1)
            sp.dma_start(wt_dram.rearrange("(p n) o -> p (n o)", p=P), weights[:].rearrange("p i k -> p (i k)")).then_inc(weights_out, 16)

        @block.scalar
        def _(act):
            act.wait_ge(gap_ready, 1)
            nc.scalar.activation(exp_gap[:], gap[:], ACT.Exp).then_inc(exp_gap_done, 1)

            def take_x(b):
                act.wait_ge(xg_T_full, b + 1)
                nc.scalar.copy(xg_T[:].rearrange("p k t -> p (k t)"), bank[0][:]).then_inc(xg_T_taken, 1)

            def gate_of(b, par):
                act.wait_ge(up_full, b + 1)
                nc.scalar.activation(gate[par][:], bank[2 + par][:, 0:PAIR], ACT.Silu).then_inc(gate_done, 1)

            def take_hidden(b):
                act.wait_ge(hidden_T_full, b + 1)
                nc.scalar.copy(hidden_T[:].rearrange("p k t -> p (k t)"), bank[4][:, 0:PAIR]).then_inc(hidden_T_taken, 1)

            def iteration(b, par, up, down, nxt):
                if up:
                    gate_of(b, par)
                if down:
                    take_hidden(b - 1)
                if nxt:
                    take_x(b + 1)

            take_x(0)
            iteration(0, 0, True, False, True)
            with act.Fori(0, NBLOCK // 2 - 1) as u:
                b = 2 * u + 1
                iteration(b, 1, True, True, True)
                iteration(b + 1, 0, True, True, True)
            iteration(NBLOCK - 1, 1, True, True, False)
            iteration(NBLOCK, 0, False, True, False)

        @block.gpsimd
        def _(pool):
            pool.memset(zero[:], 0.0).then_inc(zeroed, 1)
            pool.memset(ones[:], 1.0).then_inc(zeroed, 1)
            pool.wait_ge(routed, 1)
            pool.wait_ge(weights_out, 16)
            pool.wait_ge(pad_rows, 16)

            def gather_rows(b, par):
                if not isinstance(b, int) or b > 1:
                    pool.wait_ge(xg_T_full, b - 1)
                    pool.sem_inc(pool_held, 1)
                pool.tensor_copy(idx_in[par][:], index[:, 0, bass.ds(b, 1)]).then_inc(idx_in_done, 1)
                pool.wait_ge(idx_in_done, b + 1)
                pool.sem_inc(pool_held, 1)
                pool.indirect_dma_start(xg[par][:], None, xn_dram, bass.IndirectOffsetOnAxis(idx_in[par][:, 0:1], 0)).then_inc(xg_in[par], 16)

            def gather_weights(b, par):
                pool.tensor_copy(idx_wt[par][:], index[:, 1, bass.ds(b, 1)]).then_inc(idx_wt_done, 1)
                pool.wait_ge(idx_wt_done, b + 1)
                pool.sem_inc(pool_held, 1)
                pool.indirect_dma_start(wg[par][:], None, wt_dram, bass.IndirectOffsetOnAxis(idx_wt[par][:, 0:1], 0)).then_inc(wg_in[par], 16)

            def scatter(b, par):
                pool.tensor_copy(idx_out[par][:], index[:, 2, bass.ds(b, 1)]).then_inc(idx_out_done, 1)
                pool.wait_ge(idx_out_done, b + 1)
                pool.wait_ge(y_done, b + 1)
                if not isinstance(b, int) or b > 0:
                    pool.wait_ge(added, 16 * b)
                pool.sem_inc(pool_held, 1)
                pool.indirect_dma_start(out_dram, bass.IndirectOffsetOnAxis(idx_out[par][:, 0:1], 0), y[par][:], None,
                                        compute_op=ALU.add).then_inc(added, 16)

            for b in range(2):
                gather_rows(b, b)
                gather_weights(b, b)

            def both(u):
                for par in range(2):
                    b = 2 * u + par
                    gather_rows(b + 2, par)
                    scatter(b, par)
                    gather_weights(b + 2, par)

            both(0)
            with pool.Fori(1, NBLOCK // 2 - 1) as u:
                both(u)
            scatter(NBLOCK - 2, 0)
            scatter(NBLOCK - 1, 1)
            pool.wait_ge(added, 16 * NBLOCK)

        @block.vector
        def _(dve):
            steps = [0]

            def step(instruction):
                steps[0] += 1
                instruction.then_inc(route, 1)
                dve.wait_ge(route, steps[0])

            V = nc.vector
            over_e = lambda t: t[:].unsqueeze(2).to_broadcast(TE)
            over_i = lambda t: t[:].unsqueeze(1).to_broadcast(TE)
            flat = lambda t: t[:].rearrange("p i e -> p (i e)")
            scores = logits[:].rearrange("p (i e) -> p i e", e=NE)
            dve.wait_ge(consts_in, 16 * len(CONSTS))
            dve.wait_ge(zeroed, 2)

            for k, src in enumerate((scores, rest[:])):
                step(V.tensor_reduce(top[k][:], src, AX.X, ALU.max))
                step(V.tensor_tensor(hit[:], src, over_e(top[k]), ALU.is_ge))
                step(V.tensor_tensor(hit_m8[:], hit[:], over_i(expert_m8), ALU.mult))
                step(V.tensor_reduce(choice[:], hit_m8[:], AX.X, ALU.min))
                step(V.tensor_tensor(onehot[k][:], over_i(expert_m8), over_e(choice), ALU.is_equal))
                if k == 0:
                    step(V.scalar_tensor_tensor(flat(rest), flat(onehot[0]), -3e38, logits[:], ALU.mult, ALU.add))
            V.tensor_tensor(gap[:], top[1][:], top[0][:], ALU.subtract).then_inc(gap_ready, 1)
            V.tensor_tensor(chosen[:], onehot[0][:], onehot[1][:], ALU.add).then_inc(chosen_ready, 1)

            dve.wait_ge(exp_gap_done, 1)
            step(V.tensor_scalar(denom[:], exp_gap[:], 1.0, None, ALU.add))
            step(V.reciprocal(weights[:, :, 0], denom[:]))
            V.tensor_tensor(weights[:, :, 1], weights[:, :, 0], exp_gap[:], ALU.mult).then_inc(weights_ready, 1)

            dve.wait_ge(ranked, 1)
            step(V.tensor_copy(flat(total), bank[1][:, 0:NTILE * NE]))
            old = total
            for n in range(5):
                s, new = 2 ** n, cum[n % 2]
                V.tensor_copy(new[:, 0:s], old[:, 0:s])
                step(V.tensor_tensor(new[:, s:], old[:, s:], old[:, :NTILE - s], ALU.add))
                old = new
            step(V.tensor_tensor(earlier[:], old[:], total[:], ALU.subtract))
            step(V.tensor_tensor(flat(slot_e), bank[0][:, 0:NTILE * NE], flat(earlier), ALU.add))
            count = old[:, NTILE - 1, :]
            step(V.tensor_tensor(over[:], count.unsqueeze(2).to_broadcast([P, NE, NTILE]), rows_full[:].unsqueeze(1).to_broadcast([P, NE, NTILE]), ALU.is_gt))
            step(V.tensor_reduce(nblk[:], over[:], AX.X, ALU.add))
            step(V.tensor_tensor(prod[:], expert_low[:], nblk[:].unsqueeze(1).to_broadcast([P, NE, NE]), ALU.mult))
            step(V.tensor_reduce(first[:], prod[:], AX.X, ALU.add))
            step(V.tensor_tensor(last_b[:], first[:], nblk[:], ALU.add))
            step(V.scalar_tensor_tensor(slot_e[:], over_i(first), float(P), slot_e[:], ALU.mult, ALU.add))
            for k in range(2):
                step(V.tensor_tensor(pick[:], onehot[k][:], slot_e[:], ALU.mult))
                step(V.tensor_reduce(slot_f[:, :, k], pick[:], AX.X, ALU.add))
            step(V.tensor_copy(slot_i[:], slot_f[:].rearrange("p i k -> p (i k)")))
            V.tensor_scalar(blk_i[:], slot_i[:], 7, None, ALU.arith_shift_right)
            step(V.tensor_scalar(row_i[:], slot_i[:], P - 1, None, ALU.bitwise_and))
            V.tensor_copy(blk_f[:], blk_i[:])
            step(V.tensor_copy(row_f[:], row_i[:]))
            A = 2 * NTILE
            step(V.tensor_tensor(in_blk[:], blk_f[:].unsqueeze(2).to_broadcast([P, A, NBLOCK]), col[:, 0:NBLOCK].unsqueeze(1).to_broadcast([P, A, NBLOCK]), ALU.is_equal))
            V.tensor_scalar(marks[:, :, 0], in_blk[:], part_1[:], None, ALU.mult)
            V.tensor_tensor(marks[:, :, 1], in_blk[:], assign_ik[:].unsqueeze(2).to_broadcast([P, A, NBLOCK]), ALU.mult)
            V.tensor_tensor(in_row[:], row_f[:].unsqueeze(2).to_broadcast([P, A, P]), col[:].unsqueeze(1).to_broadcast([P, A, P]), ALU.is_equal).then_inc(marks_ready, 1)

            step(V.tensor_tensor(done_cmp[:], last_b[0:1, :].unsqueeze(1).to_broadcast([1, NBLOCK, NE]), col[0:1, 0:NBLOCK].unsqueeze(2).to_broadcast([1, NBLOCK, NE]), ALU.is_le))
            step(V.tensor_reduce(expert_f[:], done_cmp[:], AX.X, ALU.add))
            step(V.tensor_scalar(expert[:], expert_f[:], float(NE - 1), None, ALU.min))

            dve.wait_ge(list_full, 1)
            step(V.tensor_copy(listed[:].rearrange("p a b -> p (a b)"), bank[5][:, 0:2 * NBLOCK]))
            step(V.tensor_copy(tile_i[:], listed[:, 1]))
            step(V.tensor_scalar(tile_i[:], tile_i[:], 1, None, ALU.arith_shift_right))
            step(V.tensor_copy(tile_f[:], tile_i[:]))
            step(V.scalar_tensor_tensor(token[:], tile_f[:], float(P), listed[:, 0], ALU.mult, ALU.add))
            step(V.tensor_scalar(token[:], token[:], -1.0, None, ALU.add))
            V.tensor_scalar(index_f[:, 0], token[:], 0.0, None, ALU.max)
            step(V.scalar_tensor_tensor(index_f[:, 1], listed[:, 0], float(A), listed[:, 1], ALU.mult, ALU.add))
            step(V.tensor_scalar(index_f[:, 1], index_f[:, 1], -float(A), 0.0, ALU.add, ALU.max))
            step(V.tensor_scalar(unused[:], listed[:, 0], 0.0, None, ALU.is_equal))
            step(V.scalar_tensor_tensor(index_f[:, 2], unused[:], part_pad[:], token[:], ALU.mult, ALU.add))
            V.tensor_copy(index[:], index_f[:]).then_inc(routed, 1)

            def hidden_of(b, par):
                dve.wait_ge(gate_done, b + 1)
                V.tensor_tensor(hidden[par][:], gate[par][:], bank[2 + par][:, PAIR:2 * PAIR], ALU.mult).then_inc(hidden_done, 1)

            def weigh(b, par):
                dve.wait_ge(down_full, b + 1)
                dve.wait_ge(wg_in[par], 8 * (b + 2 - par))
                if not isinstance(b, int) or b > 1:
                    dve.wait_ge(added, 16 * (b - 1))
                V.tensor_scalar(y[par][:], bank[6 + par][:], wg[par][:], None, ALU.mult).then_inc(y_done, 1)

            def iteration(b, par, up, down):
                if up:
                    hidden_of(b, par)
                if down:
                    weigh(b - 1, 1 - par)

            iteration(0, 0, True, False)
            iteration(1, 1, True, True)
            iteration(2, 0, True, True)
            with dve.Fori(0, NBLOCK // 2 - 2) as u:
                b = 2 * u + 3
                iteration(b, 1, True, True)
                iteration(b + 1, 0, True, True)
            iteration(NBLOCK - 1, 1, True, True)
            iteration(NBLOCK, 0, False, True)

        @block.tensor
        def _(pe):
            pe.wait_ge(consts_in, 16 * len(CONSTS))
            pe.wait_ge(zeroed, 2)
            pe.wait_ge(chosen_ready, 1)
            nc.tensor.matmul(bank[0][:, 0:NTILE * NE], before[:], chosen[:].rearrange("p i e -> p (i e)"), start=True, stop=True)
            nc.tensor.matmul(bank[1][:, 0:NTILE * NE], ones[:], chosen[:].rearrange("p i e -> p (i e)"), start=True, stop=True).then_inc(ranked, 1)
            pe.wait_ge(marks_ready, 1)
            for a in range(2 * NTILE):
                last = nc.tensor.matmul(bank[5][:, 0:2 * NBLOCK], in_row[:, a], marks[:, a].rearrange("p c b -> p (c b)"), start=a == 0, stop=a == 2 * NTILE - 1)
            last.then_inc(list_full, 1)
            pe.wait_ge(routed, 1)
            pe.wait_ge(weights_in, 16 * 2 * NE)

            def transpose_x(b, par):
                pe.wait_ge(xg_in[par], 8 * (b + 2 - par))
                if not isinstance(b, int) or b > 0:
                    pe.wait_ge(xg_T_taken, b)
                for kt in range(KT):
                    last = nc.tensor.transpose(bank[0][:, kt * P:(kt + 1) * P], xg[par][:, kt * P:(kt + 1) * P], ident[:])
                last.then_inc(xg_T_full, 1)

            def expert_of(b):
                return pe.value_load(expert[0:1, bass.ds(b, 1)], min_val=0, max_val=NE - 1)

            def up(b, par):
                e = expert_of(b)
                pe.wait_ge(xg_T_taken, b + 1)
                if not isinstance(b, int) or b > 1:
                    pe.wait_ge(hidden_done, b - 1)
                for kt in range(KT):
                    last = nc.tensor.matmul(bank[2 + par][:], xg_T[:, kt], w12_sb[:, bass.ds(e * (KT * D) + kt * D, D)], start=kt == 0, stop=kt == KT - 1)
                last.then_inc(up_full, 1)

            def transpose_hidden(b, par):
                pe.wait_ge(hidden_done, b + 1)
                for ft in range(2):
                    last = nc.tensor.transpose(bank[4][:, ft * P:(ft + 1) * P], hidden[par][:, ft * P:(ft + 1) * P], ident[:])
                last.then_inc(hidden_T_full, 1)

            def down(b, par):
                e = expert_of(b)
                pe.wait_ge(hidden_T_taken, b + 1)
                if not isinstance(b, int) or b > 1:
                    pe.wait_ge(y_done, b - 1)
                for ft in range(2):
                    last = nc.tensor.matmul(bank[6 + par][:], hidden_T[:, ft], w3_sb[:, bass.ds(e * (2 * D) + ft * D, D)], start=ft == 0, stop=ft == 1)
                last.then_inc(down_full, 1)

            def iteration(b, par, is_up, is_down, nxt):
                if is_up:
                    up(b, par)
                if is_down:
                    transpose_hidden(b - 1, 1 - par)
                if nxt:
                    transpose_x(b + 1, 1 - par)
                if is_down:
                    down(b - 1, 1 - par)

            transpose_x(0, 0)
            iteration(0, 0, True, False, True)
            iteration(1, 1, True, True, True)
            iteration(2, 0, True, True, True)
            with pe.Fori(0, NBLOCK // 2 - 2) as u:
                b = 2 * u + 3
                iteration(b, 1, True, True, True)
                iteration(b + 1, 0, True, True, True)
            iteration(NBLOCK - 1, 1, True, True, False)
            iteration(NBLOCK, 0, False, True, False)


def shape_constants():
    f = lambda a: np.ascontiguousarray(a, dtype=np.float32)
    p = np.arange(P)
    inv_freq = (1.0 / 10000.0 ** (np.arange(0, HD, 2, dtype=np.float32) / np.float32(HD))).astype(np.float32)
    angles = np.arange(P, dtype=np.float32)[:, None] * inv_freq
    sin = np.repeat(np.sin(angles), 2, axis=1)
    sin[:, 0::2] *= -1
    e = np.arange(NE)
    rows = lambda a: f(np.broadcast_to(a, (P,) + a.shape))
    return {
        "ident": f(np.eye(P)),
        "mask": f(np.where(p[None, :] <= p[:, None], 0.0, -1e30)),
        "cos": f(np.repeat(np.cos(angles), 2, axis=1)),
        "sin": f(sin),
        "before": f(p[:, None] < p[None, :]),
        "expert_m8": rows(e - 8.0),
        "expert_low": rows((e[None, :] < e[:, None]).astype(np.float32)),
        "rows_full": rows(np.arange(NTILE) * float(P)),
        "part_1": f(p[:, None] + 1),
        "part_pad": f(p[:, None] + T + 1),
        "assign_ik": rows(np.arange(2 * NTILE) * 1.0),
        "col": rows(p * 1.0),
    }


def build(nc, a, out):
    h1_dram = nc.dram_tensor("h1_dram", (T, D), F32).ap()
    xn_dram = nc.dram_tensor("xn_dram", (T, D), F32).ap()
    wt_dram = nc.dram_tensor("wt_dram", (2 * T, 1), F32).ap()
    dilated_attention(nc, a["x_pairs"], a["wqkv"], a["bqk"], a["bv"], a["wout"], a["bout"], h1_dram, a)
    with nc.sbuf_tensor("logits", [P, NTILE * NE], F32) as logits:
        causal_attention(nc, h1_dram, a["wq"], a["wkv"], a["wo"], a["bq"], a["bkv"], a["bo"], a["router"], out, xn_dram, logits, a)
        routed_experts(nc, logits, a["w12"], a["w3"], xn_dram, wt_dram, out, a)


def laid_out(x, L0_tok_Wqkv, L0_tok_b_qkv, L0_tok_Wout, L0_tok_b_out, L0_attn_Wq, L0_attn_bq, L0_attn_Wkv, L0_attn_bkv,
             L0_attn_Wo, L0_attn_bo, L0_ffn_router_w, L0_ffn_w1, L0_ffn_w2, L0_ffn_w3):
    c = np.ascontiguousarray
    by_rows = lambda w: c(np.asarray(w).reshape(KT, P, -1).transpose(1, 0, 2))
    repeated = lambda b: c(np.broadcast_to(np.asarray(b), (P, b.shape[0])))
    x_T = np.asarray(x).reshape(2 * NTILE, SEG, 2, D).transpose(2, 3, 0, 1).reshape(2, KT, P, NPAIR, PAIR)
    w12 = np.concatenate([np.asarray(L0_ffn_w1), np.asarray(L0_ffn_w2)], axis=2)
    return {
        "x_pairs": c(x_T.transpose(0, 3, 2, 1, 4)),
        "wqkv": by_rows(L0_tok_Wqkv.T),
        "bqk": c(np.asarray(L0_tok_b_qkv)[:2 * D].reshape(2 * KT, P).T),
        "bv": repeated(L0_tok_b_qkv[2 * D:]),
        "wout": by_rows(L0_tok_Wout.T),
        "bout": repeated(L0_tok_b_out),
        "wq": by_rows(L0_attn_Wq),
        "wkv": by_rows(L0_attn_Wkv),
        "wo": c(np.asarray(L0_attn_Wo).reshape(NG, 4, HD, D).transpose(0, 2, 1, 3).reshape(P, 4, D)),
        "bq": repeated(L0_attn_bq),
        "bkv": repeated(L0_attn_bkv),
        "bo": repeated(L0_attn_bo),
        "router": by_rows(L0_ffn_router_w.T),
        "w12": c(w12.reshape(NE, KT, P, D).transpose(0, 2, 1, 3).reshape(NE, P, KT * D)),
        "w3": c(np.asarray(L0_ffn_w3).reshape(NE, 2, P, D).transpose(0, 2, 1, 3).reshape(NE, P, 2 * D)),
    }


def kernel(**inputs):
    import concourse.bacc as bacc
    from concourse.bass_utils import run_bass_kernel_spmd

    nc = bacc.Bacc("TRN2", target_bir_lowering=False, num_devices=1)
    arrays = {**laid_out(**inputs), **shape_constants()}
    aps = {n: nc.dram_tensor(n, a.shape, mybir.dt.from_np(a.dtype), kind="ExternalInput").ap() for n, a in arrays.items()}
    out = nc.dram_tensor("out", (T + P, D), F32, kind="ExternalOutput").ap()
    build(nc, aps, out)
    r = run_bass_kernel_spmd(nc, [arrays], core_ids=[0])
    return r.results[0]["out"][:T].reshape(NTILE, P, D)
```

```python
import numpy as np
import concourse.bass as bass
from concourse import mybir
from contextlib import ExitStack

F32, F32R, BF16, U32 = mybir.dt.float32, mybir.dt.float32r, mybir.dt.bfloat16, mybir.dt.uint32
ACT, ALU, AX = mybir.ActivationFunctionType, mybir.AluOpType, mybir.AxisListType

P = 128
D = 512
KT = D // P
NH, HD = 16, 32
NG = 4
SEG = 64
T = 32 * P
NTILE = T // P
PAIR = 2 * P
NPAIR = NTILE // 2
SCALE = 1.0 / float(np.sqrt(HD))
EPS = 1e-5

NE = 8
NBLOCK = 2 * T // P + NE
I32 = mybir.dt.int32
XROW = D + 2


def dilated_attention(nc, x_pairs, wqkv, bqk, bv, wout, bout, h1_dram, consts):
    ctx = ExitStack()
    with ctx:
        sb = lambda name, shape, dt=F32: ctx.enter_context(nc.sbuf_tensor("a_" + name, shape, dt))
        sem = lambda name: ctx.enter_context(nc.semaphore("a_" + name))
        bank = [ctx.enter_context(nc.psum_tensor(f"a_bank{i}", [P, 512], F32)) for i in range(8)]

        w_stage = sb("w_stage", [P, KT, 3 * D])
        wo_stage = sb("wo_stage", [P, KT, D])
        w_hi = sb("w_hi", [P, KT, 3 * D], F32R)
        w_lo = sb("w_lo", [P, KT, 3 * D], F32R)
        wo_hi = sb("wo_hi", [P, KT, D], F32R)
        wo_lo = sb("wo_lo", [P, KT, D], F32R)
        bqk_raw = sb("bqk_raw", [P, 8])
        bqk_sb = sb("bqk_sb", [P, 8])
        bv_sb = sb("bv_sb", [P, D])
        bout_sb = sb("bout_sb", [P, D])
        ident = sb("ident", [P, P])
        x_raw = sb("x_raw", [P, KT, PAIR])
        x_hi = sb("x_hi", [P, KT, PAIR], F32R)
        x_lo = sb("x_lo", [P, KT, PAIR], F32R)
        q_T = sb("q_T", [P, KT, PAIR])
        k_blk = sb("k_blk", [P, 4, KT, 4, SEG])
        v_blk = [sb(f"v_blk{a}", [P, 2, 8, 64]) for a in range(2)]
        neg_max = [sb(f"neg_max{a}", [P, NH]) for a in range(2)]
        probs = [sb(f"probs{a}", [P, NH, SEG]) for a in range(2)]
        probs_T = sb("probs_T", [P, 8, P])
        sums = [sb(f"sums{a}", [P, NH]) for a in range(2)]
        recip = [sb(f"recip{a}", [P, NH]) for a in range(2)]
        y_hi = [sb(f"y_hi{a}", [P, KT, P], F32R) for a in range(2)]
        y_lo = [sb(f"y_lo{a}", [P, KT, P], F32R) for a in range(2)]
        h1 = [sb(f"h1_{a}", [P, D]) for a in range(2)]

        consts_in, zeroed, scaled_bias = sem("consts_in"), sem("zeroed"), sem("scaled_bias")
        w_in = [sem(f"w_in{c}") for c in range(4)]
        w_hi_done, w_split = sem("w_hi_done"), sem("w_split")
        x_in, x_hi_done, x_split = sem("x_in"), sem("x_hi_done"), sem("x_split")
        qk_full, q_taken, k_taken = sem("qk_full"), sem("q_taken"), sem("k_taken")
        v_full, v_taken = sem("v_full"), sem("v_taken")
        s_full, max_done, exp_done = sem("s_full"), sem("max_done"), sem("exp_done")
        pT_full, pT_taken = sem("pT_full"), sem("pT_taken")
        recip_done, probs_scaled = sem("recip_done"), sem("probs_scaled")
        pv_full, y_hi_done, y_lo_done = sem("pv_full"), sem("y_hi_done"), sem("y_lo_done")
        out_full, h1_done = sem("out_full"), sem("h1_done")
        h1_stored = [sem(f"h1_stored{a}") for a in range(2)]

        pool_held = sem("pool_held")

        stage = [w_stage[:, :, c * D:(c + 1) * D] for c in range(3)] + [wo_stage[:, :, :]]
        his = [w_hi[:, :, c * D:(c + 1) * D] for c in range(3)] + [wo_hi[:, :, :]]
        los = [w_lo[:, :, c * D:(c + 1) * D] for c in range(3)] + [wo_lo[:, :, :]]

        block = ctx.enter_context(nc.Block())

        @block.sync
        def _(sp):
            sp.dma_start(x_raw[:], x_pairs[0, 0:1].rearrange("o p k t -> (o p) k t")).then_inc(x_in, 16)
            for c in range(3):
                sp.dma_start(stage[c], wqkv[:, :, c * D:(c + 1) * D]).then_inc(w_in[c], 16)
                if c == 0:
                    sp.dma_start(bqk_raw[:], bqk).then_inc(consts_in, 16)
                    sp.dma_start(ident[:], consts["ident"]).then_inc(consts_in, 16)
                    sp.dma_start(bv_sb[:], bv).then_inc(consts_in, 16)
                    sp.dma_start(bout_sb[:], bout).then_inc(consts_in, 16)
            sp.dma_start(stage[3], wout).then_inc(w_in[3], 16)

            def store(p, a):
                sp.wait_ge(h1_done, 2 * p + a + 1)
                sp.dma_start(h1_dram[bass.ds((2 * p + a) * P, P), :], h1[a][:]).then_inc(h1_stored[a], 16)

            def load(p):
                sp.wait_ge(x_split, p)
                sp.dma_start(x_raw[:], x_pairs[0, bass.ds(p, 1)].rearrange("o p k t -> (o p) k t")).then_inc(x_in, 16)

            load(1)
            with sp.Fori(1, NPAIR - 1) as p:
                load(p + 1)
                store(p - 1, 0)
                store(p - 1, 1)
            for p in (NPAIR - 2, NPAIR - 1):
                store(p, 0)
                store(p, 1)
            for a in range(2):
                sp.wait_ge(h1_stored[a], 16 * NPAIR)

        @block.gpsimd
        def _(pool):
            pool.memset(k_blk[:], 0.0).then_inc(zeroed, 1)
            pool.memset(v_blk[0][:], 0.0).then_inc(zeroed, 1)
            pool.memset(v_blk[1][:], 0.0).then_inc(zeroed, 1)

            def split(p):
                pool.wait_ge(x_in, 16 * (p + 1))
                pool.sem_inc(pool_held, 1)
                pool.tensor_copy(x_hi[:], x_raw[:]).then_inc(x_hi_done, 1)
                pool.wait_ge(x_hi_done, p + 1)
                pool.tensor_tensor(x_lo[:], x_raw[:], x_hi[:].bitcast(F32), ALU.subtract).then_inc(x_split, 1)

            split(0)
            with pool.Fori(1, NPAIR) as p:
                pool.wait_ge(v_full, 2 * p)
                split(p)

        @block.scalar
        def _(act):
            act.wait_ge(consts_in, 16 * 4)
            for c in range(4):
                act.wait_ge(w_in[c], 16)
                nc.scalar.copy(his[c], stage[c]).then_inc(w_hi_done, 1)
            act.wait_ge(scaled_bias, 1)
            act.wait_ge(zeroed, 3)

            def take_qk(p):
                for i in range(2):
                    act.wait_ge(qk_full, 4 * p + i + 1)
                    for ft in (2 * i, 2 * i + 1):
                        last = nc.scalar.activation(q_T[:, ft, :], bank[i][:, (ft % 2) * PAIR:(ft % 2 + 1) * PAIR],
                                                    ACT.Identity, bias=bqk_sb[:, ft:ft + 1], scale=SCALE)
                    last.then_inc(q_taken, 1)
                for i in range(2):
                    act.wait_ge(qk_full, 4 * p + i + 3)
                    for ft in (2 * i, 2 * i + 1):
                        for h in range(4):
                            r = slice(HD * h, HD * h + HD)
                            src = bank[2 + i][r, (ft % 2) * PAIR:(ft % 2 + 1) * PAIR]
                            last = nc.scalar.activation(k_blk[r, :, ft, h, :], src.rearrange("p (s k) -> p s k", s=4),
                                                        ACT.Identity, bias=bqk_sb[r, 4 + ft:5 + ft])
                    last.then_inc(k_taken, 1)

            def exps(p, a):
                for i in range(2):
                    act.wait_ge(max_done, 4 * p + 2 * a + i + 1)
                    for h in range(8 * i, 8 * i + 8):
                        last = nc.scalar.activation(probs[a][:, h, :], bank[2 * a + i][:, (h % 8) * SEG:(h % 8 + 1) * SEG],
                                                    ACT.Exp, bias=neg_max[a][:, h:h + 1], accum_out=sums[a][:, h:h + 1])
                    last.then_inc(exp_done, 1)

            def y_high(p, a):
                act.wait_ge(pv_full, 2 * p + a + 1)
                nc.scalar.copy(y_hi[a][:].rearrange("p k t -> p (k t)"), bank[5][:]).then_inc(y_hi_done, 1)

            def iteration(p, new, old):
                if new:
                    take_qk(p)
                if old:
                    y_high(p - 1, 0)
                if new:
                    exps(p, 0)
                if old:
                    y_high(p - 1, 1)
                if new:
                    exps(p, 1)

            iteration(0, True, False)
            with act.Fori(1, NPAIR) as p:
                iteration(p, True, True)
            iteration(NPAIR, False, True)

        @block.vector
        def _(dve):
            dve.wait_ge(consts_in, 16 * 4)
            nc.vector.tensor_scalar(bqk_sb[:, 0:4], bqk_raw[:, 0:4], SCALE, None, ALU.mult)
            nc.vector.tensor_copy(bqk_sb[:, 4:8], bqk_raw[:, 4:8]).then_inc(scaled_bias, 1)
            for c in range(4):
                dve.wait_ge(w_hi_done, c + 1)
                nc.vector.tensor_tensor(los[c], stage[c], his[c].bitcast(F32), ALU.subtract).then_inc(w_split, 1)
            dve.wait_ge(zeroed, 3)

            def take_probs_T(p, a):
                for i in range(2):
                    dve.wait_ge(pT_full, 4 * p + 2 * a + i + 1)
                    nc.vector.tensor_copy(probs_T[:, 4 * i:4 * i + 4, :].rearrange("p h q -> p (h q)"),
                                          bank[4 + i][:]).then_inc(pT_taken, 1)

            def take_v(p, a, old):
                dve.wait_ge(v_full, 2 * p + a + 1)
                if old:
                    dve.wait_ge(pv_full, 2 * p + a - 1)
                for s in range(2):
                    for r in range(2):
                        src = bank[6 + a][64 * s:64 * s + 64, :].rearrange("p (h r d) -> p r h d", r=2, d=HD)[:, r]
                        b = bv_sb[64 * s:64 * s + 64, :].rearrange("p (h r d) -> p r h d", r=2, d=HD)[:, r]
                        last = nc.vector.tensor_tensor(v_blk[a][64 * r:64 * r + 64, s, :, HD * r:HD * r + HD],
                                                       src, b, ALU.add)
                last.then_inc(v_taken, 1)

            def scale_probs(p, a):
                for i in range(2):
                    n = 4 * p + 2 * a + i + 1
                    hs = slice(8 * i, 8 * i + 8)
                    dve.wait_ge(exp_done, n)
                    nc.vector.reciprocal(recip[a][:, hs], sums[a][:, hs]).then_inc(recip_done, 1)
                    dve.wait_ge(recip_done, n)
                    nc.vector.tensor_tensor(probs[a][:, hs, :], probs[a][:, hs, :],
                                            recip[a][:, hs].unsqueeze(2).to_broadcast([P, 8, SEG]), ALU.mult).then_inc(probs_scaled, 1)

            def y_low(p, a):
                dve.wait_ge(y_hi_done, 2 * p + a + 1)
                nc.vector.tensor_tensor(y_lo[a][:].rearrange("p k t -> p (k t)"), bank[5][:],
                                        y_hi[a][:].rearrange("p k t -> p (k t)").bitcast(F32), ALU.subtract).then_inc(y_lo_done, 1)

            def maxima(p, a):
                for i in range(2):
                    dve.wait_ge(s_full, 4 * p + 2 * a + i + 1)
                    nc.vector.tensor_reduce(neg_max[a][:, 8 * i:8 * i + 8], bank[2 * a + i][:].rearrange("p (h k) -> p h k", k=SEG),
                                            AX.X, ALU.max, negate=True).then_inc(max_done, 1)

            def take_out(p, a, peeled):
                dve.wait_ge(out_full, 2 * p + a + 1)
                if not peeled:
                    dve.wait_ge(h1_stored[a], 16 * p)
                nc.vector.tensor_tensor(h1[a][:], bank[6 + a][:], bout_sb[:], ALU.add).then_inc(h1_done, 1)

            def iteration(p, new, old, first_old=False):
                if old:
                    scale_probs(p - 1, 0)
                    take_probs_T(p - 1, 0)
                    scale_probs(p - 1, 1)
                if new:
                    take_v(p, 0, old)
                if old:
                    y_low(p - 1, 0)
                    take_probs_T(p - 1, 1)
                if new:
                    maxima(p, 0)
                    maxima(p, 1)
                if old:
                    y_low(p - 1, 1)
                if new:
                    take_v(p, 1, old)
                if old:
                    take_out(p - 1, 0, first_old)
                    take_out(p - 1, 1, first_old)

            iteration(0, True, False)
            iteration(1, True, True, True)
            with dve.Fori(2, NPAIR) as p:
                iteration(p, True, True)
            iteration(NPAIR, False, True)

        @block.tensor
        def _(pe):
            pe.wait_ge(consts_in, 16 * 4)

            def project_qk(p, first):
                pe.wait_ge(x_split, p + 1)
                for i in range(4):
                    if first:
                        pe.wait_ge(w_split, i // 2 + 1)
                    else:
                        pe.wait_ge(exp_done, 4 * (p - 1) + i + 1)
                    for half in range(2):
                        e = (2 * i + half) * P
                        dst = bank[i][:, half * PAIR:(half + 1) * PAIR]
                        n = 0
                        for kt in range(KT):
                            for w, x in ((w_hi, x_hi), (w_hi, x_lo), (w_lo, x_hi)):
                                last = nc.tensor.matmul(dst, w[:, kt, e:e + P], x[:, kt, :], start=n == 0, stop=n == 3 * KT - 1)
                                n += 1
                    last.then_inc(qk_full, 1)

            def project_v(p, a, first):
                if first:
                    pe.wait_ge(w_split, 3)
                if not first:
                    pe.wait_ge(h1_done, 2 * (p - 1) + a - 1) if not isinstance(p, int) or p > 1 else None
                n = 0
                for kt in range(KT):
                    for x, w in ((x_hi, w_hi), (x_hi, w_lo), (x_lo, w_hi)):
                        last = nc.tensor.matmul(bank[6 + a][:], x[:, kt, a * P:(a + 1) * P], w[:, kt, 2 * D:3 * D],
                                                start=n == 0, stop=n == 3 * KT - 1)
                        n += 1
                last.then_inc(v_full, 1)

            def transpose_probs(p, a, peeled):
                if not peeled or a:
                    pe.wait_ge(y_lo_done, 2 * p + a)
                for i in range(2):
                    pe.wait_ge(probs_scaled, 4 * p + 2 * a + i + 1)
                    for hp in range(4 * i, 4 * i + 4):
                        last = nc.tensor.transpose(bank[4 + i][:, (hp % 4) * P:(hp % 4 + 1) * P],
                                                   probs[a][:, 2 * hp:2 * hp + 2, :].rearrange("p h k -> p (h k)"), ident[:])
                    last.then_inc(pT_full, 1)

            def scores(p, a):
                pe.wait_ge(q_taken, 2 * (p + 1))
                pe.wait_ge(k_taken, 2 * (p + 1))
                for i in range(2):
                    for ft in (2 * i, 2 * i + 1):
                        for s in range(2):
                            c = (ft % 2) * PAIR
                            last = nc.tensor.matmul(bank[2 * a + i][64 * s:64 * s + 64, c:c + PAIR],
                                                    q_T[:, ft, a * P + s * SEG:a * P + (s + 1) * SEG],
                                                    k_blk[:, 2 * a + s, ft, :, :].rearrange("p h k -> p (h k)"), start=True, stop=True)
                    last.then_inc(s_full, 1)

            def weigh_values(p, a):
                pe.wait_ge(pT_taken, 4 * p + 2 * a + 2)
                pe.wait_ge(v_taken, 2 * p + a + 1)
                for hp in range(8):
                    for s in range(2):
                        r, c = hp % 2, (hp // 2) * P + s * SEG
                        last = nc.tensor.matmul(bank[5][64 * r:64 * r + 64, c:c + SEG], v_blk[a][:, s, hp, :],
                                                probs_T[:, hp, s * SEG:(s + 1) * SEG], start=True, stop=True)
                last.then_inc(pv_full, 1)

            def project_out(p, a, new):
                if new:
                    pe.wait_ge(v_taken, 2 * (p + 1) + a + 1)
                pe.wait_ge(w_split, 4)
                pe.wait_ge(y_lo_done, 2 * p + a + 1)
                n = 0
                for ft in range(KT):
                    for y, w in ((y_hi[a], wo_hi), (y_hi[a], wo_lo), (y_lo[a], wo_hi)):
                        last = nc.tensor.matmul(bank[6 + a][:], y[:, ft, :], w[:, ft, :], start=n == 0, stop=n == 3 * KT - 1)
                        n += 1
                last.then_inc(out_full, 1)

            def iteration(p, new, old, first_old=False):
                if new:
                    project_qk(p, not old)
                if old:
                    transpose_probs(p - 1, 0, first_old)
                if new:
                    project_v(p, 0, not old)
                if old:
                    weigh_values(p - 1, 0)
                if new:
                    project_v(p, 1, not old)
                if old:
                    transpose_probs(p - 1, 1, first_old)
                if new:
                    scores(p, 0)
                    scores(p, 1)
                if old:
                    weigh_values(p - 1, 1)
                    project_out(p - 1, 0, new)
                    project_out(p - 1, 1, new)

            iteration(0, True, False)
            iteration(1, True, True, True)
            with pe.Fori(2, NPAIR) as p:
                iteration(p, True, True)
            iteration(NPAIR, False, True)


def causal_attention(nc, h1_dram, wq, wkv, wo, bq, bkv, bo, router, h2_dram, xn_dram, logits_T, consts):
    ctx = ExitStack()
    with ctx:
        sb = lambda name, shape, dt=F32: ctx.enter_context(nc.sbuf_tensor("b_" + name, shape, dt))
        sem = lambda name: ctx.enter_context(nc.semaphore("b_" + name))
        bank = [ctx.enter_context(nc.psum_tensor(f"b_bank{i}", [P, 512], F32)) for i in range(8)]

        wq_stage, wkv_stage, wo_stage = sb("wq_stage", [P, KT, D]), sb("wkv_stage", [P, KT, PAIR]), sb("wo_stage", [P, KT, D])
        wq_hi, wq_lo = sb("wq_hi", [P, KT, D], F32R), sb("wq_lo", [P, KT, D], F32R)
        wkv_hi, wkv_lo = sb("wkv_hi", [P, KT, PAIR], F32R), sb("wkv_lo", [P, KT, PAIR], F32R)
        wo_hi, wo_lo = sb("wo_hi", [P, KT, D], F32R), sb("wo_lo", [P, KT, D], F32R)
        router_sb = sb("router", [P, KT, NE])
        bq_sb, bkv_sb, bo_sb = sb("bq", [P, D]), sb("bkv", [P, PAIR]), sb("bo", [P, D])
        cos_sb, sin_sb = sb("cos", [P, HD]), sb("sin", [P, HD])
        ident = sb("ident", [P, P])
        ident_16 = sb("ident_16", [P, P], BF16)
        mask_f = sb("mask_f", [P, P])
        mask_16 = sb("mask_16", [P, NG, P], BF16)
        minus_half = sb("minus_half", [P, 1])

        h1 = sb("h1", [P, D])
        stats1, mv1, rstd1 = sb("stats1", [P, 6]), sb("mv1", [P, 2]), sb("rstd1", [P, 2])
        xn1 = sb("xn1", [P, D])
        xT_hi, xT_lo = sb("xT_hi", [P, KT, P], F32R), sb("xT_lo", [P, KT, P], F32R)
        qk = sb("qk", [P, NH + NG, HD])
        v_next, v = sb("v_next", [P, NG * HD]), sb("v", [P, NG * HD])
        rope_c, rope_s = sb("rope_c", [P, NH + NG, HD]), sb("rope_s", [P, NH + NG, HD])
        q_rot = sb("q_rot", [P, 4, NG, HD])
        k_rot = sb("k_rot", [P, NG * (P + HD)])
        qT_hi, qT_lo = sb("qT_hi", [P, 4, P], F32R), sb("qT_lo", [P, 4, P], F32R)
        kT_hi, kT_lo = sb("kT_hi", [P, NG * P], F32R), sb("kT_lo", [P, NG * P], F32R)
        neg_max, sums, recip = sb("neg_max", [P, NH]), sb("sums", [P, NH]), sb("recip", [P, NH])
        probs = sb("probs", [P, 4, NG, P])
        probs_T = sb("probs_T", [P, NG, 4, P])
        y_hi, y_lo = sb("y_hi", [P, 4, P], F32R), sb("y_lo", [P, 4, P], F32R)
        resid, resid_b = sb("resid", [P, D]), sb("resid_b", [P, D])
        h2 = sb("h2", [P, D])
        stats2, mv2, rstd2 = sb("stats2", [P, 6]), sb("mv2", [P, 2]), sb("rstd2", [P, 2])
        xn2 = sb("xn2", [P, D])
        xn2_T = sb("xn2_T", [P, KT, P])

        consts_in, zeroed, consts_16 = sem("consts_in"), sem("zeroed"), sem("consts_16")
        w_in = [sem(f"w_in{c}") for c in range(3)]
        w_hi_done, w_split = sem("w_hi_done"), sem("w_split")
        h1_in, resid_in, resid_done = sem("h1_in"), sem("resid_in"), sem("resid_done")
        stats1_done, mv1_done, eps1_done, rstd1_done, xn1_done = (sem(n) for n in ("stats1_done", "mv1_done", "eps1_done", "rstd1_done", "xn1_done"))
        stats2_done, mv2_done, eps2_done, rstd2_done, xn2_done = (sem(n) for n in ("stats2_done", "mv2_done", "eps2_done", "rstd2_done", "xn2_done"))
        xT_full, xT_hi_done, xT_lo_done = sem("xT_full"), sem("xT_hi_done"), sem("xT_lo_done")
        q_full, kv_full, qk_taken = sem("q_full"), sem("kv_full"), sem("qk_taken")
        v_taken, v_moved = sem("v_taken"), sem("v_moved")
        cos_done, sin_done, rope_done = sem("cos_done"), sem("sin_done"), sem("rope_done")
        qT_full, kT_full, qkT_hi_done, qkT_lo_done = sem("qT_full"), sem("kT_full"), sem("qkT_hi_done"), sem("qkT_lo_done")
        s_full, max_done, exp_done = sem("s_full"), sem("max_done"), sem("exp_done")
        recip_done, probs_scaled = sem("recip_done"), sem("probs_scaled")
        pT_full, pT_taken, pv_full = sem("pT_full"), sem("pT_taken"), sem("pv_full")
        y_hi_done, y_lo_done, wo_full = sem("y_hi_done"), sem("y_lo_done"), sem("wo_full")
        h2_done, h2_stored, xn2_stored = sem("h2_done"), sem("h2_stored"), sem("xn2_stored")
        xn2_T_full, xn2_T_taken = sem("xn2_T_full"), sem("xn2_T_taken")
        logits_full, logits_taken = sem("logits_full"), sem("logits_taken")

        dve_held, pool_held = sem("dve_held"), sem("pool_held")

        stage = [wq_stage, wkv_stage, wo_stage]
        his, los = [wq_hi, wkv_hi, wo_hi], [wq_lo, wkv_lo, wo_lo]
        k_diag = k_rot[:].rearrange("p (g c) -> p g c", g=NG)[:, :, 0:HD]

        block = ctx.enter_context(nc.Block())

        @block.sync
        def _(sp):
            def load_h1(t):
                sp.wait_ge(xn1_done, t)
                sp.dma_start(h1[:], h1_dram[bass.ds(t * P, P), :]).then_inc(h1_in, 16)

            def load_residual(t):
                sp.wait_ge(resid_done, t)
                sp.dma_start(resid[:], h1_dram[bass.ds(t * P, P), :]).then_inc(resid_in, 16)

            def store(t):
                sp.wait_ge(h2_done, t + 1)
                sp.dma_start(h2_dram[bass.ds(t * P, P), :], h2[:]).then_inc(h2_stored, 16)
                sp.wait_ge(xn2_done, t + 1)
                sp.dma_start(xn_dram[bass.ds(t * P, P), 0:D], xn2[:]).then_inc(xn2_stored, 16)

            sp.dma_start(h1[:], h1_dram[0:P, :]).then_inc(h1_in, 16)
            for src, dst in ((consts["ident"], ident), (consts["mask"], mask_f), (consts["cos"], cos_sb), (consts["sin"], sin_sb),
                             (bq, bq_sb), (bkv, bkv_sb), (bo, bo_sb), (router, router_sb)):
                sp.dma_start(dst[:], src).then_inc(consts_in, 16)
            for c, src in enumerate((wq, wkv, wo)):
                sp.dma_start(stage[c][:], src).then_inc(w_in[c], 16)
            sp.dma_start(resid[:], h1_dram[0:P, :]).then_inc(resid_in, 16)
            load_h1(1)
            load_h1(2)
            load_h1(3)
            with sp.Fori(2, NTILE - 2) as t:
                load_h1(t + 2)
                load_residual(t - 1)
                store(t - 2)
            load_residual(NTILE - 3)
            store(NTILE - 4)
            load_residual(NTILE - 2)
            store(NTILE - 3)
            load_residual(NTILE - 1)
            store(NTILE - 2)
            store(NTILE - 1)
            sp.wait_ge(h2_stored, 16 * NTILE)
            sp.wait_ge(xn2_stored, 16 * NTILE)

        @block.gpsimd
        def _(pool):
            pool.memset(k_rot[:], 0.0).then_inc(zeroed, 1)
            pool.memset(minus_half[:], -0.5).then_inc(zeroed, 1)
            pool.wait_ge(zeroed, 2)
            pool.wait_ge(consts_in, 16 * 8)

            def rstd(t, mv, out, mv_done, eps_done, done):
                pool.wait_ge(mv_done, t + 1)
                pool.sem_inc(pool_held, 1)
                pool.tensor_scalar_add(out[:, 0:1], mv[:, 1:2], EPS).then_inc(eps_done, 1)
                pool.wait_ge(eps_done, t + 1)
                pool.tensor_tensor(out[:, 1:2], out[:, 0:1], minus_half[:], ALU.pow).then_inc(done, 1)

            def rotate(t):
                pool.wait_ge(qk_taken, t + 1)
                pool.tensor_tensor(rope_s[:, :, 0::2], qk[:, :, 1::2], sin_sb[:, 0::2].unsqueeze(1).to_broadcast([P, NH + NG, HD // 2]), ALU.mult)
                pool.tensor_tensor(rope_s[:, :, 1::2], qk[:, :, 0::2], sin_sb[:, 1::2].unsqueeze(1).to_broadcast([P, NH + NG, HD // 2]), ALU.mult).then_inc(sin_done, 1)

            def residual(t):
                pool.wait_ge(resid_in, 16 * (t + 1))
                if not isinstance(t, int) or t > 0:
                    pool.wait_ge(h2_done, t)
                pool.tensor_tensor(resid_b[:], resid[:], bo_sb[:], ALU.add).then_inc(resid_done, 1)

            def move_v(t):
                pool.wait_ge(v_taken, t + 1)
                if not isinstance(t, int) or t > 0:
                    pool.wait_ge(pv_full, t)
                pool.sem_inc(pool_held, 1)
                pool.tensor_copy(v[:], v_next[:]).then_inc(v_moved, 1)

            def iteration(t, new, late, next_norm):
                if next_norm:
                    rstd(t + 1, mv1, rstd1, mv1_done, eps1_done, rstd1_done)
                if late:
                    residual(t - 2)
                if new:
                    rotate(t)
                if late:
                    rstd(t - 2, mv2, rstd2, mv2_done, eps2_done, rstd2_done)
                if new:
                    move_v(t)

            rstd(0, mv1, rstd1, mv1_done, eps1_done, rstd1_done)
            iteration(0, True, False, True)
            iteration(1, True, False, True)
            iteration(2, True, True, True)
            with pool.Fori(3, NTILE - 1) as t:
                iteration(t, True, True, True)
            iteration(NTILE - 1, True, True, False)
            iteration(NTILE, False, True, False)
            iteration(NTILE + 1, False, True, False)

        @block.scalar
        def _(act):
            act.wait_ge(consts_in, 16 * 8)
            nc.scalar.copy(ident_16[:], ident[:])
            for g in range(NG):
                last = nc.scalar.copy(mask_16[:, g, :], mask_f[:])
            last.then_inc(consts_16, 1)
            for c in range(3):
                act.wait_ge(w_in[c], 16)
                nc.scalar.copy(his[c][:], stage[c][:]).then_inc(w_hi_done, 1)

            def xT_high(t):
                act.wait_ge(xT_full, t + 1)
                nc.scalar.copy(xT_hi[:].rearrange("p k t -> p (k t)"), bank[4][:]).then_inc(xT_hi_done, 1)

            def qkT_high(t):
                act.wait_ge(qT_full, t + 1)
                nc.scalar.activation(qT_hi[:].rearrange("p j t -> p (j t)"), bank[7][:], ACT.Copy, scale=SCALE).then_inc(qkT_hi_done, 1)
                act.wait_ge(kT_full, t + 1)
                nc.scalar.copy(kT_hi[:], bank[6][:]).then_inc(qkT_hi_done, 1)

            def exps(t):
                for j in range(4):
                    act.wait_ge(max_done, 4 * t + j + 1)
                    for g in range(NG):
                        h = 4 * j + g
                        last = nc.scalar.activation(probs[:, j, g, :], bank[j][:, g * P:(g + 1) * P], ACT.Exp,
                                                    bias=neg_max[:, h:h + 1], accum_out=sums[:, h:h + 1])
                    last.then_inc(exp_done, 1)

            def take_probs_T(t):
                for j in range(4):
                    act.wait_ge(pT_full, 4 * t + j + 1)
                    nc.scalar.copy(probs_T[:, :, j, :], bank[j][:].rearrange("p (g q) -> p g q", g=NG)).then_inc(pT_taken, 1)

            def y_high(t):
                act.wait_ge(pv_full, t + 1)
                nc.scalar.copy(y_hi[:].rearrange("p j t -> p (j t)"), bank[5][:]).then_inc(y_hi_done, 1)

            def take_xn2_T(t):
                act.wait_ge(xn2_T_full, t + 1)
                nc.scalar.copy(xn2_T[:].rearrange("p k t -> p (k t)"), bank[7][:]).then_inc(xn2_T_taken, 1)

            def iteration(t, new, mid, routed, next_norm):
                if routed:
                    take_xn2_T(t - 3)
                if mid:
                    take_probs_T(t - 1)
                if new:
                    qkT_high(t)
                if mid:
                    y_high(t - 1)
                if next_norm:
                    xT_high(t + 1)
                if new:
                    exps(t)

            xT_high(0)
            iteration(0, True, False, False, True)
            iteration(1, True, True, False, True)
            iteration(2, True, True, False, True)
            with act.Fori(3, NTILE - 1) as t:
                iteration(t, True, True, True, True)
            iteration(NTILE - 1, True, True, True, False)
            iteration(NTILE, False, True, True, False)
            iteration(NTILE + 1, False, False, True, False)
            iteration(NTILE + 2, False, False, True, False)

        @block.vector
        def _(dve):
            dve.wait_ge(consts_in, 16 * 8)
            dve.wait_ge(zeroed, 2)

            def norm_stats(t, src, stats, mv, stats_done, mv_done):
                nc.vector.bn_stats(stats[:], src[:]).then_inc(stats_done, 1)
                dve.wait_ge(stats_done, t + 1)
                dve.sem_inc(dve_held, 1)
                nc.vector.bn_aggr(mv[:], stats[:]).then_inc(mv_done, 1)

            def norm(t, out, src, mv, rstd, rstd_done, done):
                dve.wait_ge(rstd_done, t + 1)
                nc.vector.tensor_scalar(out[:], src[:], mv[:, 0:1], rstd[:, 1:2], ALU.subtract, ALU.mult).then_inc(done, 1)

            def stats_of_h1(t):
                dve.wait_ge(h1_in, 16 * (t + 1))
                norm_stats(t, h1, stats1, mv1, stats1_done, mv1_done)

            def norm_h1(t):
                norm(t, xn1, h1, mv1, rstd1, rstd1_done, xn1_done)

            def xT_low(t):
                dve.wait_ge(xT_hi_done, t + 1)
                nc.vector.tensor_tensor(xT_lo[:].rearrange("p k t -> p (k t)"), bank[4][:],
                                        xT_hi[:].rearrange("p k t -> p (k t)").bitcast(F32), ALU.subtract).then_inc(xT_lo_done, 1)

            def take_q(t):
                dve.wait_ge(q_full, t + 1)
                nc.vector.tensor_tensor(qk[:, 0:NH, :].rearrange("p h d -> p (h d)"), bank[4][:], bq_sb[:], ALU.add)

            def take_kv(t):
                dve.wait_ge(kv_full, t + 1)
                nc.vector.tensor_tensor(qk[:, NH:, :].rearrange("p h d -> p (h d)"), bank[5][:, 0:P], bkv_sb[:, 0:P], ALU.add).then_inc(qk_taken, 1)
                dve.wait_ge(qk_taken, t + 1)
                nc.vector.tensor_tensor(rope_c[:], qk[:], cos_sb[:].unsqueeze(1).to_broadcast([P, NH + NG, HD]), ALU.mult).then_inc(cos_done, 1)
                if not isinstance(t, int) or t > 0:
                    dve.wait_ge(v_moved, t)
                nc.vector.tensor_tensor(v_next[:], bank[5][:, P:2 * P], bkv_sb[:, P:2 * P], ALU.add).then_inc(v_taken, 1)

            def rope(t):
                dve.wait_ge(cos_done, t + 1)
                dve.wait_ge(sin_done, t + 1)
                nc.vector.tensor_tensor(q_rot[:].rearrange("p j g d -> p g j d"), rope_c[:, 0:NH, :].rearrange("p (g j) d -> p g j d", g=NG),
                                        rope_s[:, 0:NH, :].rearrange("p (g j) d -> p g j d", g=NG), ALU.add)
                nc.vector.tensor_tensor(k_diag, rope_c[:, NH:, :], rope_s[:, NH:, :], ALU.add).then_inc(rope_done, 1)

            def qkT_low(t):
                dve.wait_ge(qkT_hi_done, 2 * t + 1)
                nc.vector.scalar_tensor_tensor(qT_lo[:].rearrange("p j t -> p (j t)"), bank[7][:], SCALE,
                                               qT_hi[:].rearrange("p j t -> p (j t)").bitcast(F32), ALU.mult, ALU.subtract).then_inc(qkT_lo_done, 1)
                dve.wait_ge(qkT_hi_done, 2 * t + 2)
                nc.vector.tensor_tensor(kT_lo[:], bank[6][:], kT_hi[:].bitcast(F32), ALU.subtract).then_inc(qkT_lo_done, 1)

            def maxima(t, js):
                for j in js:
                    dve.wait_ge(s_full, 4 * t + j + 1)
                    nc.vector.tensor_reduce(neg_max[:, 4 * j:4 * j + 4], bank[j][:].rearrange("p (g k) -> p g k", g=NG),
                                            AX.X, ALU.max, negate=True).then_inc(max_done, 1)

            def scale_probs(t, js):
                for j in js:
                    hs = slice(4 * j, 4 * j + 4)
                    dve.wait_ge(exp_done, 4 * t + j + 1)
                    nc.vector.reciprocal(recip[:, hs], sums[:, hs]).then_inc(recip_done, 1)
                    dve.wait_ge(recip_done, 4 * t + j + 1)
                    nc.vector.tensor_tensor(probs[:, j], probs[:, j], recip[:, hs].unsqueeze(2).to_broadcast([P, NG, P]),
                                            ALU.mult).then_inc(probs_scaled, 1)

            def y_low(t):
                dve.wait_ge(y_hi_done, t + 1)
                nc.vector.tensor_tensor(y_lo[:].rearrange("p j t -> p (j t)"), bank[5][:],
                                        y_hi[:].rearrange("p j t -> p (j t)").bitcast(F32), ALU.subtract).then_inc(y_lo_done, 1)

            def residual_sum(t):
                dve.wait_ge(wo_full, t + 1)
                dve.wait_ge(resid_done, t + 1)
                if not isinstance(t, int) or t > 0:
                    dve.wait_ge(h2_stored, 16 * t)
                nc.vector.tensor_tensor(h2[:], bank[6][:], resid_b[:], ALU.add).then_inc(h2_done, 1)

            def stats_of_h2(t):
                dve.wait_ge(h2_done, t + 1)
                norm_stats(t, h2, stats2, mv2, stats2_done, mv2_done)

            def norm_h2(t):
                if not isinstance(t, int) or t > 0:
                    dve.wait_ge(xn2_stored, 16 * t)
                norm(t, xn2, h2, mv2, rstd2, rstd2_done, xn2_done)

            def take_logits(t):
                dve.wait_ge(logits_full, t + 1)
                nc.vector.tensor_copy(logits_T[:, bass.ds(t * P, P)], bank[4][0:NE, 0:P]).then_inc(logits_taken, 1)

            def iteration(t, new, mid, late, routed, next_norm):
                if mid:
                    scale_probs(t - 1, (0,))
                if next_norm:
                    stats_of_h1(t + 1)
                if mid:
                    scale_probs(t - 1, (1,))
                if new:
                    take_q(t)
                if mid:
                    scale_probs(t - 1, (2,))
                if new:
                    take_kv(t)
                if next_norm:
                    norm_h1(t + 1)
                if mid:
                    scale_probs(t - 1, (3,))
                if new:
                    rope(t)
                if late:
                    residual_sum(t - 2)
                if late:
                    stats_of_h2(t - 2)
                if new:
                    qkT_low(t)
                if routed:
                    take_logits(t - 3)
                if mid:
                    y_low(t - 1)
                if new:
                    maxima(t, (0,))
                if next_norm:
                    xT_low(t + 1)
                if new:
                    maxima(t, (1, 2))
                if late:
                    norm_h2(t - 2)
                if new:
                    maxima(t, (3,))

            stats_of_h1(0)
            norm_h1(0)
            for c in range(3):
                dve.wait_ge(w_hi_done, c + 1)
                nc.vector.tensor_tensor(los[c][:], stage[c][:], his[c][:].bitcast(F32), ALU.subtract).then_inc(w_split, 1)
            xT_low(0)
            iteration(0, True, False, False, False, True)
            iteration(1, True, True, False, False, True)
            iteration(2, True, True, True, False, True)
            iteration(3, True, True, True, True, True)
            with dve.Fori(4, NTILE - 1) as t:
                iteration(t, True, True, True, True, True)
            iteration(NTILE - 1, True, True, True, True, False)
            iteration(NTILE, False, True, True, True, False)
            iteration(NTILE + 1, False, False, True, True, False)
            iteration(NTILE + 2, False, False, False, True, False)

        @block.tensor
        def _(pe):
            pe.wait_ge(consts_in, 16 * 8)
            pe.wait_ge(consts_16, 1)

            def three_products(dst, parts):
                n, count = 0, 3 * len(parts)
                for a_hi, a_lo, b_hi, b_lo in parts:
                    for a, b in ((a_hi, b_hi), (a_hi, b_lo), (a_lo, b_hi)):
                        last = nc.tensor.matmul(dst, a, b, start=n == 0, stop=n == count - 1)
                        n += 1
                return last

            def transpose_x(t):
                pe.wait_ge(xn1_done, t + 1)
                if not isinstance(t, int) or t > 3:
                    pe.wait_ge(logits_taken, t - 3)
                elif t > 0:
                    pe.wait_ge(qk_taken, t)
                for kt in range(KT):
                    last = nc.tensor.transpose(bank[4][:, kt * P:(kt + 1) * P], xn1[:, kt * P:(kt + 1) * P], ident[:])
                last.then_inc(xT_full, 1)

            def project(t):
                pe.wait_ge(xT_lo_done, t + 1)
                three_products(bank[4][:], [(xT_hi[:, k], xT_lo[:, k], wq_hi[:, k], wq_lo[:, k]) for k in range(KT)]).then_inc(q_full, 1)
                if not isinstance(t, int) or t > 1:
                    pe.wait_ge(y_lo_done, t - 1)
                elif t == 1:
                    pe.wait_ge(v_taken, 1)
                three_products(bank[5][:, 0:PAIR], [(xT_hi[:, k], xT_lo[:, k], wkv_hi[:, k], wkv_lo[:, k]) for k in range(KT)]).then_inc(kv_full, 1)

            def transpose_qk(t):
                pe.wait_ge(rope_done, t + 1)
                if not isinstance(t, int) or t > 2:
                    pe.wait_ge(xn2_T_taken, t - 2)
                for j in range(4):
                    last = nc.tensor.transpose(bank[7][:, j * P:(j + 1) * P], q_rot[:, j].rearrange("p g d -> p (g d)"), ident[:])
                last.then_inc(qT_full, 1)
                if not isinstance(t, int) or t > 1:
                    pe.wait_ge(h2_done, t - 1)
                for g in range(NG):
                    last = nc.tensor.transpose(bank[6][:, g * P:(g + 1) * P], k_rot[:, g * P:(g + 1) * P], ident[:])
                last.then_inc(kT_full, 1)

            def scores(t):
                pe.wait_ge(qkT_lo_done, 2 * (t + 1))
                for j in range(4):
                    if not isinstance(t, int) or t > 0:
                        pe.wait_ge(pT_taken, 4 * (t - 1) + j + 1)
                    nc.tensor.matmul(bank[j][:], ident_16[:], mask_16[:].rearrange("p g k -> p (g k)"), start=True, stop=False)
                    for n, (q, k) in enumerate(((qT_hi, kT_hi), (qT_hi, kT_lo), (qT_lo, kT_hi))):
                        last = nc.tensor.matmul(bank[j][:], q[:, j], k[:], start=False, stop=n == 2)
                    last.then_inc(s_full, 1)

            def transpose_probs(t):
                for j in range(4):
                    pe.wait_ge(probs_scaled, 4 * t + j + 1)
                    for g in range(NG):
                        last = nc.tensor.transpose(bank[j][:, g * P:(g + 1) * P], probs[:, j, g], ident[:])
                    last.then_inc(pT_full, 1)

            def weigh_values(t):
                pe.wait_ge(pT_taken, 4 * (t + 1))
                pe.wait_ge(v_moved, t + 1)
                if t != NTILE - 1 if isinstance(t, int) else True:
                    pe.wait_ge(v_taken, t + 2)
                else:
                    pe.wait_ge(y_lo_done, t)
                for g in range(NG):
                    last = nc.tensor.matmul(bank[5][g * HD:(g + 1) * HD, :], v[:, g * HD:(g + 1) * HD],
                                            probs_T[:, g].rearrange("p j q -> p (j q)"), start=True, stop=True)
                last.then_inc(pv_full, 1)

            def project_out(t):
                pe.wait_ge(w_split, 3)
                pe.wait_ge(y_lo_done, t + 1)
                if isinstance(t, int) and t == NTILE - 1:
                    pe.wait_ge(h2_done, t)
                three_products(bank[6][:], [(y_hi[:, j], y_lo[:, j], wo_hi[:, j], wo_lo[:, j]) for j in range(4)]).then_inc(wo_full, 1)

            def transpose_xn2(t):
                pe.wait_ge(xn2_done, t + 1)
                if isinstance(t, int) and t > NTILE - 3:
                    pe.wait_ge(xn2_T_taken, t)
                for kt in range(KT):
                    last = nc.tensor.transpose(bank[7][:, kt * P:(kt + 1) * P], xn2[:, kt * P:(kt + 1) * P], ident[:])
                last.then_inc(xn2_T_full, 1)

            def route(t, new):
                pe.wait_ge(xn2_T_taken, t + 1)
                if new:
                    pe.wait_ge(qk_taken, t + 4)
                else:
                    pe.wait_ge(logits_taken, t)
                for kt in range(KT):
                    last = nc.tensor.matmul(bank[4][0:NE, 0:P], router_sb[:, kt], xn2_T[:, kt], start=kt == 0, stop=kt == KT - 1)
                last.then_inc(logits_full, 1)

            def iteration(t, new, mid, late, routed, next_norm):
                if new:
                    project(t)
                if routed:
                    transpose_xn2(t - 3)
                if late:
                    project_out(t - 2)
                if mid:
                    transpose_probs(t - 1)
                if new:
                    transpose_qk(t)
                if routed:
                    route(t - 3, new)
                if mid:
                    weigh_values(t - 1)
                if next_norm:
                    transpose_x(t + 1)
                if new:
                    scores(t)

            transpose_x(0)
            pe.wait_ge(w_split, 2)
            iteration(0, True, False, False, False, True)
            iteration(1, True, True, False, False, True)
            iteration(2, True, True, True, False, True)
            iteration(3, True, True, True, True, True)
            with pe.Fori(4, NTILE - 1) as t:
                iteration(t, True, True, True, True, True)
            iteration(NTILE - 1, True, True, True, True, False)
            iteration(NTILE, False, True, True, True, False)
            iteration(NTILE + 1, False, False, True, True, False)
            iteration(NTILE + 2, False, False, False, True, False)


def routed_experts(nc, logits_T, w12, w3, xn_dram, out_dram, consts):
    ctx = ExitStack()
    with ctx:
        sb = lambda name, shape, dt=F32: ctx.enter_context(nc.sbuf_tensor("d_" + name, shape, dt))
        sem = lambda name: ctx.enter_context(nc.semaphore("d_" + name))
        bank = [ctx.enter_context(nc.psum_tensor(f"d_bank{i}", [P, 512], F32)) for i in range(8)]

        w12_sb = sb("w12", [P, NE * KT * D])
        w3_sb = sb("w3", [P, NE * 2 * D])
        ident = sb("ident", [P, P])
        before = sb("before", [P, P])
        ones = sb("ones", [P, P])
        expert_m8 = sb("expert_m8", [P, NE])
        expert_low = sb("expert_low", [P, NE, NE])
        rows_full = sb("rows_full", [P, NTILE])
        part_1 = sb("part_1", [P, 1])
        part_pad = sb("part_pad", [P, 1])
        assign_ik = sb("assign_ik", [P, 2 * NTILE])
        col = sb("col", [P, P])
        zero = sb("zero", [P, D])

        TE = [P, NTILE, NE]
        logits = sb("logits", [P, NTILE * NE])
        top = [sb(f"top{k}", [P, NTILE]) for k in range(2)]
        hit, hit_m8 = sb("hit", TE), sb("hit_m8", TE)
        choice = sb("choice", [P, NTILE])
        onehot = [sb(f"onehot{k}", TE) for k in range(2)]
        rest = sb("rest", TE)
        gap, exp_gap, denom = sb("gap", [P, NTILE]), sb("exp_gap", [P, NTILE]), sb("denom", [P, NTILE])
        weights = sb("weights", [P, NTILE, 2])
        chosen, total = sb("chosen", TE), sb("total", TE)
        cum = [sb(f"cum{i}", TE) for i in range(2)]
        earlier, slot_e, pick = sb("earlier", TE), sb("slot_e", TE), sb("pick", TE)
        over = sb("over", [P, NE, NTILE])
        nblk, first, last_b = sb("nblk", [P, NE]), sb("first", [P, NE]), sb("last_b", [P, NE])
        prod = sb("prod", [P, NE, NE])
        slot_f = sb("slot_f", [P, NTILE, 2])
        slot_i, blk_i, row_i = (sb(n, [P, 2 * NTILE], I32) for n in ("slot_i", "blk_i", "row_i"))
        blk_f, row_f = sb("blk_f", [P, 2 * NTILE]), sb("row_f", [P, 2 * NTILE])
        in_row = sb("in_row", [P, 2 * NTILE, P], BF16)
        in_blk = sb("in_blk", [P, 2 * NTILE, NBLOCK], BF16)
        marks = sb("marks", [P, 2 * NTILE, 2, NBLOCK], BF16)
        listed = sb("listed", [P, 2, NBLOCK])
        tile_i, tile_f = sb("tile_i", [P, NBLOCK], I32), sb("tile_f", [P, NBLOCK])
        unused, token = sb("unused", [P, NBLOCK]), sb("token", [P, NBLOCK])
        index_f = sb("index_f", [P, 2, NBLOCK])
        index = sb("index", [P, 2, NBLOCK], U32)
        which = sb("which", [P, NBLOCK, 2])
        done_cmp, expert_f = sb("done_cmp", [1, NBLOCK, NE]), sb("expert_f", [1, NBLOCK])
        expert = sb("expert", [1, NBLOCK], U32)

        idx_in = [sb(f"idx_in{i}", [P, 1], U32) for i in range(4)]
        idx_out = [sb(f"idx_out{i}", [P, 1], U32) for i in range(2)]
        xg = [sb(f"xg{i}", [P, XROW]) for i in range(4)]
        wsel = [sb(f"wsel{i}", [P, 2]) for i in range(2)]
        wg = [sb(f"wg{i}", [P, 1]) for i in range(2)]
        xg_T = sb("xg_T", [P, KT, P])
        gate = [sb(f"gate{i}", [P, PAIR]) for i in range(2)]
        hidden = [sb(f"hidden{i}", [P, PAIR]) for i in range(2)]
        hidden_T = sb("hidden_T", [P, 2, P])
        y = [sb(f"y{i}", [P, D]) for i in range(2)]

        consts_in, weights_in, zeroed, pad_rows = sem("consts_in"), sem("weights_in"), sem("zeroed"), sem("pad_rows")
        logits_full = sem("logits_full")
        route = sem("route")
        gap_ready, exp_gap_done = sem("gap_ready"), sem("exp_gap_done")
        chosen_ready, ranked = sem("chosen_ready"), sem("ranked")
        weights_ready, weights_out = sem("weights_ready"), sem("weights_out")
        marks_ready, list_full, routed = sem("marks_ready"), sem("list_full"), sem("routed")
        pool_held = sem("pool_held")
        idx_in_done, idx_out_done = sem("idx_in_done"), sem("idx_out_done")
        xg_in = [sem(f"xg_in{i}") for i in range(4)]
        wsel_done, wg_done = sem("wsel_done"), sem("wg_done")
        xg_T_full, xg_T_taken = sem("xg_T_full"), sem("xg_T_taken")
        up_full, gate_done, hidden_done = sem("up_full"), sem("gate_done"), sem("hidden_done")
        hidden_T_full, hidden_T_taken = sem("hidden_T_full"), sem("hidden_T_taken")
        down_full, y_done, added = sem("down_full"), sem("y_done"), sem("added")

        CONSTS = ((ident, "ident"), (before, "before"), (expert_m8, "expert_m8"), (expert_low, "expert_low"), (rows_full, "rows_full"),
                  (part_1, "part_1"), (part_pad, "part_pad"), (assign_ik, "assign_ik"), (col, "col"))

        block = ctx.enter_context(nc.Block())

        @block.sync
        def _(sp):
            for dst, name in CONSTS:
                sp.dma_start(dst[:], consts[name]).then_inc(consts_in, 16)
            sp.wait_ge(zeroed, 1)
            sp.dma_start(out_dram[T:T + P, :], zero[:]).then_inc(pad_rows, 16)
            for e in range(NE):
                sp.dma_start(w12_sb[:, e * KT * D:(e + 1) * KT * D], w12[e]).then_inc(weights_in, 16)
                sp.dma_start(w3_sb[:, e * 2 * D:(e + 1) * 2 * D], w3[e]).then_inc(weights_in, 16)
            sp.wait_ge(weights_ready, 1)
            sp.dma_start(xn_dram.rearrange("(i p) n -> p i n", p=P)[:, :, D:XROW], weights[:]).then_inc(weights_out, 16)

        @block.scalar
        def _(act):
            act.wait_ge(gap_ready, 1)
            nc.scalar.activation(exp_gap[:], gap[:], ACT.Exp).then_inc(exp_gap_done, 1)

            def take_x(b):
                act.wait_ge(xg_T_full, b + 1)
                nc.scalar.copy(xg_T[:].rearrange("p k t -> p (k t)"), bank[0][:]).then_inc(xg_T_taken, 1)

            def gate_of(b, par):
                act.wait_ge(up_full, b + 1)
                nc.scalar.activation(gate[par][:], bank[2 + par][:, 0:PAIR], ACT.Silu).then_inc(gate_done, 1)

            def take_hidden(b):
                act.wait_ge(hidden_T_full, b + 1)
                nc.scalar.copy(hidden_T[:].rearrange("p k t -> p (k t)"), bank[4][:, 0:PAIR]).then_inc(hidden_T_taken, 1)

            def iteration(b, par, up, down, nxt):
                if up:
                    gate_of(b, par)
                if down:
                    take_hidden(b - 1)
                if nxt:
                    take_x(b + 1)

            take_x(0)
            iteration(0, 0, True, False, True)
            with act.Fori(0, NBLOCK // 2 - 1) as u:
                b = 2 * u + 1
                iteration(b, 1, True, True, True)
                iteration(b + 1, 0, True, True, True)
            iteration(NBLOCK - 1, 1, True, True, False)
            iteration(NBLOCK, 0, False, True, False)

        @block.gpsimd
        def _(pool):
            pool.memset(zero[:], 0.0).then_inc(zeroed, 1)
            pool.memset(ones[:], 1.0).then_inc(zeroed, 1)
            pool.wait_ge(routed, 1)
            pool.wait_ge(weights_out, 16)
            pool.wait_ge(pad_rows, 16)

            def gather(b, slot):
                pool.tensor_copy(idx_in[slot][:], index[:, 0, bass.ds(b, 1)]).then_inc(idx_in_done, 1)
                pool.wait_ge(idx_in_done, b + 1)
                pool.sem_inc(pool_held, 1)
                pool.indirect_dma_start(xg[slot][:], None, xn_dram, bass.IndirectOffsetOnAxis(idx_in[slot][:, 0:1], 0)).then_inc(xg_in[slot], 16)

            def scatter(b, par):
                pool.tensor_copy(idx_out[par][:], index[:, 1, bass.ds(b, 1)]).then_inc(idx_out_done, 1)
                pool.wait_ge(idx_out_done, b + 1)
                pool.wait_ge(y_done, b + 1)
                if not isinstance(b, int) or b > 0:
                    pool.wait_ge(added, 16 * b)
                pool.sem_inc(pool_held, 1)
                pool.indirect_dma_start(out_dram, bass.IndirectOffsetOnAxis(idx_out[par][:, 0:1], 0), y[par][:], None,
                                        compute_op=ALU.add).then_inc(added, 16)

            for b in range(4):
                gather(b, b)

            def four(u, more):
                for k in range(4):
                    scatter(4 * u + k, k % 2)
                    if more:
                        gather(4 * u + k + 4, k)

            four(0, True)
            with pool.Fori(1, NBLOCK // 4 - 1) as u:
                four(u, True)
            four(NBLOCK // 4 - 1, False)
            pool.wait_ge(added, 16 * NBLOCK)

        @block.vector
        def _(dve):
            steps = [0]

            def step(instruction):
                steps[0] += 1
                instruction.then_inc(route, 1)
                dve.wait_ge(route, steps[0])

            V = nc.vector
            over_e = lambda t: t[:].unsqueeze(2).to_broadcast(TE)
            over_i = lambda t: t[:].unsqueeze(1).to_broadcast(TE)
            flat = lambda t: t[:].rearrange("p i e -> p (i e)")
            scores = logits[:].rearrange("p (i e) -> p i e", e=NE)
            dve.wait_ge(consts_in, 16 * len(CONSTS))
            dve.wait_ge(zeroed, 2)
            dve.wait_ge(logits_full, 1)
            step(V.tensor_copy(logits[:], bank[0][:, 0:NTILE * NE]))

            for k, src in enumerate((scores, rest[:])):
                step(V.tensor_reduce(top[k][:], src, AX.X, ALU.max))
                step(V.tensor_tensor(hit[:], src, over_e(top[k]), ALU.is_ge))
                step(V.tensor_tensor(hit_m8[:], hit[:], over_i(expert_m8), ALU.mult))
                step(V.tensor_reduce(choice[:], hit_m8[:], AX.X, ALU.min))
                step(V.tensor_tensor(onehot[k][:], over_i(expert_m8), over_e(choice), ALU.is_equal))
                if k == 0:
                    step(V.scalar_tensor_tensor(flat(rest), flat(onehot[0]), -3e38, logits[:], ALU.mult, ALU.add))
            V.tensor_tensor(gap[:], top[1][:], top[0][:], ALU.subtract).then_inc(gap_ready, 1)
            V.tensor_tensor(chosen[:], onehot[0][:], onehot[1][:], ALU.add).then_inc(chosen_ready, 1)

            dve.wait_ge(exp_gap_done, 1)
            step(V.tensor_scalar(denom[:], exp_gap[:], 1.0, None, ALU.add))
            step(V.reciprocal(weights[:, :, 0], denom[:]))
            V.tensor_tensor(weights[:, :, 1], weights[:, :, 0], exp_gap[:], ALU.mult).then_inc(weights_ready, 1)

            dve.wait_ge(ranked, 1)
            step(V.tensor_copy(flat(total), bank[1][:, 0:NTILE * NE]))
            old = total
            for n in range(5):
                s, new = 2 ** n, cum[n % 2]
                V.tensor_copy(new[:, 0:s], old[:, 0:s])
                step(V.tensor_tensor(new[:, s:], old[:, s:], old[:, :NTILE - s], ALU.add))
                old = new
            step(V.tensor_tensor(earlier[:], old[:], total[:], ALU.subtract))
            step(V.tensor_tensor(flat(slot_e), bank[0][:, 0:NTILE * NE], flat(earlier), ALU.add))
            count = old[:, NTILE - 1, :]
            step(V.tensor_tensor(over[:], count.unsqueeze(2).to_broadcast([P, NE, NTILE]), rows_full[:].unsqueeze(1).to_broadcast([P, NE, NTILE]), ALU.is_gt))
            step(V.tensor_reduce(nblk[:], over[:], AX.X, ALU.add))
            step(V.tensor_tensor(prod[:], expert_low[:], nblk[:].unsqueeze(1).to_broadcast([P, NE, NE]), ALU.mult))
            step(V.tensor_reduce(first[:], prod[:], AX.X, ALU.add))
            step(V.tensor_tensor(last_b[:], first[:], nblk[:], ALU.add))
            step(V.scalar_tensor_tensor(slot_e[:], over_i(first), float(P), slot_e[:], ALU.mult, ALU.add))
            for k in range(2):
                step(V.tensor_tensor(pick[:], onehot[k][:], slot_e[:], ALU.mult))
                step(V.tensor_reduce(slot_f[:, :, k], pick[:], AX.X, ALU.add))
            step(V.tensor_copy(slot_i[:], slot_f[:].rearrange("p i k -> p (i k)")))
            V.tensor_scalar(blk_i[:], slot_i[:], 7, None, ALU.arith_shift_right)
            step(V.tensor_scalar(row_i[:], slot_i[:], P - 1, None, ALU.bitwise_and))
            V.tensor_copy(blk_f[:], blk_i[:])
            step(V.tensor_copy(row_f[:], row_i[:]))
            A = 2 * NTILE
            step(V.tensor_tensor(in_blk[:], blk_f[:].unsqueeze(2).to_broadcast([P, A, NBLOCK]), col[:, 0:NBLOCK].unsqueeze(1).to_broadcast([P, A, NBLOCK]), ALU.is_equal))
            V.tensor_scalar(marks[:, :, 0], in_blk[:], part_1[:], None, ALU.mult)
            V.tensor_tensor(marks[:, :, 1], in_blk[:], assign_ik[:].unsqueeze(2).to_broadcast([P, A, NBLOCK]), ALU.mult)
            V.tensor_tensor(in_row[:], row_f[:].unsqueeze(2).to_broadcast([P, A, P]), col[:].unsqueeze(1).to_broadcast([P, A, P]), ALU.is_equal).then_inc(marks_ready, 1)

            step(V.tensor_tensor(done_cmp[:], last_b[0:1, :].unsqueeze(1).to_broadcast([1, NBLOCK, NE]), col[0:1, 0:NBLOCK].unsqueeze(2).to_broadcast([1, NBLOCK, NE]), ALU.is_le))
            step(V.tensor_reduce(expert_f[:], done_cmp[:], AX.X, ALU.add))
            step(V.tensor_scalar(expert[:], expert_f[:], float(NE - 1), None, ALU.min))

            dve.wait_ge(list_full, 1)
            step(V.tensor_copy(listed[:].rearrange("p a b -> p (a b)"), bank[5][:, 0:2 * NBLOCK]))
            step(V.tensor_copy(tile_i[:], listed[:, 1]))
            step(V.tensor_scalar(tile_i[:], tile_i[:], 1, None, ALU.arith_shift_right))
            step(V.tensor_copy(tile_f[:], tile_i[:]))
            step(V.scalar_tensor_tensor(token[:], tile_f[:], float(P), listed[:, 0], ALU.mult, ALU.add))
            step(V.tensor_scalar(token[:], token[:], -1.0, None, ALU.add))
            V.tensor_scalar(index_f[:, 0], token[:], 0.0, None, ALU.max)
            step(V.scalar_tensor_tensor(which[:, :, 1], tile_f[:], -2.0, listed[:, 1], ALU.mult, ALU.add))
            V.tensor_scalar(which[:, :, 0], which[:, :, 1], -1.0, 1.0, ALU.mult, ALU.add)
            step(V.tensor_scalar(unused[:], listed[:, 0], 0.0, None, ALU.is_equal))
            step(V.scalar_tensor_tensor(index_f[:, 1], unused[:], part_pad[:], token[:], ALU.mult, ALU.add))
            V.tensor_copy(index[:], index_f[:]).then_inc(routed, 1)

            def hidden_of(b, par):
                dve.wait_ge(gate_done, b + 1)
                V.tensor_tensor(hidden[par][:], gate[par][:], bank[2 + par][:, PAIR:2 * PAIR], ALU.mult).then_inc(hidden_done, 1)

            def weigh(b, par, slot):
                dve.wait_ge(xg_in[slot], 4 * (b - slot) + 16)
                V.tensor_tensor(wsel[par][:], xg[slot][:, D:XROW], which[:, bass.ds(b, 1), :].rearrange("p b k -> p (b k)"), ALU.mult).then_inc(wsel_done, 1)
                dve.wait_ge(wsel_done, b + 1)
                V.tensor_reduce(wg[par][:], wsel[par][:], AX.X, ALU.add).then_inc(wg_done, 1)
                dve.wait_ge(wg_done, b + 1)
                dve.wait_ge(down_full, b + 1)
                if not isinstance(b, int) or b > 1:
                    dve.wait_ge(added, 16 * (b - 1))
                V.tensor_scalar(y[par][:], bank[6 + par][:], wg[par][:], None, ALU.mult).then_inc(y_done, 1)

            def iteration(b, k, up, down):
                if up:
                    hidden_of(b, k % 2)
                if down:
                    weigh(b - 1, (k + 1) % 2, (k + 3) % 4)

            for b in range(4):
                iteration(b, b, True, b > 0)
            with dve.Fori(1, NBLOCK // 4) as u:
                for k in range(4):
                    iteration(4 * u + k, k, True, True)
            iteration(NBLOCK, 0, False, True)

        @block.tensor
        def _(pe):
            pe.wait_ge(consts_in, 16 * len(CONSTS))
            pe.wait_ge(zeroed, 2)
            for i in range(NTILE):
                last = nc.tensor.transpose(bank[0][:, i * NE:(i + 1) * NE], logits_T[:, i * P:(i + 1) * P], ident[0:NE, 0:NE])
            last.then_inc(logits_full, 1)
            pe.wait_ge(chosen_ready, 1)
            nc.tensor.matmul(bank[0][:, 0:NTILE * NE], before[:], chosen[:].rearrange("p i e -> p (i e)"), start=True, stop=True)
            nc.tensor.matmul(bank[1][:, 0:NTILE * NE], ones[:], chosen[:].rearrange("p i e -> p (i e)"), start=True, stop=True).then_inc(ranked, 1)
            pe.wait_ge(marks_ready, 1)
            for a in range(2 * NTILE):
                last = nc.tensor.matmul(bank[5][:, 0:2 * NBLOCK], in_row[:, a], marks[:, a].rearrange("p c b -> p (c b)"), start=a == 0, stop=a == 2 * NTILE - 1)
            last.then_inc(list_full, 1)
            pe.wait_ge(routed, 1)
            pe.wait_ge(weights_in, 16 * 2 * NE)

            def transpose_x(b, slot):
                pe.wait_ge(xg_in[slot], 4 * (b - slot) + 16)
                if not isinstance(b, int) or b > 0:
                    pe.wait_ge(xg_T_taken, b)
                for kt in range(KT):
                    last = nc.tensor.transpose(bank[0][:, kt * P:(kt + 1) * P], xg[slot][:, kt * P:(kt + 1) * P], ident[:])
                last.then_inc(xg_T_full, 1)

            def expert_of(b):
                return pe.value_load(expert[0:1, bass.ds(b, 1)], min_val=0, max_val=NE - 1)

            def up(b, par):
                e = expert_of(b)
                pe.wait_ge(xg_T_taken, b + 1)
                if not isinstance(b, int) or b > 1:
                    pe.wait_ge(hidden_done, b - 1)
                for kt in range(KT):
                    last = nc.tensor.matmul(bank[2 + par][:], xg_T[:, kt], w12_sb[:, bass.ds(e * (KT * D) + kt * D, D)], start=kt == 0, stop=kt == KT - 1)
                last.then_inc(up_full, 1)

            def transpose_hidden(b, par):
                pe.wait_ge(hidden_done, b + 1)
                for ft in range(2):
                    last = nc.tensor.transpose(bank[4][:, ft * P:(ft + 1) * P], hidden[par][:, ft * P:(ft + 1) * P], ident[:])
                last.then_inc(hidden_T_full, 1)

            def down(b, par):
                e = expert_of(b)
                pe.wait_ge(hidden_T_taken, b + 1)
                if not isinstance(b, int) or b > 1:
                    pe.wait_ge(y_done, b - 1)
                for ft in range(2):
                    last = nc.tensor.matmul(bank[6 + par][:], hidden_T[:, ft], w3_sb[:, bass.ds(e * (2 * D) + ft * D, D)], start=ft == 0, stop=ft == 1)
                last.then_inc(down_full, 1)

            def iteration(b, k, is_up, is_down, nxt):
                if is_up:
                    up(b, k % 2)
                if is_down:
                    transpose_hidden(b - 1, (k + 1) % 2)
                if nxt:
                    transpose_x(b + 1, (k + 1) % 4)
                if is_down:
                    down(b - 1, (k + 1) % 2)

            transpose_x(0, 0)
            for b in range(4):
                iteration(b, b, True, b > 0, True)
            with pe.Fori(1, NBLOCK // 4 - 1) as u:
                for k in range(4):
                    iteration(4 * u + k, k, True, True, True)
            for b in range(NBLOCK - 4, NBLOCK):
                iteration(b, b % 4, True, True, b < NBLOCK - 1)
            iteration(NBLOCK, 0, False, True, False)


def shape_constants():
    f = lambda a: np.ascontiguousarray(a, dtype=np.float32)
    p = np.arange(P)
    inv_freq = (1.0 / 10000.0 ** (np.arange(0, HD, 2, dtype=np.float32) / np.float32(HD))).astype(np.float32)
    angles = np.arange(P, dtype=np.float32)[:, None] * inv_freq
    sin = np.repeat(np.sin(angles), 2, axis=1)
    sin[:, 0::2] *= -1
    e = np.arange(NE)
    rows = lambda a: f(np.broadcast_to(a, (P,) + a.shape))
    return {
        "ident": f(np.eye(P)),
        "mask": f(np.where(p[None, :] <= p[:, None], 0.0, -1e30)),
        "cos": f(np.repeat(np.cos(angles), 2, axis=1)),
        "sin": f(sin),
        "before": f(p[:, None] < p[None, :]),
        "expert_m8": rows(e - 8.0),
        "expert_low": rows((e[None, :] < e[:, None]).astype(np.float32)),
        "rows_full": rows(np.arange(NTILE) * float(P)),
        "part_1": f(p[:, None] + 1),
        "part_pad": f(p[:, None] + T + 1),
        "assign_ik": rows(np.arange(2 * NTILE) * 1.0),
        "col": rows(p * 1.0),
    }


def build(nc, a, out):
    h1_dram = nc.dram_tensor("h1_dram", (T, D), F32).ap()
    xn_dram = nc.dram_tensor("xn_dram", (T, XROW), F32).ap()
    dilated_attention(nc, a["x_pairs"], a["wqkv"], a["bqk"], a["bv"], a["wout"], a["bout"], h1_dram, a)
    with nc.sbuf_tensor("logits_T", [NE, T], F32) as logits_T:
        causal_attention(nc, h1_dram, a["wq"], a["wkv"], a["wo"], a["bq"], a["bkv"], a["bo"], a["router"], out, xn_dram, logits_T, a)
        routed_experts(nc, logits_T, a["w12"], a["w3"], xn_dram, out, a)


def laid_out(x, L0_tok_Wqkv, L0_tok_b_qkv, L0_tok_Wout, L0_tok_b_out, L0_attn_Wq, L0_attn_bq, L0_attn_Wkv, L0_attn_bkv,
             L0_attn_Wo, L0_attn_bo, L0_ffn_router_w, L0_ffn_w1, L0_ffn_w2, L0_ffn_w3):
    c = np.ascontiguousarray
    by_rows = lambda w: c(np.asarray(w).reshape(KT, P, -1).transpose(1, 0, 2))
    repeated = lambda b: c(np.broadcast_to(np.asarray(b), (P, b.shape[0])))
    x_T = np.asarray(x).reshape(2 * NTILE, SEG, 2, D).transpose(2, 3, 0, 1).reshape(2, KT, P, NPAIR, PAIR)
    w12 = np.concatenate([np.asarray(L0_ffn_w1), np.asarray(L0_ffn_w2)], axis=2)
    return {
        "x_pairs": c(x_T.transpose(0, 3, 2, 1, 4)),
        "wqkv": by_rows(L0_tok_Wqkv.T),
        "bqk": c(np.asarray(L0_tok_b_qkv)[:2 * D].reshape(2 * KT, P).T),
        "bv": repeated(L0_tok_b_qkv[2 * D:]),
        "wout": by_rows(L0_tok_Wout.T),
        "bout": repeated(L0_tok_b_out),
        "wq": by_rows(L0_attn_Wq),
        "wkv": by_rows(L0_attn_Wkv),
        "wo": c(np.asarray(L0_attn_Wo).reshape(NG, 4, HD, D).transpose(0, 2, 1, 3).reshape(P, 4, D)),
        "bq": repeated(L0_attn_bq),
        "bkv": repeated(L0_attn_bkv),
        "bo": repeated(L0_attn_bo),
        "router": by_rows(L0_ffn_router_w.T),
        "w12": c(w12.reshape(NE, KT, P, D).transpose(0, 2, 1, 3).reshape(NE, P, KT * D)),
        "w3": c(np.asarray(L0_ffn_w3).reshape(NE, 2, P, D).transpose(0, 2, 1, 3).reshape(NE, P, 2 * D)),
    }


def kernel(**inputs):
    import concourse.bacc as bacc
    from concourse.bass_utils import run_bass_kernel_spmd

    nc = bacc.Bacc("TRN2", target_bir_lowering=False, num_devices=1)
    arrays = {**laid_out(**inputs), **shape_constants()}
    aps = {n: nc.dram_tensor(n, a.shape, mybir.dt.from_np(a.dtype), kind="ExternalInput").ap() for n, a in arrays.items()}
    out = nc.dram_tensor("out", (T + P, D), F32, kind="ExternalOutput").ap()
    build(nc, aps, out)
    r = run_bass_kernel_spmd(nc, [arrays], core_ids=[0])
    return r.results[0]["out"][:T].reshape(NTILE, P, D)
```

```python
import numpy as np
import concourse.bass as bass
from concourse import mybir
from contextlib import ExitStack

F32, F32R, BF16, U32 = mybir.dt.float32, mybir.dt.float32r, mybir.dt.bfloat16, mybir.dt.uint32
ACT, ALU, AX = mybir.ActivationFunctionType, mybir.AluOpType, mybir.AxisListType

P = 128
D = 512
KT = D // P
NH, HD = 16, 32
NG = 4
SEG = 64
T = 32 * P
NTILE = T // P
PAIR = 2 * P
NPAIR = NTILE // 2
SCALE = 1.0 / float(np.sqrt(HD))
EPS = 1e-5

NE = 8
NBLOCK = 2 * T // P + NE
I32 = mybir.dt.int32
XROW = D + 2
W = KT * 3 * D
EXP12 = KT * D
EXP3 = 2 * D
EARLY = (0, 1, 2, 3, 7)


def dilated_attention(nc, x_pairs, wqkv, bqk, bv, wout, bout, h1_dram, h1_stored, h1_out, next_h1, wa_parts, ident, early_loads, wb, wb_parts):
    ctx = ExitStack()
    with ctx:
        sb = lambda name, shape, dt=F32: ctx.enter_context(nc.sbuf_tensor("a_" + name, shape, dt))
        sem = lambda name: ctx.enter_context(nc.semaphore("a_" + name))
        bank = [ctx.enter_context(nc.psum_tensor(f"a_bank{i}", [P, 512], F32)) for i in range(8)]

        w_stage, w_hi, w_lo = wa_parts
        wo_stage = sb("wo_stage", [P, KT, D])
        wo_hi = sb("wo_hi", [P, KT, D], F32R)
        wo_lo = sb("wo_lo", [P, KT, D], F32R)
        bqk_raw = sb("bqk_raw", [P, 8])
        bqk_sb = sb("bqk_sb", [P, 8])
        bv_sb = sb("bv_sb", [P, D])
        bout_sb = sb("bout_sb", [P, D])
        x_raw = sb("x_raw", [P, KT, PAIR])
        x_hi = sb("x_hi", [P, KT, PAIR], F32R)
        x_lo = sb("x_lo", [P, KT, PAIR], F32R)
        q_T = sb("q_T", [P, KT, PAIR])
        k_blk = sb("k_blk", [P, 4, KT, 4, SEG])
        v_blk = [sb(f"v_blk{a}", [P, 2, 8, 64]) for a in range(2)]
        neg_max = [sb(f"neg_max{a}", [P, NH]) for a in range(2)]
        probs = [sb(f"probs{a}", [P, NH, SEG]) for a in range(2)]
        probs_T = sb("probs_T", [P, 8, P])
        sums = [sb(f"sums{a}", [P, NH]) for a in range(2)]
        recip = [sb(f"recip{a}", [P, NH]) for a in range(2)]
        y_hi = [sb(f"y_hi{a}", [P, KT, P], F32R) for a in range(2)]
        y_lo = [sb(f"y_lo{a}", [P, KT, P], F32R) for a in range(2)]
        h1 = h1_out

        consts_in, zeroed, scaled_bias = sem("consts_in"), sem("zeroed"), sem("scaled_bias")
        w_in = [sem(f"w_in{c}") for c in range(5)]
        early_in = sem("early_in")
        wb_in = [sem(f"wb_in{c}") for c in range(3)]
        wb_hi_done, wb_split = sem("wb_hi_done"), sem("wb_split")
        w_hi_done, w_split = sem("w_hi_done"), sem("w_split")
        x_in, x_hi_done, x_split = sem("x_in"), sem("x_hi_done"), sem("x_split")
        qk_full, q_taken, k_taken = sem("qk_full"), sem("q_taken"), sem("k_taken")
        v_full, v_taken = sem("v_full"), sem("v_taken")
        s_full, max_done, exp_done = sem("s_full"), sem("max_done"), sem("exp_done")
        pT_full, pT_taken = sem("pT_full"), sem("pT_taken")
        recip_done, probs_scaled = sem("recip_done"), sem("probs_scaled")
        pv_full, y_hi_done, y_lo_done = sem("pv_full"), sem("y_hi_done"), sem("y_lo_done")
        out_full, h1_done = sem("out_full"), sem("h1_done")
        next_h1_in = sem("next_h1_in")

        pool_held = sem("pool_held")

        cuts = [slice(0, PAIR), slice(PAIR, D), slice(D, 2 * D), slice(2 * D, 3 * D)]
        stage = [w_stage[:, :, c] for c in cuts] + [wo_stage[:, :, :]]
        his = [w_hi[:, :, c] for c in cuts] + [wo_hi[:, :, :]]
        los = [w_lo[:, :, c] for c in cuts] + [wo_lo[:, :, :]]

        block = ctx.enter_context(nc.Block())

        @block.sync
        def _(sp):
            sp.dma_start(x_raw[:], x_pairs[0, 0:1].rearrange("o p k t -> (o p) k t")).then_inc(x_in, 16)
            for c in range(4):
                sp.dma_start(stage[c], wqkv[:, :, cuts[c]]).then_inc(w_in[c], 16)
                if c == 0:
                    sp.dma_start(bqk_raw[:], bqk).then_inc(consts_in, 16)
                    sp.dma_start(bv_sb[:], bv).then_inc(consts_in, 16)
                    sp.dma_start(bout_sb[:], bout).then_inc(consts_in, 16)
            sp.dma_start(stage[4], wout).then_inc(w_in[4], 16)
            for dst, src in early_loads:
                sp.dma_start(dst, src).then_inc(early_in, 16)

            def store(p, a):
                sp.wait_ge(h1_done, 2 * p + a + 1)
                sp.dma_start(h1_dram[bass.ds((2 * p + a) * P, P), :], h1[a][:]).then_inc(h1_stored[a], 16)

            def load(p):
                sp.wait_ge(x_split, p)
                sp.dma_start(x_raw[:], x_pairs[0, bass.ds(p, 1)].rearrange("o p k t -> (o p) k t")).then_inc(x_in, 16)

            load(1)
            sp.wait_ge(w_split, 4)
            for c in range(3):
                sp.dma_start(wb_parts[c][0], wb[c]).then_inc(wb_in[c], 16)
            with sp.Fori(1, NPAIR - 1) as p:
                load(p + 1)
                store(p - 1, 0)
                store(p - 1, 1)
            for a in range(2):
                sp.wait_ge(h1_stored[a], 16 * (NPAIR - 2))
            sp.dma_start(next_h1, h1_dram[0:P, :]).then_inc(next_h1_in, 16)
            for p in (NPAIR - 2, NPAIR - 1):
                store(p, 0)
                store(p, 1)
            sp.wait_ge(next_h1_in, 16)
            sp.wait_ge(early_in, 16 * len(early_loads))
            sp.wait_ge(wb_in[2], 16)

        @block.gpsimd
        def _(pool):
            pool.memset(k_blk[:], 0.0).then_inc(zeroed, 1)

            def split(p):
                pool.wait_ge(x_in, 16 * (p + 1))
                pool.sem_inc(pool_held, 1)
                pool.tensor_copy(x_hi[:], x_raw[:]).then_inc(x_hi_done, 1)
                pool.wait_ge(x_hi_done, p + 1)
                pool.tensor_tensor(x_lo[:], x_raw[:], x_hi[:].bitcast(F32), ALU.subtract).then_inc(x_split, 1)

            with pool.Fori(1, NPAIR) as p:
                pool.wait_ge(v_full, 2 * p)
                split(p)
            for c in range(2):
                raw, hi, lo = wb_parts[c]
                pool.wait_ge(wb_in[c], 16)
                pool.tensor_copy(hi, raw).then_inc(wb_hi_done, 1)
                pool.wait_ge(wb_hi_done, c + 1)
                pool.tensor_tensor(lo, raw, hi.bitcast(F32), ALU.subtract).then_inc(wb_split, 1)

        @block.scalar
        def _(act):
            for c in range(5):
                act.wait_ge(w_in[c], 16)
                nc.scalar.copy(his[c], stage[c]).then_inc(w_hi_done, 1)
            act.wait_ge(scaled_bias, 1)
            act.wait_ge(zeroed, 3)

            def take_qk(p):
                for i in range(2):
                    act.wait_ge(qk_full, 4 * p + i + 1)
                    for ft in (2 * i, 2 * i + 1):
                        last = nc.scalar.activation(q_T[:, ft, :], bank[i][:, (ft % 2) * PAIR:(ft % 2 + 1) * PAIR],
                                                    ACT.Identity, bias=bqk_sb[:, ft:ft + 1], scale=SCALE)
                    last.then_inc(q_taken, 1)
                for i in range(2):
                    act.wait_ge(qk_full, 4 * p + i + 3)
                    for ft in (2 * i, 2 * i + 1):
                        for h in range(4):
                            r = slice(HD * h, HD * h + HD)
                            src = bank[2 + i][r, (ft % 2) * PAIR:(ft % 2 + 1) * PAIR]
                            last = nc.scalar.activation(k_blk[r, :, ft, h, :], src.rearrange("p (s k) -> p s k", s=4),
                                                        ACT.Identity, bias=bqk_sb[r, 4 + ft:5 + ft])
                    last.then_inc(k_taken, 1)

            def exps(p, a):
                for i in range(2):
                    act.wait_ge(max_done, 4 * p + 2 * a + i + 1)
                    for h in range(8 * i, 8 * i + 8):
                        last = nc.scalar.activation(probs[a][:, h, :], bank[2 * a + i][:, (h % 8) * SEG:(h % 8 + 1) * SEG],
                                                    ACT.Exp, bias=neg_max[a][:, h:h + 1], accum_out=sums[a][:, h:h + 1])
                    last.then_inc(exp_done, 1)

            def y_high(p, a):
                act.wait_ge(pv_full, 2 * p + a + 1)
                nc.scalar.copy(y_hi[a][:].rearrange("p k t -> p (k t)"), bank[5][:]).then_inc(y_hi_done, 1)

            def iteration(p, new, old):
                if new:
                    take_qk(p)
                if old:
                    y_high(p - 1, 0)
                if new:
                    exps(p, 0)
                if old:
                    y_high(p - 1, 1)
                if new:
                    exps(p, 1)

            iteration(0, True, False)
            with act.Fori(1, NPAIR) as p:
                iteration(p, True, True)
            iteration(NPAIR, False, True)

        @block.vector
        def _(dve):
            nc.vector.memset(v_blk[0][:], 0.0).then_inc(zeroed, 1)
            nc.vector.memset(v_blk[1][:], 0.0).then_inc(zeroed, 1)
            dve.wait_ge(x_in, 16)
            nc.vector.tensor_copy(x_hi[:], x_raw[:]).then_inc(x_hi_done, 1)
            dve.wait_ge(x_hi_done, 1)
            nc.vector.tensor_tensor(x_lo[:], x_raw[:], x_hi[:].bitcast(F32), ALU.subtract).then_inc(x_split, 1)
            dve.wait_ge(consts_in, 16 * 3)
            nc.vector.tensor_scalar(bqk_sb[:, 0:4], bqk_raw[:, 0:4], SCALE, None, ALU.mult)
            nc.vector.tensor_copy(bqk_sb[:, 4:8], bqk_raw[:, 4:8]).then_inc(scaled_bias, 1)
            for c in range(5):
                dve.wait_ge(w_hi_done, c + 1)
                nc.vector.tensor_tensor(los[c], stage[c], his[c].bitcast(F32), ALU.subtract).then_inc(w_split, 1)
            dve.wait_ge(zeroed, 3)

            def take_probs_T(p, a):
                for i in range(2):
                    dve.wait_ge(pT_full, 4 * p + 2 * a + i + 1)
                    nc.vector.tensor_copy(probs_T[:, 4 * i:4 * i + 4, :].rearrange("p h q -> p (h q)"),
                                          bank[4 + i][:]).then_inc(pT_taken, 1)

            def take_v(p, a, old):
                dve.wait_ge(v_full, 2 * p + a + 1)
                if old:
                    dve.wait_ge(pv_full, 2 * p + a - 1)
                for s in range(2):
                    for r in range(2):
                        src = bank[6 + a][64 * s:64 * s + 64, :].rearrange("p (h r d) -> p r h d", r=2, d=HD)[:, r]
                        b = bv_sb[64 * s:64 * s + 64, :].rearrange("p (h r d) -> p r h d", r=2, d=HD)[:, r]
                        last = nc.vector.tensor_tensor(v_blk[a][64 * r:64 * r + 64, s, :, HD * r:HD * r + HD],
                                                       src, b, ALU.add)
                last.then_inc(v_taken, 1)

            def scale_probs(p, a):
                for i in range(2):
                    n = 4 * p + 2 * a + i + 1
                    hs = slice(8 * i, 8 * i + 8)
                    dve.wait_ge(exp_done, n)
                    nc.vector.reciprocal(recip[a][:, hs], sums[a][:, hs]).then_inc(recip_done, 1)
                    dve.wait_ge(recip_done, n)
                    nc.vector.tensor_tensor(probs[a][:, hs, :], probs[a][:, hs, :],
                                            recip[a][:, hs].unsqueeze(2).to_broadcast([P, 8, SEG]), ALU.mult).then_inc(probs_scaled, 1)

            def y_low(p, a):
                dve.wait_ge(y_hi_done, 2 * p + a + 1)
                nc.vector.tensor_tensor(y_lo[a][:].rearrange("p k t -> p (k t)"), bank[5][:],
                                        y_hi[a][:].rearrange("p k t -> p (k t)").bitcast(F32), ALU.subtract).then_inc(y_lo_done, 1)

            def maxima(p, a):
                for i in range(2):
                    dve.wait_ge(s_full, 4 * p + 2 * a + i + 1)
                    nc.vector.tensor_reduce(neg_max[a][:, 8 * i:8 * i + 8], bank[2 * a + i][:].rearrange("p (h k) -> p h k", k=SEG),
                                            AX.X, ALU.max, negate=True).then_inc(max_done, 1)

            def take_out(p, a, peeled):
                dve.wait_ge(out_full, 2 * p + a + 1)
                if not peeled:
                    dve.wait_ge(h1_stored[a], 16 * p)
                nc.vector.tensor_tensor(h1[a][:], bank[6 + a][:], bout_sb[:], ALU.add).then_inc(h1_done, 1)

            def iteration(p, new, old, first_old=False):
                if old:
                    scale_probs(p - 1, 0)
                    take_probs_T(p - 1, 0)
                    scale_probs(p - 1, 1)
                if new:
                    take_v(p, 0, old)
                if old:
                    y_low(p - 1, 0)
                    take_probs_T(p - 1, 1)
                if new:
                    maxima(p, 0)
                    maxima(p, 1)
                if new:
                    take_v(p, 1, old)
                if old:
                    y_low(p - 1, 1)
                if old:
                    take_out(p - 1, 0, first_old)
                    take_out(p - 1, 1, first_old)

            iteration(0, True, False)
            iteration(1, True, True, True)
            with dve.Fori(2, NPAIR) as p:
                iteration(p, True, True)
            iteration(NPAIR, False, True)

        @block.tensor
        def _(pe):
            def project_qk(p, first):
                pe.wait_ge(x_split, p + 1)
                for i in range(4):
                    if first:
                        pe.wait_ge(w_split, min(i, 2) + 1)
                    else:
                        pe.wait_ge(exp_done, 4 * (p - 1) + i + 1)
                    for half in range(2):
                        e = (2 * i + half) * P
                        dst = bank[i][:, half * PAIR:(half + 1) * PAIR]
                        n = 0
                        for kt in range(KT):
                            for w, x in ((w_hi, x_hi), (w_hi, x_lo), (w_lo, x_hi)):
                                last = nc.tensor.matmul(dst, w[:, kt, e:e + P], x[:, kt, :], start=n == 0, stop=n == 3 * KT - 1)
                                n += 1
                    last.then_inc(qk_full, 1)

            def project_v(p, a, first):
                if first:
                    pe.wait_ge(w_split, 4)
                if not first:
                    pe.wait_ge(h1_done, 2 * (p - 1) + a - 1) if not isinstance(p, int) or p > 1 else None
                n = 0
                for kt in range(KT):
                    for x, w in ((x_hi, w_hi), (x_hi, w_lo), (x_lo, w_hi)):
                        last = nc.tensor.matmul(bank[6 + a][:], x[:, kt, a * P:(a + 1) * P], w[:, kt, 2 * D:3 * D],
                                                start=n == 0, stop=n == 3 * KT - 1)
                        n += 1
                last.then_inc(v_full, 1)

            def transpose_probs(p, a, peeled):
                if not peeled or a:
                    pe.wait_ge(y_lo_done, 2 * p + a)
                for i in range(2):
                    pe.wait_ge(probs_scaled, 4 * p + 2 * a + i + 1)
                    for hp in range(4 * i, 4 * i + 4):
                        last = nc.tensor.transpose(bank[4 + i][:, (hp % 4) * P:(hp % 4 + 1) * P],
                                                   probs[a][:, 2 * hp:2 * hp + 2, :].rearrange("p h k -> p (h k)"), ident[:])
                    last.then_inc(pT_full, 1)

            def scores(p, a):
                pe.wait_ge(q_taken, 2 * (p + 1))
                pe.wait_ge(k_taken, 2 * (p + 1))
                for i in range(2):
                    for ft in (2 * i, 2 * i + 1):
                        for s in range(2):
                            c = (ft % 2) * PAIR
                            last = nc.tensor.matmul(bank[2 * a + i][64 * s:64 * s + 64, c:c + PAIR],
                                                    q_T[:, ft, a * P + s * SEG:a * P + (s + 1) * SEG],
                                                    k_blk[:, 2 * a + s, ft, :, :].rearrange("p h k -> p (h k)"), start=True, stop=True)
                    last.then_inc(s_full, 1)

            def weigh_values(p, a):
                pe.wait_ge(pT_taken, 4 * p + 2 * a + 2)
                pe.wait_ge(v_taken, 2 * p + a + 1)
                for hp in range(8):
                    for s in range(2):
                        r, c = hp % 2, (hp // 2) * P + s * SEG
                        last = nc.tensor.matmul(bank[5][64 * r:64 * r + 64, c:c + SEG], v_blk[a][:, s, hp, :],
                                                probs_T[:, hp, s * SEG:(s + 1) * SEG], start=True, stop=True)
                last.then_inc(pv_full, 1)

            def project_out(p, a, new):
                if new:
                    pe.wait_ge(v_taken, 2 * (p + 1) + a + 1)
                pe.wait_ge(w_split, 5)
                pe.wait_ge(y_lo_done, 2 * p + a + 1)
                n = 0
                for ft in range(KT):
                    for y, w in ((y_hi[a], wo_hi), (y_hi[a], wo_lo), (y_lo[a], wo_hi)):
                        last = nc.tensor.matmul(bank[6 + a][:], y[:, ft, :], w[:, ft, :], start=n == 0, stop=n == 3 * KT - 1)
                        n += 1
                last.then_inc(out_full, 1)

            def iteration(p, new, old, first_old=False):
                if new:
                    project_qk(p, not old)
                if old:
                    transpose_probs(p - 1, 0, first_old)
                if new:
                    project_v(p, 0, not old)
                if old:
                    weigh_values(p - 1, 0)
                if new:
                    project_v(p, 1, not old)
                if old:
                    transpose_probs(p - 1, 1, first_old)
                if new:
                    scores(p, 0)
                    scores(p, 1)
                if old:
                    weigh_values(p - 1, 1)
                    project_out(p - 1, 0, new)
                    project_out(p - 1, 1, new)

            iteration(0, True, False)
            pe.wait_ge(early_in, 16 * len(early_loads))
            iteration(1, True, True, True)
            with pe.Fori(2, NPAIR) as p:
                iteration(p, True, True)
            iteration(NPAIR, False, True)


def causal_attention(nc, h1_dram, h1, h1_stored, wb_parts, small, h2_dram, xn_dram, logits_T, chunks, chunk_parts, halves_dram, next_small):
    ctx = ExitStack()
    with ctx:
        sb = lambda name, shape, dt=F32: ctx.enter_context(nc.sbuf_tensor("b_" + name, shape, dt))
        sem = lambda name: ctx.enter_context(nc.semaphore("b_" + name))
        bank = [ctx.enter_context(nc.psum_tensor(f"b_bank{i}", [P, 512], F32)) for i in range(8)]

        (_, wq_hi, wq_lo), (_, wkv_hi, wkv_lo), (wo_stage, _, _) = wb_parts
        wo_hi, wo_lo = sb("wo_hi", [P, KT, D], F32R), sb("wo_lo", [P, KT, D], F32R)
        ident, mask_f, cos_sb, sin_sb, bq_sb, bkv_sb, bo_sb, router_sb = (small[n] for n in ("ident", "mask", "cos", "sin", "bq", "bkv", "bo", "router"))
        ident_16 = sb("ident_16", [P, P], BF16)
        mask_16 = sb("mask_16", [P, NG, P], BF16)
        minus_half = sb("minus_half", [P, 1])

        stats1, mv1, rstd1 = sb("stats1", [P, 6]), sb("mv1", [P, 2]), sb("rstd1", [P, 2])
        xn1 = sb("xn1", [P, D])
        xT_hi, xT_lo = sb("xT_hi", [P, KT, P], F32R), sb("xT_lo", [P, KT, P], F32R)
        qk = sb("qk", [P, NH + NG, HD])
        v_next, v = sb("v_next", [P, NG * HD]), sb("v", [P, NG * HD])
        rope_c, rope_s = sb("rope_c", [P, NH + NG, HD]), sb("rope_s", [P, NH + NG, HD])
        q_rot = sb("q_rot", [P, 4, NG, HD])
        k_rot = sb("k_rot", [P, NG * (P + HD)])
        qT_hi, qT_lo = sb("qT_hi", [P, 4, P], F32R), sb("qT_lo", [P, 4, P], F32R)
        kT_hi, kT_lo = sb("kT_hi", [P, NG * P], F32R), sb("kT_lo", [P, NG * P], F32R)
        neg_max, sums, recip = sb("neg_max", [P, NH]), sb("sums", [P, NH]), sb("recip", [P, NH])
        probs = sb("probs", [P, 4, NG, P])
        probs_T = sb("probs_T", [P, NG, 4, P])
        y_hi, y_lo = sb("y_hi", [P, 4, P], F32R), sb("y_lo", [P, 4, P], F32R)
        resid, resid_b = sb("resid", [P, D]), sb("resid_b", [P, D])
        h2 = sb("h2", [P, D])
        stats2, mv2, rstd2 = sb("stats2", [P, 6]), sb("mv2", [P, 2]), sb("rstd2", [P, 2])
        xn2 = sb("xn2", [P, D])
        xn2_T = sb("xn2_T", [P, KT, P])

        zeroed, consts_16 = sem("zeroed"), sem("consts_16")
        small_in = sem("small_in")
        chunk_in, chunk_hi_done, chunk_lo_done, chunk_stored = sem("chunk_in"), sem("chunk_hi_done"), sem("chunk_lo_done"), sem("chunk_stored")
        chunk_raw, chunk_hi, chunk_lo = chunk_parts
        w_hi_done, w_split = sem("w_hi_done"), sem("w_split")
        h1_in, resid_in, resid_done = sem("h1_in"), sem("resid_in"), sem("resid_done")
        stats1_done, mv1_done, eps1_done, rstd1_done, xn1_done = (sem(n) for n in ("stats1_done", "mv1_done", "eps1_done", "rstd1_done", "xn1_done"))
        stats2_done, mv2_done, eps2_done, rstd2_done, xn2_done = (sem(n) for n in ("stats2_done", "mv2_done", "eps2_done", "rstd2_done", "xn2_done"))
        xT_full, xT_hi_done, xT_lo_done = sem("xT_full"), sem("xT_hi_done"), sem("xT_lo_done")
        q_full, kv_full, qk_taken = sem("q_full"), sem("kv_full"), sem("qk_taken")
        v_taken, v_moved = sem("v_taken"), sem("v_moved")
        cos_done, sin_done, rope_done = sem("cos_done"), sem("sin_done"), sem("rope_done")
        qT_full, kT_full, qkT_hi_done, qkT_lo_done = sem("qT_full"), sem("kT_full"), sem("qkT_hi_done"), sem("qkT_lo_done")
        s_full, max_done, exp_done = sem("s_full"), sem("max_done"), sem("exp_done")
        recip_done, probs_scaled = sem("recip_done"), sem("probs_scaled")
        pT_full, pT_taken, pv_full = sem("pT_full"), sem("pT_taken"), sem("pv_full")
        y_hi_done, y_lo_done, wo_full = sem("y_hi_done"), sem("y_lo_done"), sem("wo_full")
        h2_done, h2_stored, xn2_stored = sem("h2_done"), sem("h2_stored"), sem("xn2_stored")
        xn2_T_full, xn2_T_taken = sem("xn2_T_full"), sem("xn2_T_taken")
        logits_full, logits_taken = sem("logits_full"), sem("logits_taken")

        dve_held, pool_held = sem("dve_held"), sem("pool_held")

        k_diag = k_rot[:].rearrange("p (g c) -> p g c", g=NG)[:, :, 0:HD]

        block = ctx.enter_context(nc.Block())

        @block.sync
        def _(sp):
            def load_h1(t):
                sp.wait_ge(xn1_done, t)
                sp.dma_start(h1, h1_dram[bass.ds(t * P, P), :]).then_inc(h1_in, 16)

            def load_residual(t):
                sp.wait_ge(resid_done, t)
                sp.dma_start(resid[:], h1_dram[bass.ds(t * P, P), :]).then_inc(resid_in, 16)

            def store_chunk(t):
                sp.wait_ge(chunk_lo_done, t + 1)
                for half, src in enumerate((chunk_hi, chunk_lo)):
                    sp.dma_start(halves_dram[half, bass.ds(t, 1)].rearrange("o p n -> (o p) n"), src.bitcast(F32)).then_inc(chunk_stored, 16)

            def load_chunk(t):
                sp.dma_start(chunk_raw, chunks[bass.ds(t, 1)].rearrange("o p n -> (o p) n")).then_inc(chunk_in, 16)

            def store_h2(t):
                sp.wait_ge(h2_done, t + 1)
                sp.dma_start(h2_dram[bass.ds(t * P, P), :], h2[:]).then_inc(h2_stored, 16)

            def store_xn2(t):
                sp.wait_ge(xn2_done, t + 1)
                sp.dma_start(xn_dram[bass.ds(t * P, P), 0:D], xn2[:]).then_inc(xn2_stored, 16)

            sp.dma_start(resid[:], h1_dram[0:P, :]).then_inc(resid_in, 16)
            load_h1(1)
            load_chunk(0)
            load_h1(2)
            store_chunk(0)
            load_chunk(1)
            load_h1(3)
            for dst, src in next_small:
                sp.dma_start(dst, src).then_inc(small_in, 16)

            def iteration(t, more_h1):
                if more_h1:
                    load_h1(t + 2)
                load_residual(t - 1)
                store_h2(t - 2)
                store_chunk(t - 1)
                load_chunk(t)
                store_xn2(t - 2)

            for a in range(2):
                sp.wait_ge(h1_stored[a], 16 * NPAIR)
            with sp.Fori(2, NTILE - 2) as t:
                iteration(t, True)
            iteration(NTILE - 2, False)
            iteration(NTILE - 1, False)
            load_residual(NTILE - 1)
            store_h2(NTILE - 2)
            store_chunk(NTILE - 1)
            store_xn2(NTILE - 2)
            store_h2(NTILE - 1)
            store_xn2(NTILE - 1)
            sp.wait_ge(h2_stored, 16 * NTILE)
            sp.wait_ge(xn2_stored, 16 * NTILE)
            sp.wait_ge(small_in, 16 * len(next_small))
            sp.wait_ge(chunk_stored, 2 * 16 * NTILE)

        @block.gpsimd
        def _(pool):
            pool.memset(k_rot[:], 0.0).then_inc(zeroed, 1)
            pool.memset(minus_half[:], -0.5).then_inc(zeroed, 1)
            pool.wait_ge(zeroed, 2)

            def rstd(t, mv, out, mv_done, eps_done, done):
                pool.wait_ge(mv_done, t + 1)
                pool.sem_inc(pool_held, 1)
                pool.tensor_scalar_add(out[:, 0:1], mv[:, 1:2], EPS).then_inc(eps_done, 1)
                pool.wait_ge(eps_done, t + 1)
                pool.tensor_tensor(out[:, 1:2], out[:, 0:1], minus_half[:], ALU.pow).then_inc(done, 1)

            def rotate(t):
                pool.wait_ge(qk_taken, t + 1)
                pool.tensor_tensor(rope_s[:, :, 0::2], qk[:, :, 1::2], sin_sb[:, 0::2].unsqueeze(1).to_broadcast([P, NH + NG, HD // 2]), ALU.mult)
                pool.tensor_tensor(rope_s[:, :, 1::2], qk[:, :, 0::2], sin_sb[:, 1::2].unsqueeze(1).to_broadcast([P, NH + NG, HD // 2]), ALU.mult).then_inc(sin_done, 1)

            def residual(t):
                pool.wait_ge(resid_in, 16 * (t + 1))
                if not isinstance(t, int) or t > 0:
                    pool.wait_ge(h2_done, t)
                pool.tensor_tensor(resid_b[:], resid[:], bo_sb[:], ALU.add).then_inc(resid_done, 1)

            def move_v(t):
                pool.wait_ge(v_taken, t + 1)
                if not isinstance(t, int) or t > 0:
                    pool.wait_ge(pv_full, t)
                pool.sem_inc(pool_held, 1)
                pool.tensor_copy(v[:], v_next[:]).then_inc(v_moved, 1)

            def chunk_low(t):
                pool.wait_ge(chunk_hi_done, t + 1)
                pool.tensor_tensor(chunk_lo, chunk_raw, chunk_hi.bitcast(F32), ALU.subtract).then_inc(chunk_lo_done, 1)

            def iteration(t, new, mid, late, next_norm):
                if next_norm:
                    rstd(t + 1, mv1, rstd1, mv1_done, eps1_done, rstd1_done)
                if late:
                    residual(t - 2)
                if new:
                    rotate(t)
                if mid:
                    chunk_low(t - 1)
                if late:
                    rstd(t - 2, mv2, rstd2, mv2_done, eps2_done, rstd2_done)
                if new:
                    move_v(t)

            rstd(0, mv1, rstd1, mv1_done, eps1_done, rstd1_done)
            iteration(0, True, False, False, True)
            iteration(1, True, True, False, True)
            iteration(2, True, True, True, True)
            with pool.Fori(3, NTILE - 1) as t:
                iteration(t, True, True, True, True)
            iteration(NTILE - 1, True, True, True, False)
            iteration(NTILE, False, True, True, False)
            iteration(NTILE + 1, False, False, True, False)

        @block.scalar
        def _(act):
            nc.scalar.copy(ident_16[:], ident[:])
            for g in range(NG):
                last = nc.scalar.copy(mask_16[:, g, :], mask_f[:])
            last.then_inc(consts_16, 1)
            nc.scalar.copy(wo_hi[:], wo_stage).then_inc(w_hi_done, 1)

            def xT_high(t):
                act.wait_ge(xT_full, t + 1)
                nc.scalar.copy(xT_hi[:].rearrange("p k t -> p (k t)"), bank[4][:]).then_inc(xT_hi_done, 1)

            def qkT_high(t):
                act.wait_ge(qT_full, t + 1)
                nc.scalar.activation(qT_hi[:].rearrange("p j t -> p (j t)"), bank[7][:], ACT.Copy, scale=SCALE).then_inc(qkT_hi_done, 1)
                act.wait_ge(kT_full, t + 1)
                nc.scalar.copy(kT_hi[:], bank[6][:]).then_inc(qkT_hi_done, 1)

            def exps(t):
                for j in range(4):
                    act.wait_ge(max_done, 4 * t + j + 1)
                    for g in range(NG):
                        h = 4 * j + g
                        last = nc.scalar.activation(probs[:, j, g, :], bank[j][:, g * P:(g + 1) * P], ACT.Exp,
                                                    bias=neg_max[:, h:h + 1], accum_out=sums[:, h:h + 1])
                    last.then_inc(exp_done, 1)

            def take_probs_T(t):
                for j in range(4):
                    act.wait_ge(pT_full, 4 * t + j + 1)
                    nc.scalar.copy(probs_T[:, :, j, :], bank[j][:].rearrange("p (g q) -> p g q", g=NG)).then_inc(pT_taken, 1)

            def y_high(t):
                act.wait_ge(pv_full, t + 1)
                nc.scalar.copy(y_hi[:].rearrange("p j t -> p (j t)"), bank[5][:]).then_inc(y_hi_done, 1)

            def take_xn2_T(t):
                act.wait_ge(xn2_T_full, t + 1)
                nc.scalar.copy(xn2_T[:].rearrange("p k t -> p (k t)"), bank[7][:]).then_inc(xn2_T_taken, 1)

            def chunk_high(t):
                act.wait_ge(chunk_in, 16 * (t + 1))
                if not isinstance(t, int) or t > 0:
                    act.wait_ge(chunk_stored, 2 * 16 * t)
                nc.scalar.copy(chunk_hi, chunk_raw).then_inc(chunk_hi_done, 1)

            def iteration(t, new, mid, routed, next_norm):
                if routed:
                    take_xn2_T(t - 3)
                if mid:
                    take_probs_T(t - 1)
                if new:
                    qkT_high(t)
                if mid:
                    y_high(t - 1)
                if next_norm:
                    xT_high(t + 1)
                if new:
                    exps(t)
                    chunk_high(t)

            xT_high(0)
            iteration(0, True, False, False, True)
            iteration(1, True, True, False, True)
            iteration(2, True, True, False, True)
            with act.Fori(3, NTILE - 1) as t:
                iteration(t, True, True, True, True)
            iteration(NTILE - 1, True, True, True, False)
            iteration(NTILE, False, True, True, False)
            iteration(NTILE + 1, False, False, True, False)
            iteration(NTILE + 2, False, False, True, False)

        @block.vector
        def _(dve):
            dve.wait_ge(zeroed, 2)

            def norm_stats(t, src, stats, mv, stats_done, mv_done):
                nc.vector.bn_stats(stats[:], src).then_inc(stats_done, 1)
                dve.wait_ge(stats_done, t + 1)
                dve.sem_inc(dve_held, 1)
                nc.vector.bn_aggr(mv[:], stats[:]).then_inc(mv_done, 1)

            def norm(t, out, src, mv, rstd, rstd_done, done):
                dve.wait_ge(rstd_done, t + 1)
                nc.vector.tensor_scalar(out[:], src, mv[:, 0:1], rstd[:, 1:2], ALU.subtract, ALU.mult).then_inc(done, 1)

            def stats_of_h1(t):
                if not isinstance(t, int) or t > 0:
                    dve.wait_ge(h1_in, 16 * t)
                norm_stats(t, h1, stats1, mv1, stats1_done, mv1_done)

            def norm_h1(t):
                norm(t, xn1, h1, mv1, rstd1, rstd1_done, xn1_done)

            def xT_low(t):
                dve.wait_ge(xT_hi_done, t + 1)
                nc.vector.tensor_tensor(xT_lo[:].rearrange("p k t -> p (k t)"), bank[4][:],
                                        xT_hi[:].rearrange("p k t -> p (k t)").bitcast(F32), ALU.subtract).then_inc(xT_lo_done, 1)

            def take_q(t):
                dve.wait_ge(q_full, t + 1)
                nc.vector.tensor_tensor(qk[:, 0:NH, :].rearrange("p h d -> p (h d)"), bank[4][:], bq_sb[:], ALU.add)

            def take_kv(t):
                dve.wait_ge(kv_full, t + 1)
                nc.vector.tensor_tensor(qk[:, NH:, :].rearrange("p h d -> p (h d)"), bank[5][:, 0:P], bkv_sb[:, 0:P], ALU.add).then_inc(qk_taken, 1)
                dve.wait_ge(qk_taken, t + 1)
                nc.vector.tensor_tensor(rope_c[:], qk[:], cos_sb[:].unsqueeze(1).to_broadcast([P, NH + NG, HD]), ALU.mult).then_inc(cos_done, 1)
                if not isinstance(t, int) or t > 0:
                    dve.wait_ge(v_moved, t)
                nc.vector.tensor_tensor(v_next[:], bank[5][:, P:2 * P], bkv_sb[:, P:2 * P], ALU.add).then_inc(v_taken, 1)

            def rope(t):
                dve.wait_ge(cos_done, t + 1)
                dve.wait_ge(sin_done, t + 1)
                nc.vector.tensor_tensor(q_rot[:].rearrange("p j g d -> p g j d"), rope_c[:, 0:NH, :].rearrange("p (g j) d -> p g j d", g=NG),
                                        rope_s[:, 0:NH, :].rearrange("p (g j) d -> p g j d", g=NG), ALU.add)
                nc.vector.tensor_tensor(k_diag, rope_c[:, NH:, :], rope_s[:, NH:, :], ALU.add).then_inc(rope_done, 1)

            def qT_low(t):
                dve.wait_ge(qkT_hi_done, 2 * t + 1)
                nc.vector.scalar_tensor_tensor(qT_lo[:].rearrange("p j t -> p (j t)"), bank[7][:], SCALE,
                                               qT_hi[:].rearrange("p j t -> p (j t)").bitcast(F32), ALU.mult, ALU.subtract).then_inc(qkT_lo_done, 1)

            def kT_low(t):
                dve.wait_ge(qkT_hi_done, 2 * t + 2)
                nc.vector.tensor_tensor(kT_lo[:], bank[6][:], kT_hi[:].bitcast(F32), ALU.subtract).then_inc(qkT_lo_done, 1)

            def maxima(t, js):
                for j in js:
                    dve.wait_ge(s_full, 4 * t + j + 1)
                    nc.vector.tensor_reduce(neg_max[:, 4 * j:4 * j + 4], bank[j][:].rearrange("p (g k) -> p g k", g=NG),
                                            AX.X, ALU.max, negate=True).then_inc(max_done, 1)

            def scale_probs(t, js):
                for j in js:
                    hs = slice(4 * j, 4 * j + 4)
                    dve.wait_ge(exp_done, 4 * t + j + 1)
                    nc.vector.reciprocal(recip[:, hs], sums[:, hs]).then_inc(recip_done, 1)
                    dve.wait_ge(recip_done, 4 * t + j + 1)
                    nc.vector.tensor_tensor(probs[:, j], probs[:, j], recip[:, hs].unsqueeze(2).to_broadcast([P, NG, P]),
                                            ALU.mult).then_inc(probs_scaled, 1)

            def y_low(t):
                dve.wait_ge(y_hi_done, t + 1)
                nc.vector.tensor_tensor(y_lo[:].rearrange("p j t -> p (j t)"), bank[5][:],
                                        y_hi[:].rearrange("p j t -> p (j t)").bitcast(F32), ALU.subtract).then_inc(y_lo_done, 1)

            def residual_sum(t):
                dve.wait_ge(wo_full, t + 1)
                dve.wait_ge(resid_done, t + 1)
                if not isinstance(t, int) or t > 0:
                    dve.wait_ge(h2_stored, 16 * t)
                nc.vector.tensor_tensor(h2[:], bank[6][:], resid_b[:], ALU.add).then_inc(h2_done, 1)

            def stats_of_h2(t):
                dve.wait_ge(h2_done, t + 1)
                norm_stats(t, h2[:], stats2, mv2, stats2_done, mv2_done)

            def norm_h2(t):
                if not isinstance(t, int) or t > 0:
                    dve.wait_ge(xn2_stored, 16 * t)
                norm(t, xn2, h2[:], mv2, rstd2, rstd2_done, xn2_done)

            def take_logits(t):
                dve.wait_ge(logits_full, t + 1)
                nc.vector.tensor_copy(logits_T[0:NE, bass.ds(t * P, P)], bank[4][0:NE, 0:P]).then_inc(logits_taken, 1)

            def iteration(t, new, mid, late, routed, next_norm):
                if mid:
                    scale_probs(t - 1, (0,))
                if next_norm:
                    stats_of_h1(t + 1)
                if mid:
                    scale_probs(t - 1, (1,))
                if new:
                    take_q(t)
                if mid:
                    scale_probs(t - 1, (2,))
                if new:
                    take_kv(t)
                if next_norm:
                    norm_h1(t + 1)
                if mid:
                    scale_probs(t - 1, (3,))
                if new:
                    rope(t)
                if late:
                    residual_sum(t - 2)
                if late:
                    stats_of_h2(t - 2)
                if new:
                    qT_low(t)
                if routed:
                    take_logits(t - 3)
                if new:
                    kT_low(t)
                if mid:
                    y_low(t - 1)
                if new:
                    maxima(t, (0,))
                if next_norm:
                    xT_low(t + 1)
                if new:
                    maxima(t, (1, 2))
                if late:
                    norm_h2(t - 2)
                if new:
                    maxima(t, (3,))

            stats_of_h1(0)
            norm_h1(0)
            xT_low(0)
            dve.wait_ge(w_hi_done, 1)
            nc.vector.tensor_tensor(wo_lo[:], wo_stage, wo_hi[:].bitcast(F32), ALU.subtract).then_inc(w_split, 1)
            iteration(0, True, False, False, False, True)
            iteration(1, True, True, False, False, True)
            iteration(2, True, True, True, False, True)
            iteration(3, True, True, True, True, True)
            with dve.Fori(4, NTILE - 1) as t:
                iteration(t, True, True, True, True, True)
            iteration(NTILE - 1, True, True, True, True, False)
            iteration(NTILE, False, True, True, True, False)
            iteration(NTILE + 1, False, False, True, True, False)
            iteration(NTILE + 2, False, False, False, True, False)

        @block.tensor
        def _(pe):
            pe.wait_ge(consts_16, 1)

            def three_products(dst, parts):
                n, count = 0, 3 * len(parts)
                for a_hi, a_lo, b_hi, b_lo in parts:
                    for a, b in ((a_hi, b_hi), (a_hi, b_lo), (a_lo, b_hi)):
                        last = nc.tensor.matmul(dst, a, b, start=n == 0, stop=n == count - 1)
                        n += 1
                return last

            def transpose_x(t):
                pe.wait_ge(xn1_done, t + 1)
                if not isinstance(t, int) or t > 3:
                    pe.wait_ge(logits_taken, t - 3)
                elif t > 0:
                    pe.wait_ge(qk_taken, t)
                for kt in range(KT):
                    last = nc.tensor.transpose(bank[4][:, kt * P:(kt + 1) * P], xn1[:, kt * P:(kt + 1) * P], ident[:])
                last.then_inc(xT_full, 1)

            def project(t):
                pe.wait_ge(xT_lo_done, t + 1)
                three_products(bank[4][:], [(xT_hi[:, k], xT_lo[:, k], wq_hi[:, k], wq_lo[:, k]) for k in range(KT)]).then_inc(q_full, 1)
                if not isinstance(t, int) or t > 1:
                    pe.wait_ge(y_lo_done, t - 1)
                elif t == 1:
                    pe.wait_ge(v_taken, 1)
                three_products(bank[5][:, 0:PAIR], [(xT_hi[:, k], xT_lo[:, k], wkv_hi[:, k], wkv_lo[:, k]) for k in range(KT)]).then_inc(kv_full, 1)

            def transpose_qk(t):
                pe.wait_ge(rope_done, t + 1)
                if not isinstance(t, int) or t > 2:
                    pe.wait_ge(xn2_T_taken, t - 2)
                for j in range(4):
                    last = nc.tensor.transpose(bank[7][:, j * P:(j + 1) * P], q_rot[:, j].rearrange("p g d -> p (g d)"), ident[:])
                last.then_inc(qT_full, 1)
                if not isinstance(t, int) or t > 1:
                    pe.wait_ge(h2_done, t - 1)
                for g in range(NG):
                    last = nc.tensor.transpose(bank[6][:, g * P:(g + 1) * P], k_rot[:, g * P:(g + 1) * P], ident[:])
                last.then_inc(kT_full, 1)

            def scores(t):
                pe.wait_ge(qkT_lo_done, 2 * (t + 1))
                for j in range(4):
                    if not isinstance(t, int) or t > 0:
                        pe.wait_ge(pT_taken, 4 * (t - 1) + j + 1)
                    nc.tensor.matmul(bank[j][:], ident_16[:], mask_16[:].rearrange("p g k -> p (g k)"), start=True, stop=False)
                    for n, (q, k) in enumerate(((qT_hi, kT_hi), (qT_hi, kT_lo), (qT_lo, kT_hi))):
                        last = nc.tensor.matmul(bank[j][:], q[:, j], k[:], start=False, stop=n == 2)
                    last.then_inc(s_full, 1)

            def transpose_probs(t):
                for j in range(4):
                    pe.wait_ge(probs_scaled, 4 * t + j + 1)
                    for g in range(NG):
                        last = nc.tensor.transpose(bank[j][:, g * P:(g + 1) * P], probs[:, j, g], ident[:])
                    last.then_inc(pT_full, 1)

            def weigh_values(t):
                pe.wait_ge(pT_taken, 4 * (t + 1))
                pe.wait_ge(v_moved, t + 1)
                if t != NTILE - 1 if isinstance(t, int) else True:
                    pe.wait_ge(v_taken, t + 2)
                else:
                    pe.wait_ge(y_lo_done, t)
                for g in range(NG):
                    last = nc.tensor.matmul(bank[5][g * HD:(g + 1) * HD, :], v[:, g * HD:(g + 1) * HD],
                                            probs_T[:, g].rearrange("p j q -> p (j q)"), start=True, stop=True)
                last.then_inc(pv_full, 1)

            def project_out(t):
                pe.wait_ge(w_split, 1)
                pe.wait_ge(y_lo_done, t + 1)
                if isinstance(t, int) and t == NTILE - 1:
                    pe.wait_ge(h2_done, t)
                three_products(bank[6][:], [(y_hi[:, j], y_lo[:, j], wo_hi[:, j], wo_lo[:, j]) for j in range(4)]).then_inc(wo_full, 1)

            def transpose_xn2(t):
                pe.wait_ge(xn2_done, t + 1)
                if isinstance(t, int) and t > NTILE - 3:
                    pe.wait_ge(xn2_T_taken, t)
                for kt in range(KT):
                    last = nc.tensor.transpose(bank[7][:, kt * P:(kt + 1) * P], xn2[:, kt * P:(kt + 1) * P], ident[:])
                last.then_inc(xn2_T_full, 1)

            def route(t, new):
                pe.wait_ge(xn2_T_taken, t + 1)
                if new:
                    pe.wait_ge(qk_taken, t + 4)
                else:
                    pe.wait_ge(logits_taken, t)
                for kt in range(KT):
                    last = nc.tensor.matmul(bank[4][0:NE, 0:P], router_sb[:, kt], xn2_T[:, kt], start=kt == 0, stop=kt == KT - 1)
                last.then_inc(logits_full, 1)

            def iteration(t, new, mid, late, routed, next_norm):
                if new:
                    project(t)
                if routed:
                    transpose_xn2(t - 3)
                if late:
                    project_out(t - 2)
                if mid:
                    transpose_probs(t - 1)
                if new:
                    transpose_qk(t)
                if routed:
                    route(t - 3, new)
                if mid:
                    weigh_values(t - 1)
                if next_norm:
                    transpose_x(t + 1)
                if new:
                    scores(t)

            transpose_x(0)
            iteration(0, True, False, False, False, True)
            iteration(1, True, True, False, False, True)
            iteration(2, True, True, True, False, True)
            iteration(3, True, True, True, True, True)
            with pe.Fori(4, NTILE - 1) as t:
                iteration(t, True, True, True, True, True)
            iteration(NTILE - 1, True, True, True, True, False)
            iteration(NTILE, False, True, True, True, False)
            iteration(NTILE + 1, False, False, True, True, False)
            iteration(NTILE + 2, False, False, False, True, False)


def routed_experts(nc, logits_T, halves_dram, halves, w3, small, xn_dram, out_dram):
    ctx = ExitStack()
    with ctx:
        sb = lambda name, shape, dt=F32: ctx.enter_context(nc.sbuf_tensor("d_" + name, shape, dt, side="right"))
        rb = lambda name, shape, dt=F32: ctx.enter_context(nc.sbuf_tensor("c_" + name, shape, dt))
        sem = lambda name: ctx.enter_context(nc.semaphore("d_" + name))
        bank = [ctx.enter_context(nc.psum_tensor(f"d_bank{i}", [P, 512], F32)) for i in range(8)]

        ident, before, expert_m8, expert_low, rows_full, part_1, part_pad, assign_ik, col = (small[n] for n in NEXT_TABLES)
        before_16, ones = rb("before_16", [P, P], BF16), rb("ones", [P, P], BF16)
        zero = sb("zero", [P, D])

        TE = [P, NTILE, NE]
        top = [rb(f"top{k}", [P, NTILE]) for k in range(2)]
        hit, hit_m8 = rb("hit", TE), rb("hit_m8", TE)
        choice = rb("choice", [P, NTILE])
        onehot = rb("onehot", [P, NTILE, 2, NE])
        rest = rb("rest", TE)
        gap, exp_gap, denom = rb("gap", [P, NTILE]), rb("exp_gap", [P, NTILE]), rb("denom", [P, NTILE])
        weights = sb("weights", [P, NTILE, 2])
        chosen = rb("chosen", [P, NTILE + 1, NE], BF16)
        slot_e, pick = rb("slot_e", TE), rb("pick", [P, NTILE, 2, NE])
        over = rb("over", [P, NE, NTILE])
        nblk, first, last_b = rb("nblk", [P, NE]), rb("first", [P, NE]), rb("last_b", [P, NE])
        prod = rb("prod", [P, NE, NE])
        slot_f = rb("slot_f", [P, NTILE, 2])
        slot_i, blk_i, row_i = (rb(n, [P, 2 * NTILE], I32) for n in ("slot_i", "blk_i", "row_i"))
        blk_f, row_f = rb("blk_f", [P, 2 * NTILE]), rb("row_f", [P, 2 * NTILE])
        in_row = logits_T[:].bitcast(BF16).rearrange("p (a r) -> p a r", r=P)
        in_blk = rb("in_blk", [P, 2 * NTILE, NBLOCK], BF16)
        marks = rb("marks", [P, 2 * NTILE, 2, NBLOCK], BF16)
        listed = rb("listed", [P, 2, NBLOCK])
        tile_i, tile_f = rb("tile_i", [P, NBLOCK], I32), rb("tile_f", [P, NBLOCK])
        unused, token = rb("unused", [P, NBLOCK]), rb("token", [P, NBLOCK])
        index_f = rb("index_f", [P, 2, NBLOCK])
        index = sb("index", [P, 2, NBLOCK], U32)
        which = sb("which", [P, NBLOCK, 2])
        done_cmp, expert_f = rb("done_cmp", [1, NBLOCK, NE]), rb("expert_f", [1, NBLOCK])
        expert = sb("expert", [1, NBLOCK], U32)

        idx_in = [sb(f"idx_in{i}", [P, 1], U32) for i in range(4)]
        idx_out = [sb(f"idx_out{i}", [P, 1], U32) for i in range(2)]
        xg = [sb(f"xg{i}", [P, XROW]) for i in range(4)]
        wsel = [sb(f"wsel{i}", [P, 2]) for i in range(2)]
        wg = [sb(f"wg{i}", [P, 1]) for i in range(2)]
        xg_T_hi, xg_T_lo = sb("xg_T_hi", [P, KT, P], F32R), sb("xg_T_lo", [P, KT, P], F32R)
        gate = [sb(f"gate{i}", [P, PAIR]) for i in range(2)]
        hidden = [sb(f"hidden{i}", [P, PAIR]) for i in range(2)]
        hidden_T = sb("hidden_T", [P, 2, P])
        y = [sb(f"y{i}", [P, D]) for i in range(2)]

        halves_in, experts_loaded = [sem(f"halves_in{e}") for e in range(NE)], sem("experts_loaded")
        zeroed, pad_rows = sem("zeroed"), sem("pad_rows")
        logits_full = sem("logits_full")
        route = sem("route")
        gap_ready, exp_gap_done = sem("gap_ready"), sem("exp_gap_done")
        chosen_ready, ranked = sem("chosen_ready"), sem("ranked")
        weights_ready, weights_out = sem("weights_ready"), sem("weights_out")
        marks_ready, list_full, routed = sem("marks_ready"), sem("list_full"), sem("routed")
        experts_known, parts_marked = sem("experts_known"), sem("parts_marked")
        ones_ready, blocks_marked, tiles_marked = sem("ones_ready"), sem("blocks_marked"), sem("tiles_marked")
        pool_held = sem("pool_held")
        idx_in_done, idx_out_done = sem("idx_in_done"), sem("idx_out_done")
        xg_in = [sem(f"xg_in{i}") for i in range(4)]
        wsel_done, wg_done = sem("wsel_done"), sem("wg_done")
        xg_T_full, xg_T_hi_done, xg_T_taken = sem("xg_T_full"), sem("xg_T_hi_done"), sem("xg_T_taken")
        up_full, gate_done, hidden_done = sem("up_full"), sem("gate_done"), sem("hidden_done")
        hidden_T_full, hidden_T_taken = sem("hidden_T_full"), sem("hidden_T_taken")
        down_full, y_done, added = sem("down_full"), sem("y_done"), sem("added")

        halves_flat = halves.rearrange("p s h n -> p (s h n)")
        A = 2 * NTILE
        CHUNKS = 4
        part = lambda c: slice(c * (A // CHUNKS), (c + 1) * (A // CHUNKS))

        block = ctx.enter_context(nc.Block())

        @block.sync
        def _(sp):
            sp.wait_ge(zeroed, 1)
            sp.dma_start(out_dram[T:T + P, :], zero[:]).then_inc(pad_rows, 16)
            sp.wait_ge(weights_ready, 1)
            sp.dma_start(xn_dram.rearrange("(i p) n -> p i n", p=P)[:, :, D:XROW], weights[:]).then_inc(weights_out, 16)
            for e in range(NE):
                sp.wait_ge(halves_in[e], 2 * 16)
                sp.sem_inc(experts_loaded, 1)

        @block.scalar
        def _(act):
            act.wait_ge(gap_ready, 1)
            nc.scalar.activation(exp_gap[:], gap[:], ACT.Exp).then_inc(exp_gap_done, 1)

            act.wait_ge(blocks_marked, 1)
            for c in range(CHUNKS):
                nc.scalar.activation(marks[:, part(c), 0], in_blk[:, part(c)], ACT.Copy, scale=part_1[:]).then_inc(parts_marked, 1)

            def take_x(b):
                act.wait_ge(xg_T_full, b + 1)
                nc.scalar.copy(xg_T_hi[:].rearrange("p k t -> p (k t)"), bank[0][:]).then_inc(xg_T_hi_done, 1)

            def gate_of(b, par):
                act.wait_ge(up_full, b + 1)
                nc.scalar.activation(gate[par][:], bank[2 + par][:, 0:PAIR], ACT.Silu).then_inc(gate_done, 1)

            def take_hidden(b):
                act.wait_ge(hidden_T_full, b + 1)
                nc.scalar.copy(hidden_T[:].rearrange("p k t -> p (k t)"), bank[4][:, 0:PAIR]).then_inc(hidden_T_taken, 1)

            def iteration(b, par, up, down, nxt):
                if down:
                    take_hidden(b - 1)
                if up:
                    gate_of(b, par)
                if nxt:
                    take_x(b + 1)

            take_x(0)
            iteration(0, 0, True, False, True)
            with act.Fori(0, NBLOCK // 2 - 1) as u:
                b = 2 * u + 1
                iteration(b, 1, True, True, True)
                iteration(b + 1, 0, True, True, True)
            iteration(NBLOCK - 1, 1, True, True, False)
            iteration(NBLOCK, 0, False, True, False)

        @block.gpsimd
        def _(pool):
            def load_halves(e):
                for half in range(2):
                    pool.dma_start(halves[:, e, half].rearrange("p (k n) -> p k n", k=KT),
                                   halves_dram[half, e * KT:(e + 1) * KT].rearrange("k p n -> p k n")).then_inc(halves_in[e], 16)

            pool.memset(zero[:], 0.0).then_inc(zeroed, 1)
            pool.memset(ones[:], 1.0).then_inc(ones_ready, 1)
            pool.memset(chosen[:, NTILE], 0.0).then_inc(ones_ready, 1)
            pool.tensor_copy(before_16[:], before[:]).then_inc(ones_ready, 1)
            for e in EARLY:
                load_halves(e)
            pool.wait_ge(blocks_marked, 1)
            for c in range(CHUNKS):
                pool.tensor_tensor(marks[:, part(c), 1], in_blk[:, part(c)], assign_ik[:, part(c)].unsqueeze(2).to_broadcast([P, A // CHUNKS, NBLOCK]), ALU.mult).then_inc(tiles_marked, 1)
            pool.wait_ge(routed, 1)
            pool.wait_ge(weights_out, 16)
            pool.wait_ge(pad_rows, 16)

            def gather(b, slot):
                pool.tensor_copy(idx_in[slot][:], index[:, 0, bass.ds(b, 1)]).then_inc(idx_in_done, 1)
                pool.wait_ge(idx_in_done, b + 1)
                pool.sem_inc(pool_held, 1)
                pool.indirect_dma_start(xg[slot][:], None, xn_dram, bass.IndirectOffsetOnAxis(idx_in[slot][:, 0:1], 0)).then_inc(xg_in[slot], 16)

            def scatter(b, par):
                pool.tensor_copy(idx_out[par][:], index[:, 1, bass.ds(b, 1)]).then_inc(idx_out_done, 1)
                pool.wait_ge(idx_out_done, b + 1)
                pool.wait_ge(y_done, b + 1)
                if not isinstance(b, int) or b > 0:
                    pool.wait_ge(added, 16 * b)
                pool.sem_inc(pool_held, 1)
                pool.indirect_dma_start(out_dram, bass.IndirectOffsetOnAxis(idx_out[par][:, 0:1], 0), y[par][:], None,
                                        compute_op=ALU.add).then_inc(added, 16)

            for b in range(4):
                gather(b, b)
            pool.wait_ge(experts_known, 1)
            for e in sorted(set(range(NE)) - set(EARLY)):
                load_halves(e)

            def four(u, more):
                for k in range(4):
                    scatter(4 * u + k, k % 2)
                    if more:
                        gather(4 * u + k + 4, k)

            four(0, True)
            with pool.Fori(1, NBLOCK // 4 - 1) as u:
                four(u, True)
            four(NBLOCK // 4 - 1, False)
            pool.wait_ge(added, 16 * NBLOCK)

        @block.vector
        def _(dve):
            steps = [0]

            def step(instruction):
                steps[0] += 1
                instruction.then_inc(route, 1)
                dve.wait_ge(route, steps[0])

            V = nc.vector
            over_e = lambda t: t[:].unsqueeze(2).to_broadcast(TE)
            over_i = lambda t: t[:].unsqueeze(1).to_broadcast(TE)
            flat = lambda t: t[:].rearrange("p i e -> p (i e)")
            scores = bank[1][:, 0:NTILE * NE].rearrange("p (i e) -> p i e", e=NE)
            dve.wait_ge(logits_full, 1)

            for k, src in enumerate((scores, rest[:])):
                step(V.tensor_reduce(top[k][:], src, AX.X, ALU.max))
                step(V.tensor_tensor(hit[:], src, over_e(top[k]), ALU.is_ge))
                step(V.tensor_tensor(hit_m8[:], hit[:], over_i(expert_m8), ALU.mult))
                step(V.tensor_reduce(choice[:], hit_m8[:], AX.X, ALU.min))
                step(V.tensor_tensor(onehot[:, :, k], over_i(expert_m8), over_e(choice), ALU.is_equal))
                if k == 0:
                    step(V.scalar_tensor_tensor(rest[:], onehot[:, :, 0], -3e38, scores, ALU.mult, ALU.add))
            V.tensor_tensor(gap[:], top[1][:], top[0][:], ALU.subtract).then_inc(gap_ready, 1)
            V.tensor_tensor(chosen[:, 0:NTILE], onehot[:, :, 0], onehot[:, :, 1], ALU.add).then_inc(chosen_ready, 1)

            dve.wait_ge(exp_gap_done, 1)
            step(V.tensor_scalar(denom[:], exp_gap[:], 1.0, None, ALU.add))
            step(V.reciprocal(weights[:, :, 0], denom[:]))
            V.tensor_tensor(weights[:, :, 1], weights[:, :, 0], exp_gap[:], ALU.mult).then_inc(weights_ready, 1)

            dve.wait_ge(ranked, 1)
            ranks = bank[0][:, 0:(NTILE + 1) * NE].rearrange("p (i e) -> p i e", e=NE)
            step(V.tensor_tensor(over[:], ranks[:, NTILE].unsqueeze(2).to_broadcast([P, NE, NTILE]), rows_full[:].unsqueeze(1).to_broadcast([P, NE, NTILE]), ALU.is_gt))
            step(V.tensor_reduce(nblk[:], over[:], AX.X, ALU.add))
            step(V.tensor_tensor(prod[:], expert_low[:], nblk[:].unsqueeze(1).to_broadcast([P, NE, NE]), ALU.mult))
            step(V.tensor_reduce(first[:], prod[:], AX.X, ALU.add))
            step(V.tensor_tensor(last_b[:], first[:], nblk[:], ALU.add))
            step(V.scalar_tensor_tensor(slot_e[:], over_i(first), float(P), ranks[:, 0:NTILE], ALU.mult, ALU.add))
            step(V.tensor_tensor(pick[:], onehot[:], slot_e[:].unsqueeze(2).to_broadcast([P, NTILE, 2, NE]), ALU.mult))
            step(V.tensor_reduce(slot_f[:], pick[:], AX.X, ALU.add))
            step(V.tensor_copy(slot_i[:], slot_f[:].rearrange("p i k -> p (i k)")))
            V.tensor_scalar(blk_i[:], slot_i[:], 7, None, ALU.arith_shift_right)
            step(V.tensor_scalar(row_i[:], slot_i[:], P - 1, None, ALU.bitwise_and))
            V.tensor_copy(blk_f[:], blk_i[:])
            step(V.tensor_copy(row_f[:], row_i[:]))
            V.tensor_tensor(in_blk[:], blk_f[:].unsqueeze(2).to_broadcast([P, A, NBLOCK]), col[:, 0:NBLOCK].unsqueeze(1).to_broadcast([P, A, NBLOCK]), ALU.is_equal).then_inc(blocks_marked, 1)
            for c in range(CHUNKS):
                V.tensor_tensor(in_row[:, part(c)], row_f[:, part(c)].unsqueeze(2).to_broadcast([P, A // CHUNKS, P]),
                                col[:].unsqueeze(1).to_broadcast([P, A // CHUNKS, P]), ALU.is_equal).then_inc(marks_ready, 1)

            dve.wait_ge(list_full, 1)
            step(V.tensor_copy(listed[:].rearrange("p a b -> p (a b)"), bank[5][:, 0:2 * NBLOCK]))
            step(V.tensor_copy(tile_i[:], listed[:, 1]))
            step(V.tensor_scalar(tile_i[:], tile_i[:], 1, None, ALU.arith_shift_right))
            step(V.tensor_copy(tile_f[:], tile_i[:]))
            step(V.scalar_tensor_tensor(token[:], tile_f[:], float(P), listed[:, 0], ALU.mult, ALU.add))
            step(V.tensor_scalar(token[:], token[:], -1.0, None, ALU.add))
            V.tensor_scalar(index_f[:, 0], token[:], 0.0, None, ALU.max)
            step(V.scalar_tensor_tensor(which[:, :, 1], tile_f[:], -2.0, listed[:, 1], ALU.mult, ALU.add))
            V.tensor_scalar(which[:, :, 0], which[:, :, 1], -1.0, 1.0, ALU.mult, ALU.add)
            step(V.tensor_scalar(unused[:], listed[:, 0], 0.0, None, ALU.is_equal))
            step(V.scalar_tensor_tensor(index_f[:, 1], unused[:], part_pad[:], token[:], ALU.mult, ALU.add))
            V.tensor_copy(index[:], index_f[:]).then_inc(routed, 1)

            step(V.tensor_tensor(done_cmp[:], last_b[0:1, :].unsqueeze(1).to_broadcast([1, NBLOCK, NE]), col[0:1, 0:NBLOCK].unsqueeze(2).to_broadcast([1, NBLOCK, NE]), ALU.is_le))
            step(V.tensor_reduce(expert_f[:], done_cmp[:], AX.X, ALU.add))
            step(V.tensor_scalar(expert_f[:], expert_f[:], float(NE - 1), None, ALU.min))
            V.tensor_copy(expert[:], expert_f[:]).then_inc(experts_known, 1)

            def x_low(b):
                dve.wait_ge(xg_T_hi_done, b + 1)
                V.tensor_tensor(xg_T_lo[:].rearrange("p k t -> p (k t)"), bank[0][:], xg_T_hi[:].rearrange("p k t -> p (k t)").bitcast(F32), ALU.subtract).then_inc(xg_T_taken, 1)

            def hidden_of(b, par):
                dve.wait_ge(gate_done, b + 1)
                V.tensor_tensor(hidden[par][:], gate[par][:], bank[2 + par][:, PAIR:2 * PAIR], ALU.mult).then_inc(hidden_done, 1)

            def weigh(b, par, slot):
                dve.wait_ge(xg_in[slot], 4 * (b - slot) + 16)
                V.tensor_tensor(wsel[par][:], xg[slot][:, D:XROW], which[:, bass.ds(b, 1), :].rearrange("p b k -> p (b k)"), ALU.mult).then_inc(wsel_done, 1)
                dve.wait_ge(wsel_done, b + 1)
                V.tensor_reduce(wg[par][:], wsel[par][:], AX.X, ALU.add).then_inc(wg_done, 1)
                dve.wait_ge(wg_done, b + 1)
                dve.wait_ge(down_full, b + 1)
                if not isinstance(b, int) or b > 1:
                    dve.wait_ge(added, 16 * (b - 1))
                V.tensor_scalar(y[par][:], bank[6 + par][:], wg[par][:], None, ALU.mult).then_inc(y_done, 1)

            def iteration(b, k, up, down, nxt):
                if up:
                    hidden_of(b, k % 2)
                if nxt:
                    x_low(b + 1)
                if down:
                    weigh(b - 1, (k + 1) % 2, (k + 3) % 4)

            x_low(0)
            for b in range(4):
                iteration(b, b, True, b > 0, True)
            with dve.Fori(1, NBLOCK // 4 - 1) as u:
                for k in range(4):
                    iteration(4 * u + k, k, True, True, True)
            for b in range(NBLOCK - 4, NBLOCK):
                iteration(b, b % 4, True, True, b < NBLOCK - 1)
            iteration(NBLOCK, 0, False, True, False)

        @block.tensor
        def _(pe):
            for i in range(NTILE):
                last = nc.tensor.transpose(bank[1][:, i * NE:(i + 1) * NE], logits_T[0:NE, i * P:(i + 1) * P], ident[0:NE, 0:NE])
            last.then_inc(logits_full, 1)
            pe.wait_ge(ones_ready, 3)
            pe.wait_ge(chosen_ready, 1)
            nc.tensor.matmul(bank[0][:, 0:(NTILE + 1) * NE], before_16[:], chosen[:].rearrange("p i e -> p (i e)"), start=True, stop=False)
            for i in range(NTILE):
                last = nc.tensor.matmul(bank[0][:, (i + 1) * NE:(NTILE + 1) * NE], ones[:], chosen[:, i].unsqueeze(1).to_broadcast([P, NTILE - i, NE]),
                                        start=False, stop=i == NTILE - 1)
            last.then_inc(ranked, 1)
            for c in range(CHUNKS):
                pe.wait_ge(marks_ready, c + 1)
                pe.wait_ge(tiles_marked, c + 1)
                pe.wait_ge(parts_marked, c + 1)
                for a in range(*part(c).indices(A)):
                    last = nc.tensor.matmul(bank[5][:, 0:2 * NBLOCK], in_row[:, a], marks[:, a].rearrange("p c b -> p (c b)"), start=a == 0, stop=a == A - 1)
            last.then_inc(list_full, 1)
            pe.wait_ge(routed, 1)
            pe.wait_ge(experts_known, 1)

            def transpose_x(b, slot):
                pe.wait_ge(xg_in[slot], 4 * (b - slot) + 16)
                if not isinstance(b, int) or b > 0:
                    pe.wait_ge(xg_T_taken, b)
                for kt in range(KT):
                    last = nc.tensor.transpose(bank[0][:, kt * P:(kt + 1) * P], xg[slot][:, kt * P:(kt + 1) * P], ident[:])
                last.then_inc(xg_T_full, 1)

            def expert_of(b):
                return pe.value_load(expert[0:1, bass.ds(b, 1)], min_val=0, max_val=NE - 1)

            def up(b, par, e):
                pe.wait_ge(experts_loaded, e + 1)
                pe.wait_ge(xg_T_taken, b + 1)
                if not isinstance(b, int) or b > 1:
                    pe.wait_ge(hidden_done, b - 1)
                n = 0
                for kt in range(KT):
                    w_hi, w_lo = (halves_flat[:, bass.ds(e * (2 * EXP12) + half * EXP12 + kt * D, D)] for half in range(2))
                    for x, w in ((xg_T_hi, w_hi), (xg_T_hi, w_lo), (xg_T_lo, w_hi)):
                        last = nc.tensor.matmul(bank[2 + par][:], x[:, kt], w, start=n == 0, stop=n == 3 * KT - 1)
                        n += 1
                last.then_inc(up_full, 1)

            def transpose_hidden(b, par):
                pe.wait_ge(hidden_done, b + 1)
                for ft in range(2):
                    last = nc.tensor.transpose(bank[4][:, ft * P:(ft + 1) * P], hidden[par][:, ft * P:(ft + 1) * P], ident[:])
                last.then_inc(hidden_T_full, 1)

            def down(b, par):
                e = expert_of(b)
                pe.wait_ge(hidden_T_taken, b + 1)
                if not isinstance(b, int) or b > 1:
                    pe.wait_ge(y_done, b - 1)
                for ft in range(2):
                    last = nc.tensor.matmul(bank[6 + par][:], hidden_T[:, ft], w3[:, bass.ds(e * EXP3 + ft * D, D)], start=ft == 0, stop=ft == 1)
                last.then_inc(down_full, 1)

            def iteration(b, k, is_up, is_down, nxt):
                e = expert_of(b) if is_up else None
                if is_down:
                    transpose_hidden(b - 1, (k + 1) % 2)
                if is_up:
                    up(b, k % 2, e)
                if nxt:
                    transpose_x(b + 1, (k + 1) % 4)
                if is_down:
                    down(b - 1, (k + 1) % 2)

            transpose_x(0, 0)
            for b in range(4):
                iteration(b, b, True, b > 0, True)
            with pe.Fori(1, NBLOCK // 4 - 1) as u:
                for k in range(4):
                    iteration(4 * u + k, k, True, True, True)
            for b in range(NBLOCK - 4, NBLOCK):
                iteration(b, b % 4, True, True, b < NBLOCK - 1)
            iteration(NBLOCK, 0, False, True, False)


def shape_constants():
    f = lambda a: np.ascontiguousarray(a, dtype=np.float32)
    p = np.arange(P)
    inv_freq = (1.0 / 10000.0 ** (np.arange(0, HD, 2, dtype=np.float32) / np.float32(HD))).astype(np.float32)
    angles = np.arange(P, dtype=np.float32)[:, None] * inv_freq
    sin = np.repeat(np.sin(angles), 2, axis=1)
    sin[:, 0::2] *= -1
    e = np.arange(NE)
    rows = lambda a: f(np.broadcast_to(a, (P,) + a.shape))
    return {
        "ident": f(np.eye(P)),
        "mask": f(np.where(p[None, :] <= p[:, None], 0.0, -1e30)),
        "cos": f(np.repeat(np.cos(angles), 2, axis=1)),
        "sin": f(sin),
        "before": f(p[:, None] < p[None, :]),
        "expert_m8": rows(e - 8.0),
        "expert_low": rows((e[None, :] < e[:, None]).astype(np.float32)),
        "rows_full": rows(np.arange(NTILE) * float(P)),
        "part_1": f(p[:, None] + 1),
        "part_pad": f(p[:, None] + T + 1),
        "assign_ik": rows(np.arange(2 * NTILE) * 1.0),
        "col": rows(p * 1.0),
    }


SMALL = {"ident": [P, P], "mask": [P, P], "cos": [P, HD], "sin": [P, HD], "bq": [P, D], "bkv": [P, PAIR], "bo": [P, D], "router": [P, KT, NE]}
TABLES = {"before": [P, P], "expert_m8": [P, NE], "expert_low": [P, NE, NE], "rows_full": [P, NTILE], "part_1": [P, 1], "part_pad": [P, 1],
          "assign_ik": [P, 2 * NTILE], "col": [P, P]}
NEXT_TABLES = ("ident",) + tuple(TABLES)


def build(nc, a, out):
    h1_dram = nc.dram_tensor("h1_dram", (T, D), F32).ap()
    xn_dram = nc.dram_tensor("xn_dram", (T, XROW), F32).ap()
    with ExitStack() as ctx:
        base = (nc.sbuf_base + 31) // 32 * 32
        arena = ctx.enter_context(nc.sbuf_tensor("weights_arena", [P, 4 * W], F32))
        small = {n: ctx.enter_context(nc.sbuf_tensor("small_" + n, shape, F32, side="right")) for n, shape in {"ident": [P, P], **TABLES}.items()}
        over_arena = lambda name, at, n: nc.alloc_sbuf_tensor_at(name, [P, KT, n], F32R, offset=base + 4 * at)
        in_arena = lambda at, n: arena[:, at:at + KT * n].rearrange("p (k n) -> p k n", k=KT)
        raw, split = 2 * W, 3 * W
        wb_parts = [
            (in_arena(raw, D), over_arena("wq_hi", split, D)[:], over_arena("wq_lo", split + KT * D, D)[:]),
            (in_arena(raw + KT * D, PAIR), over_arena("wkv_hi", split + 2 * KT * D, PAIR)[:], over_arena("wkv_lo", split + 2 * KT * D + KT * PAIR, PAIR)[:]),
            (in_arena(raw + KT * (D + PAIR), D), None, None),
        ]
        wa_parts = (in_arena(raw, 3 * D), over_arena("wqkv_hi", 0, 3 * D)[:], over_arena("wqkv_lo", W, 3 * D)[:])
        tile = NE * EXP3
        chunk_parts = (arena[:, tile:tile + D], nc.alloc_sbuf_tensor_at("chunk_hi", [P, D], F32R, offset=base + 4 * (tile + D))[:],
                       nc.alloc_sbuf_tensor_at("chunk_lo", [P, D], F32R, offset=base + 4 * (tile + 2 * D))[:])
        halves_dram = nc.dram_tensor("halves_dram", (2, NTILE, P, D), F32).ap()
        w3 = arena[:, 0:NE * EXP3]
        halves = nc.alloc_sbuf_tensor_at("halves", [P, NE, 2, EXP12], F32R, offset=base + 4 * NE * EXP3)[:]
        assert NE * EXP3 + 3 * D <= 2 * W and NE * (EXP3 + 2 * EXP12) * 4 <= nc.sbuf_usable_end - base
        loads = lambda names: [(small[n][:], a[n]) for n in names]
        attention_ctx = ExitStack()
        small.update({n: attention_ctx.enter_context(nc.sbuf_tensor("small_" + n, shape, F32)) for n, shape in SMALL.items() if n != "ident"})
        h1_out = [attention_ctx.enter_context(nc.sbuf_tensor(f"h1_out{i}", [P, D], F32)) for i in range(2)]
        next_h1 = attention_ctx.enter_context(nc.sbuf_tensor("next_h1", [P, D], F32))[:]
        h1_stored = [ctx.enter_context(nc.semaphore(f"h1_stored{i}")) for i in range(2)]
        dilated_attention(nc, a["x_pairs"], a["wqkv"], a["bqk"], a["bv"], a["wout"], a["bout"], h1_dram, h1_stored, h1_out, next_h1, wa_parts, small["ident"],
                          loads(SMALL), (a["wq"], a["wkv"], a["wo"]), wb_parts)
        logits_T = ctx.enter_context(nc.sbuf_tensor("logits_T", [P, T], F32, side="right"))
        causal_attention(nc, h1_dram, next_h1, h1_stored, wb_parts, small, out, xn_dram, logits_T, a["w12"], chunk_parts, halves_dram,
                         loads(TABLES) + [(w3.rearrange("p (e n) -> p e n", e=NE), a["w3"].rearrange("e p n -> p e n"))])
        attention_ctx.close()
        routed_experts(nc, logits_T, halves_dram, halves, w3, small, xn_dram, out)


def laid_out(x, L0_tok_Wqkv, L0_tok_b_qkv, L0_tok_Wout, L0_tok_b_out, L0_attn_Wq, L0_attn_bq, L0_attn_Wkv, L0_attn_bkv,
             L0_attn_Wo, L0_attn_bo, L0_ffn_router_w, L0_ffn_w1, L0_ffn_w2, L0_ffn_w3):
    c = np.ascontiguousarray
    by_rows = lambda w: c(np.asarray(w).reshape(KT, P, -1).transpose(1, 0, 2))
    repeated = lambda b: c(np.broadcast_to(np.asarray(b), (P, b.shape[0])))
    x_T = np.asarray(x).reshape(2 * NTILE, SEG, 2, D).transpose(2, 3, 0, 1).reshape(2, KT, P, NPAIR, PAIR)
    w12 = np.concatenate([np.asarray(L0_ffn_w1), np.asarray(L0_ffn_w2)], axis=2)
    return {
        "x_pairs": c(x_T.transpose(0, 3, 2, 1, 4)),
        "wqkv": by_rows(L0_tok_Wqkv.T),
        "bqk": c(np.asarray(L0_tok_b_qkv)[:2 * D].reshape(2 * KT, P).T),
        "bv": repeated(L0_tok_b_qkv[2 * D:]),
        "wout": by_rows(L0_tok_Wout.T),
        "bout": repeated(L0_tok_b_out),
        "wq": by_rows(L0_attn_Wq),
        "wkv": by_rows(L0_attn_Wkv),
        "wo": c(np.asarray(L0_attn_Wo).reshape(NG, 4, HD, D).transpose(0, 2, 1, 3).reshape(P, 4, D)),
        "bq": repeated(L0_attn_bq),
        "bkv": repeated(L0_attn_bkv),
        "bo": repeated(L0_attn_bo),
        "router": by_rows(L0_ffn_router_w.T),
        "w12": c(w12.reshape(NTILE, P, D)),
        "w3": c(np.asarray(L0_ffn_w3).reshape(NE, 2, P, D).transpose(0, 2, 1, 3).reshape(NE, P, EXP3)),
    }


def kernel(**inputs):
    import concourse.bacc as bacc
    from concourse.bass_utils import run_bass_kernel_spmd

    nc = bacc.Bacc("TRN2", target_bir_lowering=False, num_devices=1)
    arrays = {**laid_out(**inputs), **shape_constants()}
    aps = {n: nc.dram_tensor(n, a.shape, mybir.dt.from_np(a.dtype), kind="ExternalInput").ap() for n, a in arrays.items()}
    out = nc.dram_tensor("out", (T + P, D), F32, kind="ExternalOutput").ap()
    build(nc, aps, out)
    r = run_bass_kernel_spmd(nc, [arrays], core_ids=[0])
    return r.results[0]["out"][:T].reshape(NTILE, P, D)
```
